# Optimizing a Trainium2 kernel written in Bass

```python
import numpy as np
import jax
import jax.numpy as jnp

def _softmax(x, axis=-1):
    return jax.nn.softmax(x, axis=axis)

def _gelu(x):
    return jax.nn.gelu(x, approximate=True)

def _silu(x):
    return jax.nn.silu(x)

def _sigmoid(x):
    return jax.nn.sigmoid(x)

def _layernorm(x, axis=-1, eps=1e-05):
    m = jnp.mean(x, axis=axis, keepdims=True)
    v = jnp.var(x, axis=axis, keepdims=True)
    return (x - m) / jnp.sqrt(v + eps)

def _scatter_add(tgt, idx, src, axis=0):
    return tgt.at[idx].add(src)

def _segment_sum(src, seg, n):
    return jax.ops.segment_sum(src, seg, n)
kernel_name = 'mk_cond_seq_d1_seqx_r2_a3c5b6'

def setup_inputs(seed: int=0):
    np.random.seed(seed)
    _w = jnp.asarray

    def _rec_inputs():
        import jax
        import jax.numpy as jnp
        _rk = jax.random.key(seed)
        x = -0.0003482 + 1 * jax.random.normal(jax.random.fold_in(_rk, 1), (2, 2048, 576), jnp.float32)
        _lenS = 2048 - jax.random.randint(jax.random.fold_in(_rk, 7), (2,), 0, max(1, 2048 // 4) + 1, jnp.int32)
        _lenS2 = 2048 - jax.random.randint(jax.random.fold_in(_rk, 8), (2,), 0, max(1, 2048 // 4) + 1, jnp.int32)
        cond_1152 = 0.00257642 + 1.0011 * jax.random.normal(jax.random.fold_in(_rk, 11), (2, 576), jnp.float32)
        return (x, cond_1152)
    x, cond_1152 = _rec_inputs()

    def _L0_cond_setup():
        import jax, jax.numpy as jnp
        import numpy as np
        H = 576
        NH = 16
        HD = H // NH
        MLP = int(H * 4.0)
        EPS = 1e-06

        def _ln(z, scale=None):
            m = jnp.mean(z, axis=-1, keepdims=True)
            v = jnp.mean(jnp.square(z - m), axis=-1, keepdims=True)
            y = (z - m) * jax.lax.rsqrt(v + EPS)
            if scale is not None:
                y = y * scale
            return y
        key = jax.random.key(seed)
        ks = jax.random.split(key, 16)
        B, N = (16, 512)
        x = jax.random.normal(ks[0], (B, N, H), dtype=jnp.float32)
        c = jax.random.normal(ks[1], (B, H), dtype=jnp.float32)

        def xav(k, fan_in, fan_out):
            lim = np.sqrt(6.0 / (fan_in + fan_out))
            return jax.random.uniform(k, (fan_in, fan_out), jnp.float32, -lim, lim)
        w_mod = 0.02 * jax.random.normal(ks[2], (H, 6 * H), dtype=jnp.float32)
        b_mod = 0.02 * jax.random.normal(ks[3], (6 * H,), dtype=jnp.float32)
        w_qkv = xav(ks[4], H, 3 * H)
        b_qkv = jnp.zeros((3 * H,), jnp.float32)
        g_q = jnp.ones((HD,), jnp.float32)
        g_k = jnp.ones((HD,), jnp.float32)
        w_proj = xav(ks[5], H, H)
        b_proj = jnp.zeros((H,), jnp.float32)
        w1 = xav(ks[6], H, MLP)
        b1 = jnp.zeros((MLP,), jnp.float32)
        w2 = xav(ks[7], MLP, H)
        b2 = jnp.zeros((H,), jnp.float32)
        return dict(x=x, c=c, w_mod=w_mod, b_mod=b_mod, w_qkv=w_qkv, b_qkv=b_qkv, g_q=g_q, g_k=g_k, w_proj=w_proj, b_proj=b_proj, w1=w1, b1=b1, w2=w2, b2=b2)
    _L0_cond_all = _L0_cond_setup()
    _L0_cond_in = {k: v for k, v in _L0_cond_all.items() if k in ('w_mod', 'b_mod', 'w_qkv', 'b_qkv', 'g_q', 'g_k', 'w_proj', 'b_proj', 'w1', 'b1', 'w2', 'b2')}
    del _L0_cond_all
    return {'x': x, 'cond_1152': cond_1152, 'L0_cond_w_mod': _L0_cond_in['w_mod'], 'L0_cond_b_mod': _L0_cond_in['b_mod'], 'L0_cond_w_qkv': _L0_cond_in['w_qkv'], 'L0_cond_b_qkv': _L0_cond_in['b_qkv'], 'L0_cond_g_q': _L0_cond_in['g_q'], 'L0_cond_g_k': _L0_cond_in['g_k'], 'L0_cond_w_proj': _L0_cond_in['w_proj'], 'L0_cond_b_proj': _L0_cond_in['b_proj'], 'L0_cond_w1': _L0_cond_in['w1'], 'L0_cond_b1': _L0_cond_in['b1'], 'L0_cond_w2': _L0_cond_in['w2'], 'L0_cond_b2': _L0_cond_in['b2']}

def reference(x, cond_1152, L0_cond_w_mod, L0_cond_b_mod, L0_cond_w_qkv, L0_cond_b_qkv, L0_cond_g_q, L0_cond_g_k, L0_cond_w_proj, L0_cond_b_proj, L0_cond_w1, L0_cond_b1, L0_cond_w2, L0_cond_b2):
    import jax
    import jax.numpy as jnp

    def _L0_cond_ref(x, c, w_mod, b_mod, w_qkv, b_qkv, g_q, g_k, w_proj, b_proj, w1, b1, w2, b2):
        import jax, jax.numpy as jnp
        import numpy as np
        H = 576
        NH = 16
        HD = H // NH
        MLP = int(H * 4.0)
        EPS = 1e-06

        def _ln(z, scale=None):
            m = jnp.mean(z, axis=-1, keepdims=True)
            v = jnp.mean(jnp.square(z - m), axis=-1, keepdims=True)
            y = (z - m) * jax.lax.rsqrt(v + EPS)
            if scale is not None:
                y = y * scale
            return y
        B, N, _ = x.shape
        mod = jax.nn.swish(c) @ w_mod + b_mod
        sh_msa, sc_msa, g_msa, sh_mlp, sc_mlp, g_mlp = jnp.split(mod, 6, axis=1)
        xn = _ln(x) * (1 + sc_msa[:, None, :]) + sh_msa[:, None, :]
        qkv = xn @ w_qkv + b_qkv
        qkv = qkv.reshape(B, N, 3, NH, HD).transpose(2, 0, 3, 1, 4)
        q, k, v = (qkv[0], qkv[1], qkv[2])
        q = _ln(q, g_q)
        k = _ln(k, g_k)
        attn = jax.nn.softmax(jnp.einsum('bhqd,bhkd->bhqk', q, k) * HD ** (-0.5), axis=-1)
        o = jnp.einsum('bhqk,bhkd->bhqd', attn, v)
        o = o.transpose(0, 2, 1, 3).reshape(B, N, H) @ w_proj + b_proj
        x = x + g_msa[:, None, :] * o
        xn2 = _ln(x) * (1 + sc_mlp[:, None, :]) + sh_mlp[:, None, :]
        h = jax.nn.gelu(xn2 @ w1 + b1, approximate=True)
        x = x + g_mlp[:, None, :] * (h @ w2 + b2)
        return x
    x = _L0_cond_ref(x, cond_1152, L0_cond_w_mod, L0_cond_b_mod, L0_cond_w_qkv, L0_cond_b_qkv, L0_cond_g_q, L0_cond_g_k, L0_cond_w_proj, L0_cond_b_proj, L0_cond_w1, L0_cond_b1, L0_cond_w2, L0_cond_b2)
    return x

_drawn_inputs = setup_inputs


def setup_inputs(seed=0):
    import zlib

    import numpy as np

    out = dict(_drawn_inputs(seed))
    spreads = {'L0_cond_b_qkv': (0.0, 0.33),
     'L0_cond_g_q': (1.0, 0.6),
     'L0_cond_g_k': (1.0, 0.6),
     'L0_cond_b_proj': (0.0, 0.289),
     'L0_cond_b1': (0.0, 0.361),
     'L0_cond_b2': (0.0, 0.329)}
    factors = {'L0_cond_b_mod': 4.309}
    for name, (base, spread) in spreads.items():
        noise = np.random.default_rng([zlib.crc32(name.encode()), seed]).standard_normal(out[name].shape)
        drawn = base * np.exp(spread * noise) if base else spread * noise
        out[name] = jnp.asarray(drawn.astype(out[name].dtype))
    for name, factor in factors.items():
        out[name] = (out[name] * factor).astype(out[name].dtype)
    return out
```

```python
import concourse.bass as bass
import numpy as np
from concourse import mybir
from contextlib import ExitStack

F32 = mybir.dt.float32
F32R = mybir.dt.float32r
F16 = mybir.dt.float16
BF16 = mybir.dt.bfloat16
I32 = mybir.dt.int32
ALU = mybir.AluOpType
ACT = mybir.ActivationFunctionType
AX = mybir.AxisListType

B, N, H = 2, 2048, 576
NH = 16
HD = H // NH
MLP = 4 * H
EPS = 1e-6
P = 128

KF = H // P
KT = H - KF * P
KC = KF + 1
CH = 512
TPC = CH // P
NCH = N // CH
NT = N // P
GH = 4
NG = NH // GH
GW = GH * HD
QK = 2 * GH
VW = 2 * HD + 1
VP = VW + 1
RW = HD + 1
RP = RW + 1
SW = 3 * HD + 1
SP = 112
FT = MLP // P
HALF = H // 2
WS = 64.0
STEPS = NT // 2
UNITS = GH * NCH
LAG = 3
NP = 4
SAFE = 64.0


def bcast(ap, axis, n):
    v = ap.unsqueeze(axis)
    shape = list(v.shape)
    shape[axis] = n
    return v.broadcast_to(shape)


def modulation(nc, keep, c, w_mod, b_mod, g_q, g_k, b2, dummy=None):
    with ExitStack() as ctx:
        sb = lambda n, s, d: ctx.enter_context(nc.sbuf_tensor(n, s, d))
        sem = lambda n: ctx.enter_context(nc.semaphore(n))
        wm = sb("wm", [P, KC, 6 * H], F32)
        cT = sb("cT", [P, KC, B], F32)
        sT = sb("sT", [P, KC, B], F32)
        eT = sb("eT", [P, KC, B], F32)
        rT = sb("rT", [P, KC, B], F32)
        sbc = sb("sbc", [P, KC, B, P], F32)
        bcol = sb("bcol", [P, 4, KC], F32)
        grow = sb("grow", [P, 2, H], F32)
        b2row = sb("b2row", [P, H], F32)
        gain2 = sb("gain2", [P, 2, HD], F32)
        bound = sb("bound", [P, 2], F32)
        pcol = ctx.enter_context(nc.psum_tensor("pcol", [P, 512], F32))
        prow = ctx.enter_context(nc.psum_tensor("prow", [P, 4, 512], F32))
        c_loaded, w_loaded, small_loaded = sem("c_loaded"), sem("wm_loaded"), sem("small_loaded")
        zeroed, exp_ready, silu_step, silu_ready = sem("zeroed"), sem("silu_exp"), sem("silu_step"), sem("silu_ready")
        cols_ready, rows_ready, rows_taken = sem("cols_ready"), sem("rows_ready"), sem("rows_taken")
        col_step, gain_step = sem("col_step"), sem("gain_step")
        ident_zero = sem("ident_zero")
        VECS = (0, 1, 3, 4)
        block = ctx.enter_context(nc.Block())

        @block.sync
        def _(sp):
            with nc.allow_non_contiguous_dma(reason="two short vectors"):
                for b in range(B):
                    sp.dma_start(cT[:, 0:KF, b], c[b, 0:KF * P].rearrange("(k p) -> p k", p=P)).then_inc(c_loaded, 16)
                    sp.dma_start(cT[0:KT, KF, b:b + 1], c[b, KF * P:H].rearrange("(p k) -> p k", k=1)).then_inc(c_loaded, 16)
            for k in range(KC):
                rows = P if k < KF else KT
                sp.dma_start(wm[0:rows, k, :], w_mod[k * P:k * P + rows, :]).then_inc(w_loaded, 16)

        @block.scalar
        def _(act):
            with nc.allow_non_contiguous_dma(reason="short vectors"):
                for n, vec in enumerate(VECS):
                    v = b_mod[vec * H:(vec + 1) * H]
                    act.dma_start(bcol[:, n, 0:KF], v[0:KF * P].rearrange("(k p) -> p k", p=P)).then_inc(small_loaded, 16)
                    for half in range(2):
                        act.dma_start(bcol[half * KT:(half + 1) * KT, n, KF:KC], v[KF * P:H].rearrange("(p k) -> p k", k=1)).then_inc(small_loaded, 16)
            for n, vec in enumerate((2, 5)):
                act.dma_start(grow[:, n, :], bcast(b_mod[vec * H:(vec + 1) * H], 0, P)).then_inc(small_loaded, 16)
            act.dma_start(b2row[:, :], bcast(b2, 0, P)).then_inc(small_loaded, 16)
            act.dma_start(gain2[:, 0, :], bcast(g_q, 0, P)).then_inc(small_loaded, 16)
            act.dma_start(gain2[:, 1, :], bcast(g_k, 0, P)).then_inc(small_loaded, 16)
            act.wait_ge(zeroed, 1)
            act.wait_ge(c_loaded, 16 * 2 * B)
            act.activation(eT[:, :, :], cT[:, :, :], ACT.Exp, scale=-1.0).then_inc(exp_ready, 1)

        @block.gpsimd
        def _(pool):
            pool.memset(keep.ident[:, :], 0.0).then_inc(ident_zero, 1)
            pool.memset(keep.ident16[:, :], 0.0).then_inc(ident_zero, 1)
            pool.memset(keep.fold[:, :], 0.0).then_inc(ident_zero, 1)
            pool.memset(keep.power[:, :], -0.5)
            pool.memset(keep.eps[:, :], EPS)
            pool.memset(keep.head_eps[:, :], HD * EPS * WS * WS)
            pool.memset(keep.ones16[:, :], 1.0)
            pool.wait_ge(ident_zero, 3)
            for m in (keep.ident, keep.ident16):
                pool.affine_select(out=m[:, :], in_=m[:, :], compare_op=ALU.not_equal, fill=1.0,
                                   base=0, pattern=[[-1, P]], channel_multiplier=1)
            pool.affine_select(out=keep.fold[:, :], in_=keep.fold[:, :], compare_op=ALU.not_equal, fill=1.0,
                               base=0, pattern=[[-1, RP]], channel_multiplier=1).then_inc(ident_zero, 1)
            pool.wait_ge(ident_zero, 4)
            pool.affine_select(out=keep.fold[:, 0:HD], in_=keep.fold[:, 0:HD], compare_op=ALU.not_equal, fill=1.0,
                               base=-RW, pattern=[[-1, HD]], channel_multiplier=1)

        @block.vector
        def _(dve):
            nc.vector.memset(cT[KT:P, KF, :], 0.0).then_inc(zeroed, 1)
            dve.wait_ge(exp_ready, 1)
            nc.vector.tensor_scalar_add(rT[:, :, :], eT[:, :, :], 1.0).then_inc(silu_step, 1)
            dve.wait_ge(silu_step, 1)
            nc.vector.reciprocal(eT[:, :, :], rT[:, :, :]).then_inc(silu_step, 1)
            dve.wait_ge(silu_step, 2)
            nc.vector.tensor_tensor(sT[:, :, :], cT[:, :, :], eT[:, :, :], ALU.mult).then_inc(silu_step, 1)
            dve.wait_ge(silu_step, 3)
            nc.vector.tensor_copy(sbc[:, :, :, :].rearrange("p k b n -> p (k b) n"),
                                  bcast(sT[:, :, :].rearrange("p k b -> p (k b)"), 2, P)).then_inc(silu_ready, 1)
            dve.wait_ge(small_loaded, 16 * 17)
            nc.vector.scalar_tensor_tensor(out=keep.gain[:, :], in0=gain2[:, 0, :], scalar=HD ** -0.5,
                                           in1=gain2[:, 1, :], op0=ALU.mult, op1=ALU.mult).then_inc(gain_step, 1)
            dve.wait_ge(gain_step, 1)
            nc.vector.tensor_reduce(bound[:, 0:1], keep.gain[:, :], AX.X, ALU.max,
                                    apply_absolute_value=True).then_inc(gain_step, 1)
            dve.wait_ge(gain_step, 2)
            nc.vector.tensor_scalar(bound[:, 1:2], bound[:, 0:1], float(HD), SAFE, ALU.mult, ALU.is_gt).then_inc(gain_step, 1)
            dve.wait_ge(gain_step, 3)
            nc.vector.tensor_copy(keep.unsafe[:, :], bound[:, 1:2])
            dve.wait_ge(cols_ready, 1)
            for b in range(B):
                nc.vector.tensor_tensor(keep.cols[:, b, :, :], pcol[:, 0:4 * KC * B].rearrange("p (v k b) -> p b v k", v=4, b=B)[:, b, :, :],
                                        bcol[:, :, :], ALU.add).then_inc(col_step, 1)
            dve.wait_ge(col_step, B)
            for v in (1, 3):
                nc.vector.tensor_scalar_add(keep.cols[:, :, v, :], keep.cols[:, :, v, :], 1.0)
            for n in range(2 * B):
                b, v = n // 2, n % 2
                dve.wait_ge(rows_ready, n + 1)
                out = keep.gates[:, b, v, :].rearrange("p (h n) -> p h n", h=2)
                nc.vector.tensor_tensor(out, prow[:, (n % 2) * 2:(n % 2) * 2 + 2, 0:HALF],
                                        grow[:, v, :].rearrange("p (h n) -> p h n", h=2), ALU.add).then_inc(rows_taken, 1)
                dve.wait_ge(rows_taken, n + 1)
                if v == 1:
                    nc.vector.tensor_tensor(keep.gb2[:, b, :], keep.gates[:, b, v, :], b2row[:, :], ALU.mult).then_inc(gain_step, 1)
                    dve.wait_ge(gain_step, 4 + b)
                nc.vector.tensor_scalar_mul(keep.gates[:, b, v, :], keep.gates[:, b, v, :], 1.0 / WS)

        @block.tensor
        def _(pe):
            pe.wait_ge(silu_ready, 1)
            pe.wait_ge(w_loaded, 16 * KC)
            for n, vec in enumerate(VECS):
                for m in range(KC + 1):
                    f, rows, at = min(m, KF), P if m < KF else KT, KT if m == KC else 0
                    for k in range(KC):
                        kr = P if k < KF else KT
                        last = nc.tensor.matmul(pcol[at:at + rows, (n * KC + f) * B:(n * KC + f + 1) * B],
                                                wm[0:kr, k, vec * H + f * P:vec * H + f * P + rows], sT[0:kr, k, :],
                                                start=(k == 0), stop=(k == KC - 1))
            last.then_inc(cols_ready, 1)
            for n in range(2 * B):
                b, vec = n // 2, (2, 5)[n % 2]
                if n >= 2:
                    pe.wait_ge(rows_taken, n - 1)
                for half in range(2):
                    for k in range(KC):
                        kr = P if k < KF else KT
                        last = nc.tensor.matmul(prow[:, (n % 2) * 2 + half, 0:HALF], sbc[0:kr, k, b, :],
                                                wm[0:kr, k, vec * H + half * HALF:vec * H + (half + 1) * HALF],
                                                start=(k == 0), stop=(k == KC - 1))
                last.then_inc(rows_ready, 1)


class Cut:

    def __init__(self, w, bias, out, cols, thirds=False):
        self.w, self.bias, self.out, self.cols, self.thirds = w, bias, out, cols, thirds
        self.width = 2 * H if cols > 3 * H else H

    def part(self, p0, p1, slot, c0):
        row = self.out[p0:p1, slot, :]
        if self.thirds:
            return row.rearrange("p (g t j) -> p g t j", g=NG, t=3)[:, :, c0 // H, :]
        return row[:, c0:c0 + self.width].rearrange("p (g j) -> p g j", g=NG)

    def grouped(self, ap):
        return ap[:, 0:self.width].rearrange("p (g j) -> p g j", g=NG)


def cut_weights(nc, tag, mats, w2=None, w2s=None, b1=None, b1col=None):
    with ExitStack() as ctx:
        sb = lambda n, s, d: ctx.enter_context(nc.sbuf_tensor(tag + n, s, d))
        sem = lambda n: ctx.enter_context(nc.semaphore(tag + n))
        pieces = [(m, c0) for m in mats for c0 in range(0, m.cols, m.width)]
        wide = max(m.width for m in mats)
        stage = sb("stage", [P, 2, KC * wide], F32)
        tails = sb("tails", [P, 2, wide], F16)
        biases = sb("biases", [P, 2, wide], F32)
        bias_hi = sb("bias_hi", [P, 2, wide], F16)
        full, tail, bias_in = [[sem(f"{n}{i}") for i in range(2)] for n in ("full", "tail", "bias")]
        high, low, blank, b1_in = sem("high"), sem("low"), sem("blank"), sem("b1_in")
        W2P = 4 if w2 is not None else 0
        lots = [5, 5, 4, 4]
        lot_at = [sum(lots[:n]) for n in range(4)]
        w2_in = [sem(f"w2in{i}") for i in range(2)]
        n_pieces = len(pieces)
        block = ctx.enter_context(nc.Block())

        def staged(s, width):
            return stage[:, s, 0:KC * width].rearrange("p (k n) -> p k n", k=KC)

        def lot(n):
            a, m = lot_at[n], lots[n]
            return (stage[:, (n_pieces + n) % 2, 0:m * H], w2s[:, 0, a:a + m, :].rearrange("p f n -> p (f n)"),
                    w2s[:, 1, a:a + m, :].rearrange("p f n -> p (f n)"))

        @block.sync
        def _(sp):
            for n, (m, c0) in enumerate(pieces):
                if n >= 2:
                    sp.wait_ge(low, n - 1)
                s, w = n % 2, m.width
                sp.dma_start(staged(s, w)[:, 0:KF, :], m.w[0:KF * P, c0:c0 + w].rearrange("(k p) n -> p k n", p=P)).then_inc(full[s], 16)
                for half in range(2):
                    sp.dma_start(staged(s, w)[half * KT:(half + 1) * KT, KF, :], m.w[KF * P:H, c0:c0 + w]).then_inc(tail[s], 16)
                if m.bias is not None:
                    for row in (64, 96):
                        sp.dma_start(biases[row:row + 1, s, 0:w], m.bias[c0:c0 + w].unsqueeze(0)).then_inc(bias_in[s], 16)
            if b1 is not None:
                with nc.allow_non_contiguous_dma(reason="a short vector"):
                    sp.dma_start(b1col[:, :], b1.rearrange("(f p) -> p f", p=P)).then_inc(b1_in, 16)
            for n in range(W2P):
                if n_pieces + n >= 2:
                    sp.wait_ge(low, n_pieces + n - 1)
                a, m = lot_at[n], lots[n]
                sp.dma_start(lot(n)[0].rearrange("p (f n) -> p f n", n=H),
                             w2[a * P:(a + m) * P, :].rearrange("(f p) n -> p f n", p=P)).then_inc(w2_in[n % 2], 16)
            if b1 is not None:
                sp.wait_ge(b1_in, 16)

        def loaded(eng, n):
            s = n % 2
            eng.wait_ge(full[s], 16 * (n // 2 + 1))
            eng.wait_ge(tail[s], 32 * (n // 2 + 1))
            with_bias = sum(1 for q in range(s, n + 1, 2) if pieces[q][0].bias is not None)
            if with_bias:
                eng.wait_ge(bias_in[s], 32 * with_bias)

        @block.scalar
        def _(act):
            blanks = 0
            for n, (m, c0) in enumerate(pieces):
                s, x = n % 2, staged(n % 2, m.width)
                loaded(act, n)
                if n >= 2:
                    act.wait_ge(low, n - 1)
                for k in range(KF):
                    act.activation(m.part(0, P, k, c0), m.grouped(x[:, k, :]), ACT.Copy, scale=WS)
                act.activation(m.part(0, KT, 8, c0), m.grouped(x[0:KT, KF, :]), ACT.Copy, scale=WS)
                if m.bias is not None:
                    blanks += c0 == 0
                    act.wait_ge(blank, blanks)
                    act.activation(m.part(0, KT, 9, c0), m.grouped(x[0:KT, KF, :]), ACT.Copy, scale=WS)
                    act.activation(m.part(64, 65, 9, c0), m.grouped(biases[64:65, s, :]), ACT.Copy, scale=WS)
                    act.activation(bias_hi[96:97, s, 0:m.width], biases[96:97, s, 0:m.width], ACT.Copy, scale=WS)
                act.activation(tails[KT:P, s, 0:m.width], x[KT:P, KF, :], ACT.Copy, scale=WS).then_inc(high, 1)
            for n in range(W2P):
                act.wait_ge(w2_in[n % 2], 16 * (n // 2 + 1))
                act.activation(lot(n)[1], lot(n)[0], ACT.Copy, scale=WS).then_inc(high, 1)

        @block.vector
        def _(dve):
            def lower(out, src, hi):
                return nc.vector.scalar_tensor_tensor(out=out, in0=src, scalar=WS, in1=hi, op0=ALU.mult, op1=ALU.subtract)

            for m in mats:
                if m.bias is not None:
                    nc.vector.memset(m.out[64:P, 9, :], 0.0).then_inc(blank, 1)
            for n, (m, c0) in enumerate(pieces):
                s, x = n % 2, staged(n % 2, m.width)
                loaded(dve, n)
                dve.wait_ge(high, n + 1)
                for k in range(KF):
                    lower(m.part(0, P, KF + k, c0), m.grouped(x[:, k, :]), m.part(0, P, k, c0))
                last = lower(m.part(KT, P, 8, c0), m.grouped(x[KT:P, KF, :]), m.grouped(tails[KT:P, s, :]))
                if m.bias is not None:
                    last = lower(m.part(96, 97, 9, c0), m.grouped(biases[96:97, s, :]), m.grouped(bias_hi[96:97, s, :]))
                last.then_inc(low, 1)
            for n in range(W2P):
                dve.wait_ge(w2_in[n % 2], 16 * (n // 2 + 1))
                dve.wait_ge(high, n_pieces + n + 1)
                lower(lot(n)[2], lot(n)[0], lot(n)[1]).then_inc(low, 1)


def split_products(xhi, xlo, w, tokens, cols, bias=True):
    for k in range(KF):
        yield xhi[:, k, tokens], w[:, k, cols]
        yield xhi[:, k, tokens], w[:, KF + k, cols]
        yield xlo[:, k, tokens], w[:, k, cols]
    yield xhi[:, KF, tokens], w[:, 8, cols]
    if bias:
        yield xlo[0:97, KF, tokens], w[0:97, 9, cols]
    else:
        yield xlo[0:KT, KF, tokens], w[0:KT, 8, cols]


def attention(nc, keep, x, o_dram, wq):
    with ExitStack() as ctx:
        sb = lambda n, s, d: ctx.enter_context(nc.sbuf_tensor("at_" + n, s, d))
        sem = lambda n: ctx.enter_context(nc.semaphore("at_" + n))
        xf = x.rearrange("b n h -> (b n) h")
        stats = sb("stats", [P, TPC, 2, 6], F32)
        mv = sb("mv", [P, TPC, 2], F32)
        rstd = sb("rstd", [P, 2, TPC], F32)
        xhi = sb("xhi", [P, KC, N], F16)
        xlo = sb("xlo", [P, KC, N], F16)
        total = sb("total", [P, TPC * QK], F32)
        ssq = sb("ssq", [P, 2, TPC * QK], F32)
        qkT = sb("qkT", [SP, QK, N], F16)
        v16 = sb("v16", [P, NT, GH, VP], F16)
        vr = sb("vr", [P, NT, GH, RP], F32R)
        oT = sb("oT", [VW, CH], F32)
        rden = sb("rden", [P, TPC], F32)
        og = sb("og", [P, NT, GW], F32)
        nmax = sb("nmax", [P, 2], F32)
        diag = sb("diag", [P, P], F16)

        def overlaid(*sets):
            size = lambda tensors: sum(-(-int(np.prod(shape[1:])) * (2 if d == F16 else 4) // 32) * 32 for _, shape, d in tensors)
            pad = max(map(size, sets)) - size(sets[-1])
            if pad:
                sets = (*sets[:-1], [*sets[-1], (sets[-1][0][0] + "_pad", [P, pad // 4], F32)])
            made = []
            for n, tensors in enumerate(sets):
                with ExitStack() as one:
                    place = ctx if n == len(sets) - 1 else one
                    made += [place.enter_context(nc.sbuf_tensor("at_" + name, shape, d)) for name, shape, d in tensors]
            return made

        xin, stk, p, *_ = overlaid([("xin", [P, 2 * TPC, H], F32)],
                               [("stk", [P, 2, TPC, QK, SP], F16)],
                               [("p", [P, NP, 2 * CH], F32)])
        y, aff, raw, xc, sq, plo, *_ = overlaid([("y", [P, TPC, KC * P], F32),
                                             ("aff", [P, 2, CH], F32)],
                                            [("raw", [P, TPC, 3 * GW], F32), ("xc", [P, TPC, QK, HD], F32),
                                             ("sq", [P, TPC, QK, HD], F32)],
                                            [("plo", [P, NP, 2 * CH], F32R)])
        ps = ctx.enter_context(nc.psum_tensor("at_ps", [P, 8, 512], F32))
        mm_bank = lambda i: ps[:, i, :]
        tq_bank = lambda i: ps[:, 4 + i, :].bitcast(F16)
        acc = ps[:, 4:6, :].rearrange("p a n -> p (a n)")
        fold_bank = ps[:, 6, :]

        x_loaded = sem("x_loaded")
        stats_ready, mv_ready, var_ready, rstd_ready, y_ready = sem("stats"), sem("mv"), sem("var"), sem("rstd"), sem("y")
        xt_ready, aff_ready, xhi_ready, xlo_ready = sem("xt"), sem("aff"), sem("xhi"), sem("xlo")
        qkv_ready, raw_ready = sem("qkv"), sem("raw")
        v_ready, total_ready, xc_ready, sq_ready, ssq_ready, msq_ready, hrstd_ready = (
            sem("v"), sem("total"), sem("xc"), sem("sq"), sem("ssq"), sem("msq"), sem("hrstd"))
        yn_ready, yg_ready, high_ready, low_ready = sem("yn"), sem("yg"), sem("high"), sem("low")
        tq_ready, tq_act, tq_dve, fixed = sem("tq"), sem("tq_act"), sem("tq_dve"), sem("fixed")
        scores_ready, exp_done, plo_ready, pv_done = sem("scores"), sem("exp"), sem("plo"), sem("pv")
        oT_ready, fold_ready, rden_ready, o_ready, o_stored = sem("oT"), sem("foldr"), sem("rden"), sem("o"), sem("o_stored")
        g_scores, g_max, g_diag, g_row, g_done = sem("g_scores"), sem("g_max"), sem("g_diag"), sem("g_row"), sem("g_done")

        block = ctx.enter_context(nc.Block())

        @block.sync
        def _(sp):
            with sp.Fori(0, B) as b:
                with sp.Fori(0, NCH) as j:
                    J = b * NCH + j
                    sp.wait_ge(y_ready, J + 1)
                    sp.wait_ge(x_loaded, 16 * J + 16)
                    sp.dma_start(xin[:, bass.ds((j % 2) * TPC, TPC), :],
                                 xf[bass.ds(b * N + j * CH, CH), :].rearrange("(i p) n -> p i n", p=P)).then_inc(x_loaded, 16)
                with sp.Fori(0, NG) as g:
                    it = b * NG + g
                    sp.wait_ge(o_ready, (it + 1) * UNITS + 1)
                    sp.dma_start(o_dram[bass.ds(b * N, N), bass.ds(g * GW, GW)].rearrange("(t p) n -> p t n", p=P),
                                 og[:, :, :]).then_inc(o_stored, 16)
            sp.wait_ge(o_stored, 16 * (B * NG + 1))

        @block.gpsimd
        def _(pool):
            with pool.Fori(0, B) as b:
                with pool.Fori(0, NCH) as j:
                    J = b * NCH + j
                    pool.wait_ge(mv_ready, J + 1)
                    pool.tensor_tensor(rstd[:, 0, :], mv[:, :, 1], keep.eps[:, 0:TPC], ALU.add).then_inc(var_ready, 1)
                    pool.wait_ge(var_ready, J + 1)
                    pool.tensor_tensor(rstd[:, 1, :], rstd[:, 0, :], keep.power[:, 0:TPC], ALU.pow).then_inc(rstd_ready, 1)
                with pool.Fori(0, NG * NCH) as gj:
                    C = b * NG * NCH + gj
                    pool.wait_ge(ssq_ready, C + 1)
                    pool.tensor_tensor(ssq[:, 1, :], ssq[:, 0, :], keep.head_eps[:, :], ALU.add).then_inc(msq_ready, 1)
                    pool.wait_ge(msq_ready, C + 1)
                    pool.tensor_tensor(ssq[:, 1, :], ssq[:, 1, :], keep.power[:, 0:TPC * QK], ALU.pow).then_inc(hrstd_ready, 1)

        @block.scalar
        def _(act):
            def store_tq(bank, i, j):
                t0 = (j * TPC + i) * P
                return act.copy(qkT[0:SW, :, t0:t0 + P], bank[0:SW, :].rearrange("p (e n) -> p e n", e=QK))

            def keep_oT(done):
                act.wait_ge(pv_done, done * STEPS + 1)
                act.wait_ge(fold_ready, done)
                act.copy(oT[:, :], acc[0:VW, bass.ds(((done + 1) % 2) * CH, CH)]).then_inc(oT_ready, 1)

            def exps(unit, first=False):
                for s in range(STEPS):
                    n = unit * STEPS + s
                    if s == LAG and not first:
                        keep_oT(unit)
                    act.wait_ge(scores_ready, n + 1)
                    act.wait_ge(pv_done, n + 1 - NP + 1 if not first or s >= NP else base_done)
                    act.activation(p[:, s % NP, :], ps[:, 2 * (s % 2):2 * (s % 2) + 2, :].rearrange("p a n -> p (a n)"),
                                   ACT.Exp).then_inc(exp_done, 1)

            with act.Fori(0, B) as b:
                with act.Fori(0, NCH) as j:
                    J = b * NCH + j
                    for k in range(KC):
                        n = J * KC + k
                        act.wait_ge(xt_ready, n + 1)
                        act.wait_ge(xlo_ready, n + (0 if k else 1))
                        act.activation(aff[:, k % 2, :], ps[:, 4 + k % 2, :], ACT.Identity,
                                       bias=keep.cols[:, bass.ds(b, 1), 0, k:k + 1].rearrange("p b k -> p (b k)"),
                                       scale=keep.cols[:, bass.ds(b, 1), 1, k:k + 1].rearrange("p b k -> p (b k)")).then_inc(aff_ready, 1)
                        act.wait_ge(aff_ready, n + 2)
                        act.copy(xhi[:, k, bass.ds(j * CH, CH)], aff[:, k % 2, :]).then_inc(xhi_ready, 1)
                with act.Fori(0, NG) as g:
                    it = b * NG + g
                    base_done = it * UNITS * STEPS + 1
                    act.wait_ge(pv_done, base_done)
                    for j in range(NCH + 1):
                        C = it * NCH + j
                        if j < NCH:
                            for hh in range(2):
                                act.wait_ge(qkv_ready, 2 * C + hh + 1)
                                if hh == 0:
                                    act.wait_ge(xc_ready, C + 1)
                                act.copy(raw[:, 2 * hh:2 * hh + 2, :], ps[:, 2 * hh:2 * hh + 2, 0:3 * GW]).then_inc(raw_ready, 1)
                            act.wait_ge(raw_ready, 2 * C + 2)
                            v = raw[:, :, 2 * GW:3 * GW].rearrange("p i (h d) -> p i h d", h=GH)
                            act.activation(v16[:, j * TPC:(j + 1) * TPC, :, 0:HD], v, ACT.Copy, scale=1.0 / WS)
                            act.activation(vr[:, j * TPC:(j + 1) * TPC, :, 0:HD], v, ACT.Copy, scale=1.0 / WS).then_inc(v_ready, 1)
                        for jt in ([j - 2] if j >= 2 else []) + ([j - 1] if j == NCH else []):
                            for i in range(2):
                                act.wait_ge(tq_ready, (it * NCH + jt) * TPC + i + 1)
                                store_tq(tq_bank(i), i, jt).then_inc(tq_act, 1)
                        if j < NCH:
                            act.wait_ge(xc_ready, C + 2)
                            act.activation(sq[:, :, :, :].rearrange("p a b c -> p (a b c)"), xc[:, :, :, :].rearrange("p a b c -> p (a b c)"),
                                           ACT.Square).then_inc(sq_ready, 1)
                            if j >= 2:
                                act.wait_ge(tq_ready, (C - 1) * TPC)
                            act.wait_ge(yg_ready, C + 1)
                            part = stk[:, j % 2, :, :, :]
                            act.copy(part[:, :, :, 1:1 + HD], xc[:, :, :, :]).then_inc(high_ready, 1)
                            act.copy(part[:, :, 0:GH, 1 + 2 * HD:SW], xc[:, :, 0:GH, :])
                            act.copy(part[:, :, GH:QK, 1 + HD:1 + 2 * HD], xc[:, :, GH:QK, :]).then_inc(high_ready, 1)
                    exps(it * UNITS, first=True)
                    with act.Fori(1, UNITS) as u:
                        exps(it * UNITS + u)
                    keep_oT((it + 1) * UNITS)

        @block.vector
        def _(dve):
            def low_parts(unit):
                for s in range(STEPS):
                    n = unit * STEPS + s
                    dve.wait_ge(exp_done, n + 3)
                    high = p[:, s % NP, :].bitcast(BF16).rearrange("p (n t) -> p n t", t=2)[:, :, 1]
                    nc.vector.tensor_tensor(plo[:, s % NP, :], p[:, s % NP, :], high, ALU.subtract).then_inc(plo_ready, 1)
                    yield s

            def finish(done, u):
                dve.wait_ge(fold_ready, done + 1)
                out = fold_bank[:, 0:TPC * RP].rearrange("p (i d) -> p i d", i=TPC)
                nc.vector.reciprocal(rden[:, :], out[:, :, HD]).then_inc(rden_ready, 1)
                dve.wait_ge(rden_ready, done)
                h, qc = u // NCH, u % NCH
                nc.vector.tensor_tensor(og[:, bass.ds(qc * TPC, TPC), bass.ds(h * HD, HD)], out[:, :, 0:HD],
                                        bcast(rden[:, :], 2, HD), ALU.mult).then_inc(o_ready, 1)

            nc.vector.memset(xlo[64:P, KF, :], 1.0)
            nc.vector.memset(v16[:, :, :, HD:HD + 1], 1.0)
            nc.vector.memset(vr[:, :, :, HD:HD + 1].bitcast(F32), 1.0)
            for n, (s_, credit) in enumerate(((y_ready, 2), (x_loaded, 16), (xlo_ready, 1), (aff_ready, 1), (xc_ready, 1), (exp_done, 2), (pv_done, 1),
                               (o_ready, 1), (fold_ready, 1), (o_stored, 16), (g_max, 1))):
                nc.vector.memset(keep.gate[:, n:n + 1], 0.0).then_inc(s_, credit)

            dve_unsafe = dve.value_load(keep.unsafe[0:1, 0:1], min_val=0, max_val=1)
            with dve.Fori(0, B) as b:
                with dve.Fori(0, NCH) as j:
                    J = b * NCH + j
                    xt = lambda i: xin[:, bass.ds((j % 2) * TPC + i, 1), :].rearrange("p a n -> p (a n)")
                    dve.wait_ge(x_loaded, 16 * (J + 2))
                    nc.vector.memset(keep.gate[:, 13:14], 0.0)
                    for i in range(TPC):
                        for h in range(2):
                            last = nc.vector.bn_stats(stats[:, i, h, :], xt(i)[:, h * HALF:(h + 1) * HALF])
                    last.then_inc(stats_ready, 1)
                    dve.wait_ge(stats_ready, J + 1)
                    nc.vector.memset(keep.gate[:, 14:15], 0.0)
                    for i in range(TPC):
                        last = nc.vector.bn_aggr(mv[:, i, :], stats[:, i, :, :].rearrange("p a b -> p (a b)"))
                    last.then_inc(mv_ready, 1)
                    dve.wait_ge(rstd_ready, J + 1)
                    dve.wait_ge(xlo_ready, J * KC + 1)
                    for i in range(TPC):
                        for c0, c1, at in ((0, H, 0), (KF * P, H, H)):
                            last = nc.vector.tensor_scalar(y[:, i, at:at + c1 - c0], xt(i)[:, c0:c1], mv[:, i, 0:1],
                                                           rstd[:, 1, i:i + 1], ALU.subtract, ALU.mult)
                    last.then_inc(y_ready, 1)
                    for k in range(KC):
                        rows = P if k < KF else KT
                        dve.wait_ge(xhi_ready, J * KC + k + 1)
                        nc.vector.tensor_tensor(xlo[0:rows, k, bass.ds(j * CH, CH)], aff[0:rows, k % 2, :],
                                                xhi[0:rows, k, bass.ds(j * CH, CH)], ALU.subtract).then_inc(xlo_ready, 1)
                with dve.Fori(0, NG) as g:
                    it = b * NG + g
                    for a in range(2):
                        nc.vector.memset(stk[:, a, :, 0:GH, 0:1], 0.0)
                        nc.vector.memset(stk[:, a, :, GH:QK, 0:1], 1.0)
                    for j in range(NCH + 1):
                        C = it * NCH + j
                        if j < NCH:
                            dve.wait_ge(raw_ready, 2 * C + 2)
                            qk = raw[:, :, 0:2 * GW].rearrange("p i (e d) -> p i e d", e=QK)
                            nc.vector.tensor_reduce(total[:, :], qk, AX.X, ALU.add).then_inc(total_ready, 1)
                            dve.wait_ge(v_ready, C + 1)
                            for i in range(TPC):
                                nc.vector.scalar_tensor_tensor(
                                    out=v16[:, j * TPC + i, :, RW:VW], in0=raw[:, i, 2 * GW:3 * GW].rearrange("p (h d) -> p h d", h=GH),
                                    scalar=1.0 / WS, in1=v16[:, j * TPC + i, :, 0:HD], op0=ALU.mult, op1=ALU.subtract)
                            dve.wait_ge(total_ready, C + 1)
                            for i in range(TPC):
                                last = nc.vector.scalar_tensor_tensor(
                                    out=xc[:, i, :, :], in0=bcast(total[:, i * QK:(i + 1) * QK], 2, HD), scalar=-1.0 / HD,
                                    in1=qk[:, i, :, :], op0=ALU.mult, op1=ALU.add)
                            last.then_inc(xc_ready, 1)
                        for jt in ([j - 2] if j >= 2 else []) + ([j - 1] if j == NCH else []):
                            for i in range(2, TPC):
                                dve.wait_ge(tq_ready, (it * NCH + jt) * TPC + i + 1)
                                t0 = (jt * TPC + i) * P
                                nc.vector.tensor_copy(qkT[0:SW, :, t0:t0 + P], tq_bank(i)[0:SW, :].rearrange("p (e n) -> p e n", e=QK)).then_inc(tq_dve, 1)
                        if j < NCH:
                            dve.wait_ge(sq_ready, C + 1)
                            nc.vector.tensor_reduce(ssq[:, 0, :], sq[:, :, :, :], AX.X, ALU.add).then_inc(ssq_ready, 1)
                            dve.wait_ge(hrstd_ready, C + 1)
                            heads = xc[:, :, :, :].rearrange("p i e d -> p (i e) d")
                            nc.vector.scalar_tensor_tensor(out=heads, in0=heads, scalar=HD ** 0.5, in1=bcast(ssq[:, 1, :], 2, HD),
                                                           op0=ALU.mult, op1=ALU.mult).then_inc(yn_ready, 1)
                            dve.wait_ge(yn_ready, C + 1)
                            nc.vector.tensor_tensor(xc[:, :, 0:GH, :], xc[:, :, 0:GH, :], bcast(bcast(keep.gain[:, :], 1, GH), 1, TPC),
                                                    ALU.mult).then_inc(yg_ready, 1)
                            part = stk[:, j % 2, :, :, :]
                            dve.wait_ge(high_ready, 2 * C + 1)
                            for e, at in ((0, 1 + HD), (GH, 1 + 2 * HD)):
                                last = nc.vector.tensor_tensor(part[:, :, e:e + GH, at:at + HD], xc[:, :, e:e + GH, :],
                                                               part[:, :, e:e + GH, 1:1 + HD], ALU.subtract)
                            last.then_inc(low_ready, 1)
                            dve.wait_ge(high_ready, 2 * C + 2)
                    with dve.If(dve_unsafe > 0):
                        with dve.Fori(0, GH * NT) as n:
                            G, h, i = it * GH * NT + n, n // NT, n % NT
                            dve.wait_ge(g_scores, G + 1)
                            nc.vector.tensor_reduce(nmax[:, 0:1], ps[:, 0:NCH, :].rearrange("p a n -> p (a n)"), AX.X, ALU.max,
                                                    negate=True).then_inc(g_max, 1)
                            dve.wait_ge(g_max, G + 2)
                            nc.vector.tensor_scalar(diag[:, :], keep.ident16[:, :], nmax[:, 0:1], None, ALU.mult).then_inc(g_diag, 1)
                            dve.wait_ge(g_row, G + 1)
                            nc.vector.tensor_copy(qkT[0:1, bass.ds(h, 1), bass.ds(i * P, P)].rearrange("p a n -> p (a n)"),
                                                  ps[0:1, 4, 0:P]).then_inc(g_done, 1)
                        dve.nop()
                    dve.wait_ge(o_stored, 16 * (it + 1))
                    for s in low_parts(it * UNITS):
                        pass
                    with dve.Fori(1, UNITS) as u:
                        for s in low_parts(it * UNITS + u):
                            if s == LAG + 3:
                                finish(it * UNITS + u, u - 1)
                    finish((it + 1) * UNITS, UNITS - 1)

        @block.tensor
        def _(pe):
            def scores(unit, h, qc, s):
                pe.wait_ge(exp_done, unit * STEPS + s + 1)
                for a in range(2):
                    last = nc.tensor.matmul(ps[:, 2 * (s % 2) + a, :],
                                            qkT[0:SW, GH + h, (2 * s + a) * P:(2 * s + a + 1) * P],
                                            qkT[0:SW, h, bass.ds(qc * CH, CH)],
                                            start=True, stop=True)
                last.then_inc(scores_ready, 1)

            def sums(unit, h, s):
                pe.wait_ge(plo_ready, unit * STEPS + s + 1)
                for a in range(2):
                    high = p[:, s % NP, a * CH:(a + 1) * CH].bitcast(BF16).rearrange("p (n t) -> p n t", t=2)[:, :, 1]
                    nc.tensor.matmul(acc[0:VW, bass.ds((unit % 2) * CH, CH)],
                                     v16[:, 2 * s + a, h, 0:VW], high,
                                     start=(s == 0 and a == 0), stop=False, skip_group_check=True)
                    last = nc.tensor.matmul(acc[0:RW, bass.ds((unit % 2) * CH, CH)],
                                            vr[:, 2 * s + a, h, 0:RW],
                                            plo[:, s % NP, a * CH:(a + 1) * CH],
                                            start=False, stop=(s == STEPS - 1 and a == 1), skip_group_check=True)
                last.then_inc(pv_done, 1)

            def fold(done):
                pe.wait_ge(oT_ready, done)
                pe.wait_ge(o_ready, done)
                for i in range(TPC):
                    last = nc.tensor.matmul(fold_bank[:, i * RP:(i + 1) * RP], oT[0:VW, i * P:(i + 1) * P], keep.fold[0:VW, :],
                                            start=True, stop=True)
                last.then_inc(fold_ready, 1)

            def transposes(it, j):
                for i in range(TPC):
                    C = it * NCH + j
                    if i == 0:
                        pe.wait_ge(low_ready, C + 1)
                        pe.wait_ge(high_ready, 2 * C + 2)
                    if j == 0 and i == 0:
                        pe.wait_ge(o_ready, it * UNITS + 1)
                    elif j > 0 and i == 0:
                        pe.wait_ge(tq_act, 2 * C)
                        pe.wait_ge(tq_dve, 2 * C)
                    for e in range(QK):
                        last = nc.tensor.transpose(tq_bank(i)[0:SW, e * P:(e + 1) * P], stk[:, j % 2, i, e, 0:SW], keep.ident16[:, :])
                    last.then_inc(tq_ready, 1)

            pe_unsafe = pe.value_load(keep.unsafe[0:1, 0:1], min_val=0, max_val=1)
            with pe.Fori(0, B) as b:
                with pe.Fori(0, NCH) as j:
                    J = b * NCH + j
                    pe.wait_ge(y_ready, J + 3)
                    for k in range(KC):
                        pe.wait_ge(aff_ready, J * KC + k + (0 if k else 1))
                        for i in range(TPC):
                            last = nc.tensor.transpose(ps[:, 4 + k % 2, i * P:(i + 1) * P], y[:, i, k * P:(k + 1) * P], keep.ident[:, :])
                        last.then_inc(xt_ready, 1)
                with pe.Fori(0, NG) as g:
                    it = b * NG + g
                    for j in range(NCH):
                        C = it * NCH + j
                        for i in range(TPC):
                            if j == 0 and i == 0:
                                pe.wait_ge(xlo_ready, (b + 1) * NCH * KC + 1)
                                pe.wait_ge(exp_done, it * UNITS * STEPS + 2)
                            elif j > 0 and i % 2 == 0:
                                pe.wait_ge(raw_ready, 2 * C + i // 2 - 1)
                            t0 = (j * TPC + i) * P
                            ops = list(split_products(xhi, xlo, wq, slice(t0, t0 + P), slice(None)))
                            for n, (l, r) in enumerate(ops):
                                last = nc.tensor.matmul(mm_bank(i)[:, 0:3 * GW], l, r[:, bass.ds(g * 3 * GW, 3 * GW)],
                                                        start=(n == 0), stop=(n == len(ops) - 1))
                            if i % 2:
                                last.then_inc(qkv_ready, 1)
                        if j >= 2:
                            transposes(it, j - 2)
                    transposes(it, NCH - 2)
                    transposes(it, NCH - 1)
                    pe.wait_ge(tq_act, 2 * (it + 1) * NCH)
                    pe.wait_ge(tq_dve, 2 * (it + 1) * NCH)
                    pe.wait_ge(raw_ready, 2 * (it + 1) * NCH)
                    with pe.If(pe_unsafe > 0):
                        with pe.Fori(0, GH * NT) as n:
                            G, h, i = it * GH * NT + n, n // NT, n % NT
                            pe.wait_ge(g_max, G + 1)
                            for c in range(NCH):
                                last = nc.tensor.matmul(ps[:, c, :], qkT[0:RW, bass.ds(h, 1), bass.ds(i * P, P)].rearrange("p a n -> p (a n)"),
                                                        qkT[0:RW, bass.ds(GH + h, 1), c * CH:(c + 1) * CH].rearrange("p a n -> p (a n)"),
                                                        start=True, stop=True)
                            last.then_inc(g_scores, 1)
                            pe.wait_ge(g_diag, G + 1)
                            nc.tensor.matmul(ps[0:1, 4, 0:P], keep.ones16[:, 0:1], diag[:, :], start=True, stop=True).then_inc(g_row, 1)
                        pe.wait_ge(g_done, (it + 1) * GH * NT)
                        pe.nop()

                    def attend(h, qc, first=False):
                        unit = it * UNITS + h * NCH + qc
                        for s in range(STEPS):
                            scores(unit, h, qc, s)
                            if s >= LAG:
                                sums(unit, h, s - LAG)
                            elif not first:
                                sums(unit - 1, h - 1 if isinstance(qc, int) else h, s - LAG + STEPS)
                            if s == LAG + 2 and not first:
                                fold(unit)

                    for h in range(GH):
                        attend(h, 0, first=(h == 0))
                        with pe.Fori(1, NCH) as qc:
                            attend(h, qc)
                    for s in range(STEPS - LAG, STEPS):
                        sums((it + 1) * UNITS - 1, GH - 1, s)
                    fold((it + 1) * UNITS)


def mlp(nc, keep, x, o_dram, out, wp, w1, w2s, b1col):
    with ExitStack() as ctx:
        sb = lambda n, s, d: ctx.enter_context(nc.sbuf_tensor("ml_" + n, s, d))
        sem = lambda n: ctx.enter_context(nc.semaphore("ml_" + n))
        xf = x.rearrange("b n h -> (b n) h")
        outf = out.rearrange("b n h -> (b n) h")
        tok = sb("tok", [P, TPC, KC * P], F32)
        x1 = sb("x1", [P, 2 * TPC, H], F32)
        part = sb("part", [P, 2, H], F32)
        stats = sb("stats", [P, TPC, 2, 6], F32)
        mv = sb("mv", [P, TPC, 2], F32)
        rstd = sb("rstd", [P, 2, TPC], F32)
        aff = sb("aff", [P, 2, CH], F32)
        ohi = sb("ohi", [P, KC, CH], F16)
        olo = sb("olo", [P, KC, CH], F16)
        xhi = sb("xhi", [P, KC, CH], F16)
        xlo = sb("xlo", [P, KC, CH], F16)
        g32 = sb("g32", [P, 2, CH], F32)
        hhi = sb("hhi", [P, FT, CH], F16)
        hlo = sb("hlo", [P, FT, CH], F16)
        ps = ctx.enter_context(nc.psum_tensor("ml_ps", [P, 8, 512], F32))
        up_bank = lambda f: ps[:, f % 2, :]
        pair = lambda r: ps[:, 2 + 2 * (r % 2):4 + 2 * (r % 2), 0:HALF]
        tr_bank = lambda k: ps[:, 6 + k % 2, :]

        o_loaded, x_loaded, stored = sem("o_loaded"), sem("x_loaded"), sem("stored")
        ot_ready, ohi_ready, olo_ready = sem("ot"), sem("ohi"), sem("olo")
        pair_ready, pair_taken, x1_ready = sem("pair"), sem("pair_taken"), sem("x1r")
        stats_ready, mv_ready, var_ready, rstd_ready, y_ready, x1b_ready = (
            sem("stats"), sem("mv"), sem("var"), sem("rstd"), sem("y"), sem("x1b"))
        xt_ready, aff_ready, xhi_ready, xlo_ready = sem("xt"), sem("aff"), sem("xhi"), sem("xlo")
        up_ready, gelu_done, hhi_ready, hlo_ready, out_ready = sem("up"), sem("gelu"), sem("hhi"), sem("hlo"), sem("outr")
        CHUNKS = B * NCH
        block = ctx.enter_context(nc.Block())

        @block.sync
        def _(sp):
            def load(J, first=False):
                if not first:
                    sp.wait_ge(xt_ready, J * KC)
                o = o_dram[bass.ds(J * CH, CH), :].rearrange("(i p) n -> p i n", p=P)
                sp.dma_start(tok[:, :, 0:H], o).then_inc(o_loaded, 16)
                sp.dma_start(tok[:, :, H:KC * P], o[:, :, KF * P:H]).then_inc(o_loaded, 16)
                if not first:
                    sp.wait_ge(stored, 16 * J)
                sp.dma_start(x1[:, bass.ds((J % 2) * TPC, TPC), :],
                             xf[bass.ds(J * CH, CH), :].rearrange("(i p) n -> p i n", p=P)).then_inc(x_loaded, 16)

            def store(J):
                sp.wait_ge(out_ready, TPC * (J + 1))
                sp.dma_start(outf[bass.ds(J * CH, CH), :].rearrange("(i p) n -> p i n", p=P),
                             x1[:, bass.ds((J % 2) * TPC, TPC), :]).then_inc(stored, 16)

            load(0, first=True)
            with sp.Fori(0, CHUNKS - 1) as J:
                load(J + 1)
                store(J)
            store(CHUNKS - 1)
            sp.wait_ge(stored, 16 * (CHUNKS + 1))

        @block.gpsimd
        def _(pool):
            with pool.Fori(0, CHUNKS) as J:
                pool.wait_ge(mv_ready, J + 1)
                pool.tensor_tensor(rstd[:, 0, :], mv[:, :, 1], keep.eps[:, 0:TPC], ALU.add).then_inc(var_ready, 1)
                pool.wait_ge(var_ready, J + 1)
                pool.tensor_tensor(rstd[:, 1, :], rstd[:, 0, :], keep.power[:, 0:TPC], ALU.pow).then_inc(rstd_ready, 1)
                pool.wait_ge(y_ready, J + 1)
                for i in range(TPC):
                    row = x1[:, bass.ds((J % 2) * TPC + i, 1), :].rearrange("p a n -> p (a n)")
                    last = pool.tensor_tensor(row, row, keep.gb2[:, bass.ds(J // NCH, 1), :].rearrange("p a n -> p (a n)"), ALU.add)
                last.then_inc(x1b_ready, 1)

        @block.scalar
        def _(act):
            def high_o(J):
                for k in range(KC):
                    act.wait_ge(ot_ready, J * KC + k + 1)
                    act.copy(ohi[:, k, :], tr_bank(k)).then_inc(ohi_ready, 1)

            def affine(J):
                for k in range(KC):
                    n = J * KC + k
                    act.wait_ge(xt_ready, n + 1)
                    act.wait_ge(xlo_ready, n + (0 if k else 1))
                    b = J // NCH
                    col = lambda v: keep.cols[:, bass.ds(b, 1), v, k:k + 1].rearrange("p b k -> p (b k)")
                    act.activation(aff[:, k % 2, :], tr_bank(k), ACT.Identity, bias=col(2), scale=col(3)).then_inc(aff_ready, 1)
                    act.wait_ge(aff_ready, n + 1)
                    act.copy(xhi[:, k, :], aff[:, k % 2, :]).then_inc(xhi_ready, 1)

            def gelus(J, f0, f1):
                for f in range(f0, f1):
                    m = J * FT + f
                    act.wait_ge(up_ready, m + 1)
                    act.wait_ge(hlo_ready, m + 1)
                    act.activation(g32[:, f % 2, :], up_bank(f), ACT.Gelu_apprx_tanh, bias=b1col[:, f:f + 1],
                                   scale=1.0 / WS).then_inc(gelu_done, 1)

            high_o(0)
            affine(0)
            with act.Fori(0, CHUNKS - 1) as J:
                gelus(J, 0, FT // 2)
                high_o(J + 1)
                gelus(J, FT // 2, FT)
                affine(J + 1)
            gelus(CHUNKS - 1, 0, FT)

        @block.vector
        def _(dve):
            def low_o(J):
                for k in range(KC):
                    rows = P if k < KF else KT
                    dve.wait_ge(ohi_ready, J * KC + k + 1)
                    nc.vector.tensor_tensor(olo[0:rows, k, :], tr_bank(k)[0:rows, :], ohi[0:rows, k, :], ALU.subtract).then_inc(olo_ready, 1)

            def residual(J, i, r, v, after):
                row = x1[:, bass.ds((J % 2) * TPC + i, 1), :].rearrange("p a n -> p (a n)")
                dve.wait_ge(pair_ready, r + 1)
                gate = keep.gates[:, bass.ds(J // NCH, 1), v, :].rearrange("p a (h n) -> p (a h) n", h=2)
                nc.vector.tensor_tensor(part[:, i % 2, :].rearrange("p (h n) -> p h n", h=2), pair(i), gate, ALU.mult).then_inc(pair_taken, 1)
                dve.wait_ge(pair_taken, r + 1)
                nc.vector.tensor_tensor(row, row, part[:, i % 2, :], ALU.add).then_inc(after, 1)

            def project(J, r0):
                dve.wait_ge(x_loaded, 16 * (J + 1))
                for i in range(TPC):
                    residual(J, i, r0 + i, 0, x1_ready)
                dve.wait_ge(x1_ready, TPC * (J + 1))
                nc.vector.memset(keep.gate[:, 15:16], 0.0)
                row = lambda i: x1[:, bass.ds((J % 2) * TPC + i, 1), :].rearrange("p a n -> p (a n)")
                for i in range(TPC):
                    for h in range(2):
                        last = nc.vector.bn_stats(stats[:, i, h, :], row(i)[:, h * HALF:(h + 1) * HALF])
                last.then_inc(stats_ready, 1)
                dve.wait_ge(stats_ready, J + 1)
                nc.vector.memset(keep.gate[:, 14:15], 0.0)
                for i in range(TPC):
                    last = nc.vector.bn_aggr(mv[:, i, :], stats[:, i, :, :].rearrange("p a b -> p (a b)"))
                last.then_inc(mv_ready, 1)
                dve.wait_ge(rstd_ready, J + 1)
                for i in range(TPC):
                    for c0, c1, at in ((0, H, 0), (KF * P, H, H)):
                        last = nc.vector.tensor_scalar(tok[:, i, at:at + c1 - c0], row(i)[:, c0:c1], mv[:, i, 0:1],
                                                       rstd[:, 1, i:i + 1], ALU.subtract, ALU.mult)
                last.then_inc(y_ready, 1)

            def low_x(J):
                for k in range(KC):
                    rows = P if k < KF else KT
                    dve.wait_ge(xhi_ready, J * KC + k + 1)
                    nc.vector.tensor_tensor(xlo[0:rows, k, :], aff[0:rows, k % 2, :], xhi[0:rows, k, :], ALU.subtract).then_inc(xlo_ready, 1)

            def hidden(J, f0, f1):
                for f in range(f0, f1):
                    m = J * FT + f
                    dve.wait_ge(gelu_done, m + 3)
                    nc.vector.tensor_copy(hhi[:, f, :], g32[:, f % 2, :]).then_inc(hhi_ready, 1)
                    dve.wait_ge(hhi_ready, m + 1)
                    nc.vector.tensor_tensor(hlo[:, f, :], g32[:, f % 2, :], hhi[:, f, :], ALU.subtract).then_inc(hlo_ready, 1)

            def down(J, r0):
                dve.wait_ge(x1b_ready, J + 1)
                for i in range(TPC):
                    residual(J, i, r0 + i, 1, out_ready)

            nc.vector.memset(olo[64:P, KF, :], 1.0)
            for n, (s_, credit) in enumerate(((stored, 16), (gelu_done, 2), (hlo_ready, 2), (xlo_ready, 1))):
                nc.vector.memset(keep.gate[:, n:n + 1], 0.0).then_inc(s_, credit)
            low_o(0)
            project(0, 0)
            low_x(0)
            with dve.Fori(0, CHUNKS - 1) as J:
                hidden(J, 0, FT // 2)
                low_o(J + 1)
                hidden(J, FT // 2, FT)
                project(J + 1, TPC + 2 * TPC * J)
                down(J, 2 * TPC + 2 * TPC * J)
                low_x(J + 1)
            hidden(CHUNKS - 1, 0, FT)
            down(CHUNKS - 1, TPC + 2 * TPC * (CHUNKS - 1))

        @block.tensor
        def _(pe):
            def transposes(src, J, k, ready):
                for i in range(TPC):
                    last = nc.tensor.transpose(tr_bank(k)[:, i * P:(i + 1) * P], src[:, i, k * P:(k + 1) * P], keep.ident[:, :])
                last.then_inc(ready, 1)

            def turn_o(J, first=False):
                pe.wait_ge(o_loaded, 32 * (J + 1))
                for k in range(KC):
                    if k >= 2:
                        pe.wait_ge(olo_ready, J * KC + k - 1)
                    elif not first:
                        pe.wait_ge(aff_ready, J * KC)
                    transposes(tok, J, k, ot_ready)

            def turn_y(J):
                pe.wait_ge(y_ready, J + 1)
                for k in range(KC):
                    if k >= 2:
                        pe.wait_ge(aff_ready, J * KC + k - 1)
                    else:
                        pe.wait_ge(olo_ready, (J + 1) * KC)
                    transposes(tok, J, k, xt_ready)

            def by_token(i, r, first, ops):
                if not first or i >= 2:
                    pe.wait_ge(pair_taken, r - 1)
                ops = list(ops)
                for n, (l, w) in enumerate(ops):
                    for half in range(2):
                        last = nc.tensor.matmul(pair(i)[:, half, :], l, w[:, half * HALF:(half + 1) * HALF],
                                                start=(n == 0), stop=(n == len(ops) - 1))
                last.then_inc(pair_ready, 1)

            def project(J, r0, first=False):
                pe.wait_ge(olo_ready, KC * (J + 1))
                for i in range(TPC):
                    by_token(i, r0 + i, first, split_products(ohi, olo, wp, slice(i * P, (i + 1) * P), slice(0, H)))

            def up(J, f0, f1):
                if f0 == 0:
                    pe.wait_ge(xlo_ready, KC * (J + 1) + 1)
                for f in range(f0, f1):
                    m = J * FT + f
                    pe.wait_ge(gelu_done, m + 1)
                    ops = list(split_products(xhi, xlo, w1, slice(0, CH), slice(f * P, (f + 1) * P), bias=False))
                    for n, (xs, w) in enumerate(ops):
                        last = nc.tensor.matmul(up_bank(f), w, xs, start=(n == 0), stop=(n == len(ops) - 1))
                    last.then_inc(up_ready, 1)

            def down(J, r0):
                pe.wait_ge(hlo_ready, FT * (J + 1) + 2)
                for i in range(TPC):
                    t = slice(i * P, (i + 1) * P)
                    by_token(i, r0 + i, False, ((l, w) for f in range(FT) for l, w in (
                        (hhi[:, f, t], w2s[:, 0, f, :]), (hhi[:, f, t], w2s[:, 1, f, :]), (hlo[:, f, t], w2s[:, 0, f, :]))))

            turn_o(0, first=True)
            project(0, 0, first=True)
            turn_y(0)
            with pe.Fori(0, CHUNKS - 1) as J:
                up(J, 0, FT // 2)
                turn_o(J + 1)
                up(J, FT // 2, FT)
                project(J + 1, TPC + 2 * TPC * J)
                down(J, 2 * TPC + 2 * TPC * J)
                turn_y(J + 1)
            up(CHUNKS - 1, 0, FT)
            down(CHUNKS - 1, TPC + 2 * TPC * (CHUNKS - 1))


class Keep:

    def __init__(self, ctx, nc):
        sb = lambda n, s, d: ctx.enter_context(nc.sbuf_tensor(n, s, d))
        self.ident = sb("ident", [P, P], F32)
        self.ident16 = sb("ident16", [P, P], F16)
        self.fold = sb("fold", [P, RP], F32)
        self.power = sb("power", [P, TPC * QK], F32)
        self.eps = sb("eps", [P, TPC], F32)
        self.head_eps = sb("head_eps", [P, TPC * QK], F32)
        self.gate = sb("gate", [P, 16], F32)
        self.ones16 = sb("ones16", [P, 1], F16)
        self.gain = sb("gain", [P, HD], F32)
        self.unsafe = sb("unsafe", [P, 1], I32)
        self.cols = sb("cols", [P, B, 4, KC], F32)
        self.gates = sb("gates", [P, B, 2, H], F32)
        self.gb2 = sb("gb2", [P, B, H], F32)


def dit_block(nc, x, c, w_mod, b_mod, w_qkv, b_qkv, g_q, g_k, w_proj, b_proj, w1, b1, w2, b2, out, o_dram):
    o_flat = o_dram.rearrange("b n h -> (b n) h")
    with ExitStack() as ctx:
        keep = Keep(ctx, nc)
        modulation(nc, keep, c, w_mod, b_mod, g_q, g_k, b2)
        with nc.sbuf_tensor("wq", [P, 10, 3 * H], F16) as wq:
            cut_weights(nc, "q_", [Cut(w_qkv, b_qkv, wq, 3 * H, thirds=True)])
            attention(nc, keep, x, o_flat, wq)
        with (nc.sbuf_tensor("wp", [P, 10, H], F16) as wp, nc.sbuf_tensor("w1c", [P, 9, MLP], F16) as w1c,
              nc.sbuf_tensor("w2s", [P, 2, FT, H], F16) as w2s, nc.sbuf_tensor("b1col", [P, FT], F32) as b1col):
            cut_weights(nc, "m_", [Cut(w_proj, b_proj, wp, H), Cut(w1, None, w1c, MLP)], w2, w2s, b1, b1col)
            mlp(nc, keep, x, o_flat, out, wp, w1c, w2s, b1col)


_INS = ["x", "cond_1152"] + ["L0_cond_" + n for n in
        ("w_mod", "b_mod", "w_qkv", "b_qkv", "g_q", "g_k", "w_proj", "b_proj", "w1", "b1", "w2", "b2")]


def kernel(**inputs):
    import numpy as _np
    import concourse.bacc as _bacc
    from concourse.bass_utils import run_bass_kernel_spmd as _run

    nc = _bacc.Bacc("TRN2", target_bir_lowering=False, num_devices=1)
    arrays, args = {}, []
    for name in _INS:
        a = _np.ascontiguousarray(inputs[name])
        arrays[f"in_{name}"] = a
        args.append(nc.dram_tensor(f"in_{name}", a.shape, mybir.dt.from_np(a.dtype), kind="ExternalInput").ap())
    out = nc.dram_tensor("out_0", (B, N, H), F32, kind="ExternalOutput").ap()
    o_dram = nc.dram_tensor("attention_out", (B, N, H), F32, kind="Internal").ap()
    dit_block(nc, *args, out, o_dram)
    return _run(nc, [arrays], core_ids=[0]).results[0]["out_0"]
```

```python
import concourse.bass as bass
import numpy as np
from concourse import mybir
from contextlib import ExitStack

F32 = mybir.dt.float32
F32R = mybir.dt.float32r
F16 = mybir.dt.float16
BF16 = mybir.dt.bfloat16
I32 = mybir.dt.int32
ALU = mybir.AluOpType
ACT = mybir.ActivationFunctionType
AX = mybir.AxisListType

B, N, H = 2, 2048, 576
NH = 16
HD = H // NH
MLP = 4 * H
EPS = 1e-6
P = 128

KF = H // P
KT = H - KF * P
KC = KF + 1
CH = 512
TPC = CH // P
NCH = N // CH
NT = N // P
GH = 4
NG = NH // GH
GW = GH * HD
QK = 2 * GH
VW = 2 * HD + 1
VP = VW + 1
RW = HD + 1
RP = RW + 1
SW = 3 * HD + 1
SP = 112
FT = MLP // P
HALF = H // 2
WS = 64.0
STEPS = NT // 2
UNITS = GH * NCH
LAG = 3
NP = 4
SAFE = 64.0


def bcast(ap, axis, n):
    v = ap.unsqueeze(axis)
    shape = list(v.shape)
    shape[axis] = n
    return v.broadcast_to(shape)


def modulation(nc, keep, c, w_mod, b_mod, g_q, g_k, b2, gates_dram):
    with ExitStack() as ctx:
        sb = lambda n, s, d: ctx.enter_context(nc.sbuf_tensor(n, s, d))
        sem = lambda n: ctx.enter_context(nc.semaphore(n))
        wm = sb("wm", [P, KC, 6 * H], F32)
        cT = sb("cT", [P, KC, B], F32)
        sT = sb("sT", [P, KC, B], F32)
        eT = sb("eT", [P, KC, B], F32)
        rT = sb("rT", [P, KC, B], F32)
        sbc = sb("sbc", [P, KC, B, P], F32)
        bcol = sb("bcol", [P, 4, KC], F32)
        gates = sb("gates", [P, B, 3, H], F32)
        grow = sb("grow", [P, 2, H], F32)
        b2row = sb("b2row", [P, H], F32)
        gain2 = sb("gain2", [P, 2, HD], F32)
        bound = sb("bound", [P, 2], F32)
        pcol = ctx.enter_context(nc.psum_tensor("pcol", [P, 512], F32))
        prow = ctx.enter_context(nc.psum_tensor("prow", [P, 4, 512], F32))
        c_loaded, w_loaded, small_loaded = sem("c_loaded"), sem("wm_loaded"), sem("small_loaded")
        zeroed, exp_ready, silu_step, silu_ready = sem("zeroed"), sem("silu_exp"), sem("silu_step"), sem("silu_ready")
        cols_ready, rows_ready, rows_taken = sem("cols_ready"), sem("rows_ready"), sem("rows_taken")
        col_step, gain_step = sem("col_step"), sem("gain_step")
        ident_zero, gates_ready, gates_stored = sem("ident_zero"), sem("gates_ready"), sem("gates_stored")
        VECS = (0, 1, 3, 4)
        block = ctx.enter_context(nc.Block())

        @block.sync
        def _(sp):
            with nc.allow_non_contiguous_dma(reason="two short vectors"):
                for b in range(B):
                    sp.dma_start(cT[:, 0:KF, b], c[b, 0:KF * P].rearrange("(k p) -> p k", p=P)).then_inc(c_loaded, 16)
                    sp.dma_start(cT[0:KT, KF, b:b + 1], c[b, KF * P:H].rearrange("(p k) -> p k", k=1)).then_inc(c_loaded, 16)
            for k in range(KC):
                rows = P if k < KF else KT
                sp.dma_start(wm[0:rows, k, :], w_mod[k * P:k * P + rows, :]).then_inc(w_loaded, 16)
            sp.wait_ge(gates_ready, 2 * B)
            sp.dma_start(gates_dram.unsqueeze(0), gates[0:1, :, :, :].rearrange("p b v n -> p (b v n)")).then_inc(gates_stored, 16)
            sp.wait_ge(gates_stored, 16)

        @block.scalar
        def _(act):
            with nc.allow_non_contiguous_dma(reason="short vectors"):
                for n, vec in enumerate(VECS):
                    v = b_mod[vec * H:(vec + 1) * H]
                    act.dma_start(bcol[:, n, 0:KF], v[0:KF * P].rearrange("(k p) -> p k", p=P)).then_inc(small_loaded, 16)
                    for half in range(2):
                        act.dma_start(bcol[half * KT:(half + 1) * KT, n, KF:KC], v[KF * P:H].rearrange("(p k) -> p k", k=1)).then_inc(small_loaded, 16)
            for n, vec in enumerate((2, 5)):
                act.dma_start(grow[:, n, :], bcast(b_mod[vec * H:(vec + 1) * H], 0, P)).then_inc(small_loaded, 16)
            act.dma_start(b2row[:, :], bcast(b2, 0, P)).then_inc(small_loaded, 16)
            act.dma_start(gain2[:, 0, :], bcast(g_q, 0, P)).then_inc(small_loaded, 16)
            act.dma_start(gain2[:, 1, :], bcast(g_k, 0, P)).then_inc(small_loaded, 16)
            act.wait_ge(zeroed, 1)
            act.wait_ge(c_loaded, 16 * 2 * B)
            act.activation(eT[:, :, :], cT[:, :, :], ACT.Exp, scale=-1.0).then_inc(exp_ready, 1)

        @block.gpsimd
        def _(pool):
            pool.memset(keep.ident[:, :], 0.0).then_inc(ident_zero, 1)
            pool.memset(keep.ident16[:, :], 0.0).then_inc(ident_zero, 1)
            pool.memset(keep.fold[:, :], 0.0).then_inc(ident_zero, 1)
            pool.memset(keep.power[:, :], -0.5)
            pool.memset(keep.eps[:, :], EPS)
            pool.memset(keep.head_eps[:, :], HD * EPS * WS * WS)
            pool.memset(keep.ones16[:, :], 1.0)
            pool.wait_ge(ident_zero, 3)
            for m in (keep.ident, keep.ident16):
                pool.affine_select(out=m[:, :], in_=m[:, :], compare_op=ALU.not_equal, fill=1.0,
                                   base=0, pattern=[[-1, P]], channel_multiplier=1)
            pool.affine_select(out=keep.fold[:, :], in_=keep.fold[:, :], compare_op=ALU.not_equal, fill=1.0,
                               base=0, pattern=[[-1, RP]], channel_multiplier=1).then_inc(ident_zero, 1)
            pool.wait_ge(ident_zero, 4)
            pool.affine_select(out=keep.fold[:, 0:HD], in_=keep.fold[:, 0:HD], compare_op=ALU.not_equal, fill=1.0,
                               base=-RW, pattern=[[-1, HD]], channel_multiplier=1)

        @block.vector
        def _(dve):
            nc.vector.memset(cT[KT:P, KF, :], 0.0).then_inc(zeroed, 1)
            dve.wait_ge(exp_ready, 1)
            nc.vector.tensor_scalar_add(rT[:, :, :], eT[:, :, :], 1.0).then_inc(silu_step, 1)
            dve.wait_ge(silu_step, 1)
            nc.vector.reciprocal(eT[:, :, :], rT[:, :, :]).then_inc(silu_step, 1)
            dve.wait_ge(silu_step, 2)
            nc.vector.tensor_tensor(sT[:, :, :], cT[:, :, :], eT[:, :, :], ALU.mult).then_inc(silu_step, 1)
            dve.wait_ge(silu_step, 3)
            nc.vector.tensor_copy(sbc[:, :, :, :].rearrange("p k b n -> p (k b) n"),
                                  bcast(sT[:, :, :].rearrange("p k b -> p (k b)"), 2, P)).then_inc(silu_ready, 1)
            dve.wait_ge(small_loaded, 16 * 17)
            nc.vector.scalar_tensor_tensor(out=keep.gain[:, :], in0=gain2[:, 0, :], scalar=HD ** -0.5,
                                           in1=gain2[:, 1, :], op0=ALU.mult, op1=ALU.mult).then_inc(gain_step, 1)
            dve.wait_ge(gain_step, 1)
            nc.vector.tensor_reduce(bound[:, 0:1], keep.gain[:, :], AX.X, ALU.max,
                                    apply_absolute_value=True).then_inc(gain_step, 1)
            dve.wait_ge(gain_step, 2)
            nc.vector.tensor_scalar(bound[:, 1:2], bound[:, 0:1], float(HD), SAFE, ALU.mult, ALU.is_gt).then_inc(gain_step, 1)
            dve.wait_ge(gain_step, 3)
            nc.vector.tensor_copy(keep.unsafe[:, :], bound[:, 1:2])
            dve.wait_ge(cols_ready, 1)
            for b in range(B):
                nc.vector.tensor_tensor(keep.cols[:, b, :, :], pcol[:, 0:4 * KC * B].rearrange("p (v k b) -> p b v k", v=4, b=B)[:, b, :, :],
                                        bcol[:, :, :], ALU.add).then_inc(col_step, 1)
            dve.wait_ge(col_step, B)
            for v in (1, 3):
                nc.vector.tensor_scalar_add(keep.cols[:, :, v, :], keep.cols[:, :, v, :], 1.0)
            for n in range(2 * B):
                b, v = n // 2, n % 2
                dve.wait_ge(rows_ready, n + 1)
                nc.vector.tensor_tensor(gates[:, b, v, :].rearrange("p (h n) -> p h n", h=2), prow[:, (n % 2) * 2:(n % 2) * 2 + 2, 0:HALF],
                                        grow[:, v, :].rearrange("p (h n) -> p h n", h=2), ALU.add).then_inc(rows_taken, 1)
                dve.wait_ge(rows_taken, n + 1)
                if v == 1:
                    nc.vector.tensor_tensor(gates[:, b, 2, :], gates[:, b, v, :], b2row[:, :], ALU.mult).then_inc(gain_step, 1)
                    dve.wait_ge(gain_step, 4 + b)
                nc.vector.tensor_scalar_mul(gates[:, b, v, :], gates[:, b, v, :], 1.0 / WS).then_inc(gates_ready, 1)

        @block.tensor
        def _(pe):
            pe.wait_ge(silu_ready, 1)
            pe.wait_ge(w_loaded, 16 * KC)
            for n, vec in enumerate(VECS):
                for m in range(KC + 1):
                    f, rows, at = min(m, KF), P if m < KF else KT, KT if m == KC else 0
                    for k in range(KC):
                        kr = P if k < KF else KT
                        last = nc.tensor.matmul(pcol[at:at + rows, (n * KC + f) * B:(n * KC + f + 1) * B],
                                                wm[0:kr, k, vec * H + f * P:vec * H + f * P + rows], sT[0:kr, k, :],
                                                start=(k == 0), stop=(k == KC - 1))
            last.then_inc(cols_ready, 1)
            for n in range(2 * B):
                b, vec = n // 2, (2, 5)[n % 2]
                if n >= 2:
                    pe.wait_ge(rows_taken, n - 1)
                for half in range(2):
                    for k in range(KC):
                        kr = P if k < KF else KT
                        last = nc.tensor.matmul(prow[:, (n % 2) * 2 + half, 0:HALF], sbc[0:kr, k, b, :],
                                                wm[0:kr, k, vec * H + half * HALF:vec * H + (half + 1) * HALF],
                                                start=(k == 0), stop=(k == KC - 1))
                last.then_inc(rows_ready, 1)


class Cut:

    def __init__(self, w, bias, out, cols, thirds=False):
        self.w, self.bias, self.out, self.cols, self.thirds = w, bias, out, cols, thirds
        self.width = 2 * H if cols > 3 * H else H

    def part(self, p0, p1, slot, c0):
        row = self.out[p0:p1, slot, :]
        if self.thirds:
            return row.rearrange("p (g t j) -> p g t j", g=NG, t=3)[:, :, c0 // H, :]
        return row[:, c0:c0 + self.width].rearrange("p (g j) -> p g j", g=NG)

    def grouped(self, ap):
        return ap[:, 0:self.width].rearrange("p (g j) -> p g j", g=NG)


def cut_weights(nc, tag, mats, w2=None, w2s=None, b1=None, b1col=None):
    with ExitStack() as ctx:
        sb = lambda n, s, d: ctx.enter_context(nc.sbuf_tensor(tag + n, s, d))
        sem = lambda n: ctx.enter_context(nc.semaphore(tag + n))
        pieces = [(m, c0) for m in mats for c0 in range(0, m.cols, m.width)]
        wide = max(m.width for m in mats)
        stage = sb("stage", [P, 2, KC * wide], F32)
        tails = sb("tails", [P, 2, wide], F16)
        biases = sb("biases", [P, 2, wide], F32)
        bias_hi = sb("bias_hi", [P, 2, wide], F16)
        full, tail, bias_in = [[sem(f"{n}{i}") for i in range(2)] for n in ("full", "tail", "bias")]
        high, low, blank, b1_in = sem("high"), sem("low"), sem("blank"), sem("b1_in")
        W2P = 4 if w2 is not None else 0
        lots = [5, 5, 4, 4]
        lot_at = [sum(lots[:n]) for n in range(4)]
        w2_in = [sem(f"w2in{i}") for i in range(2)]
        n_pieces = len(pieces)
        block = ctx.enter_context(nc.Block())

        def staged(s, width):
            return stage[:, s, 0:KC * width].rearrange("p (k n) -> p k n", k=KC)

        def lot(n):
            a, m = lot_at[n], lots[n]
            return (stage[:, (n_pieces + n) % 2, 0:m * H], w2s[:, 0, a:a + m, :].rearrange("p f n -> p (f n)"),
                    w2s[:, 1, a:a + m, :].rearrange("p f n -> p (f n)"))

        @block.sync
        def _(sp):
            for n, (m, c0) in enumerate(pieces):
                if n >= 2:
                    sp.wait_ge(low, n - 1)
                s, w = n % 2, m.width
                sp.dma_start(staged(s, w)[:, 0:KF, :], m.w[0:KF * P, c0:c0 + w].rearrange("(k p) n -> p k n", p=P)).then_inc(full[s], 16)
                for half in range(2):
                    sp.dma_start(staged(s, w)[half * KT:(half + 1) * KT, KF, :], m.w[KF * P:H, c0:c0 + w]).then_inc(tail[s], 16)
                if m.bias is not None:
                    for row in (64, 96):
                        sp.dma_start(biases[row:row + 1, s, 0:w], m.bias[c0:c0 + w].unsqueeze(0)).then_inc(bias_in[s], 16)
            if b1 is not None:
                with nc.allow_non_contiguous_dma(reason="a short vector"):
                    sp.dma_start(b1col[:, :], b1.rearrange("(f p) -> p f", p=P)).then_inc(b1_in, 16)
            for n in range(W2P):
                if n_pieces + n >= 2:
                    sp.wait_ge(low, n_pieces + n - 1)
                a, m = lot_at[n], lots[n]
                sp.dma_start(lot(n)[0].rearrange("p (f n) -> p f n", n=H),
                             w2[a * P:(a + m) * P, :].rearrange("(f p) n -> p f n", p=P)).then_inc(w2_in[n % 2], 16)
            if b1 is not None:
                sp.wait_ge(b1_in, 16)

        def loaded(eng, n):
            s = n % 2
            eng.wait_ge(full[s], 16 * (n // 2 + 1))
            eng.wait_ge(tail[s], 32 * (n // 2 + 1))
            with_bias = sum(1 for q in range(s, n + 1, 2) if pieces[q][0].bias is not None)
            if with_bias:
                eng.wait_ge(bias_in[s], 32 * with_bias)

        @block.scalar
        def _(act):
            blanks = 0
            for n, (m, c0) in enumerate(pieces):
                s, x = n % 2, staged(n % 2, m.width)
                loaded(act, n)
                if n >= 2:
                    act.wait_ge(low, n - 1)
                for k in range(KF):
                    act.activation(m.part(0, P, k, c0), m.grouped(x[:, k, :]), ACT.Copy, scale=WS)
                act.activation(m.part(0, KT, 8, c0), m.grouped(x[0:KT, KF, :]), ACT.Copy, scale=WS)
                if m.bias is not None:
                    blanks += c0 == 0
                    act.wait_ge(blank, blanks)
                    act.activation(m.part(0, KT, 9, c0), m.grouped(x[0:KT, KF, :]), ACT.Copy, scale=WS)
                    act.activation(m.part(64, 65, 9, c0), m.grouped(biases[64:65, s, :]), ACT.Copy, scale=WS)
                    act.activation(bias_hi[96:97, s, 0:m.width], biases[96:97, s, 0:m.width], ACT.Copy, scale=WS)
                act.activation(tails[KT:P, s, 0:m.width], x[KT:P, KF, :], ACT.Copy, scale=WS).then_inc(high, 1)
            for n in range(W2P):
                act.wait_ge(w2_in[n % 2], 16 * (n // 2 + 1))
                act.activation(lot(n)[1], lot(n)[0], ACT.Copy, scale=WS).then_inc(high, 1)

        @block.vector
        def _(dve):
            def lower(out, src, hi):
                return nc.vector.scalar_tensor_tensor(out=out, in0=src, scalar=WS, in1=hi, op0=ALU.mult, op1=ALU.subtract)

            for m in mats:
                if m.bias is not None:
                    nc.vector.memset(m.out[64:P, 9, :], 0.0).then_inc(blank, 1)
            for n, (m, c0) in enumerate(pieces):
                s, x = n % 2, staged(n % 2, m.width)
                loaded(dve, n)
                dve.wait_ge(high, n + 1)
                for k in range(KF):
                    lower(m.part(0, P, KF + k, c0), m.grouped(x[:, k, :]), m.part(0, P, k, c0))
                last = lower(m.part(KT, P, 8, c0), m.grouped(x[KT:P, KF, :]), m.grouped(tails[KT:P, s, :]))
                if m.bias is not None:
                    last = lower(m.part(96, 97, 9, c0), m.grouped(biases[96:97, s, :]), m.grouped(bias_hi[96:97, s, :]))
                last.then_inc(low, 1)
            for n in range(W2P):
                dve.wait_ge(w2_in[n % 2], 16 * (n // 2 + 1))
                dve.wait_ge(high, n_pieces + n + 1)
                lower(lot(n)[2], lot(n)[0], lot(n)[1]).then_inc(low, 1)


def split_products(xhi, xlo, w, tokens, cols, bias=True):
    for k in range(KF):
        yield xhi[:, k, tokens], w[:, k, cols]
        yield xhi[:, k, tokens], w[:, KF + k, cols]
        yield xlo[:, k, tokens], w[:, k, cols]
    yield xhi[:, KF, tokens], w[:, 8, cols]
    if bias:
        yield xlo[0:97, KF, tokens], w[0:97, 9, cols]
    else:
        yield xlo[0:KT, KF, tokens], w[0:KT, 8, cols]


def attention(nc, keep, x, o_dram, wq):
    with ExitStack() as ctx:
        sb = lambda n, s, d: ctx.enter_context(nc.sbuf_tensor("at_" + n, s, d))
        sem = lambda n: ctx.enter_context(nc.semaphore("at_" + n))
        xf = x.rearrange("b n h -> (b n) h")
        stats = sb("stats", [P, TPC, 2, 6], F32)
        mv = sb("mv", [P, TPC, 2], F32)
        rstd = sb("rstd", [P, 2, TPC], F32)
        xhi = sb("xhi", [P, KC, N], F16)
        xlo = sb("xlo", [P, KC, N], F16)
        total = sb("total", [P, TPC * QK], F32)
        ssq = sb("ssq", [P, 2, TPC * QK], F32)
        qkT = sb("qkT", [SP, 2 * QK, N], F16)
        v32 = sb("v32", [P, 2 * NT, GH, HD], F32)
        v16 = sb("v16", [P, 2, NT, VP], F16)
        vr = sb("vr", [P, 2, NT, RP], F32R)
        traw = sb("traw", [P, QK, HD], F32)
        txc = sb("txc", [P, QK, HD], F32)
        ttotal = sb("ttotal", [P, QK], F32)
        diag = txc[:, :, :].rearrange("p e d -> p (e d)").bitcast(F16)[:, 0:P]
        tssq = sb("tssq", [P, 2, QK], F32)
        tstk = sb("tstk", [P, QK, SP], F16)
        oT = sb("oT", [VW, CH], F32)
        rden = sb("rden", [P, TPC], F32)
        og = sb("og", [P, NT, HD], F32)
        pgate = keep.gate[:, 20:24]
        nmax = sb("nmax", [P, 2], F32)

        def overlaid(*sets):
            size = lambda tensors: sum(-(-int(np.prod(shape[1:])) * (2 if d == F16 else 4) // 32) * 32 for _, shape, d in tensors)
            pad = max(map(size, sets)) - size(sets[-1])
            if pad:
                sets = (*sets[:-1], [*sets[-1], (sets[-1][0][0] + "_pad", [P, pad // 4], F32)])
            made = []
            for n, tensors in enumerate(sets):
                with ExitStack() as one:
                    place = ctx if n == len(sets) - 1 else one
                    made += [place.enter_context(nc.sbuf_tensor("at_" + name, shape, d)) for name, shape, d in tensors]
            return made

        xin, y, aff, stk, raw, xc, sq, p, plo, *_ = overlaid(
            [("xin", [P, 2 * TPC, H], F32),
             ("y", [P, TPC, KC * P], F32),
             ("aff", [P, 2, CH], F32)],
            [("stk", [P, 2, TPC, QK, SP], F16),
             ("raw", [P, TPC, 3 * GW], F32), ("xc", [P, TPC, QK, HD], F32), ("sq", [P, TPC, QK, HD], F32)],
            [("p", [P, NP, 2 * CH], F32),
             ("plo", [P, NP, 2 * CH], F32R)])
        ps = ctx.enter_context(nc.psum_tensor("at_ps", [P, 8, 512], F32))
        mm_bank = lambda i: ps[:, i, :]
        tq_bank = lambda i: ps[:, 4 + i, :].bitcast(F16)
        acc = ps[:, 4:6, :].rearrange("p a n -> p (a n)")
        fold_bank = ps[:, 6, :]
        tile_bank = ps[:, 7, :]

        x_loaded = sem("x_loaded")
        stats_ready, mv_ready, var_ready, rstd_ready, y_ready = sem("stats"), sem("mv"), sem("var"), sem("rstd"), sem("y")
        xt_ready, aff_ready, xhi_ready, xlo_ready = sem("xt"), sem("aff"), sem("xhi"), sem("xlo")
        qkv_ready, raw_ready = sem("qkv"), sem("raw")
        v_ready, total_ready, xc_ready, sq_ready, ssq_ready, msq_ready, hrstd_ready = (
            sem("v"), sem("total"), sem("xc"), sem("sq"), sem("ssq"), sem("msq"), sem("hrstd"))
        yn_ready, yg_ready, high_ready, low_ready = sem("yn"), sem("yg"), sem("high"), sem("low")
        tq_ready, tq_act, tq_dve, fixed = sem("tq"), sem("tq_act"), sem("tq_dve"), sem("fixed")
        scores_ready, exp_done, plo_ready, pv_done = sem("scores"), sem("exp"), sem("plo"), sem("pv")
        oT_ready, fold_ready, rden_ready, o_ready, o_stored = sem("oT"), sem("foldr"), sem("rden"), sem("o"), sem("o_stored")
        t_mm, t_raw, t_total, t_xc, t_sq, t_ssq, t_msq, t_rstd, t_yn, t_yg, t_high, t_low, t_tq, t_evac = (
            sem("t_" + n) for n in ("mm", "raw", "total", "xc", "sq", "ssq", "msq", "rstd", "yn", "yg", "high", "low", "tq", "evac"))
        vh_ready, head_ready = sem("vh"), sem("head")
        g_scores, g_max, g_diag, g_row, g_done = sem("g_scores"), sem("g_max"), sem("g_diag"), sem("g_row"), sem("g_done")

        block = ctx.enter_context(nc.Block())

        @block.sync
        def _(sp):
            with sp.Fori(0, B) as b:
                with sp.Fori(0, NCH) as j:
                    J = b * NCH + j
                    sp.wait_ge(y_ready, J + 1)
                    sp.wait_ge(x_loaded, 16 * J + 16)
                    sp.dma_start(xin[:, bass.ds((j % 2) * TPC, TPC), :],
                                 xf[bass.ds(b * N + j * CH, CH), :].rearrange("(i p) n -> p i n", p=P)).then_inc(x_loaded, 16)
                with sp.Fori(0, NH) as h:
                    sp.wait_ge(o_ready, (b * NH + h + 1) * NCH + 1)
                    sp.dma_start(o_dram[bass.ds(b * N, N), bass.ds(h * HD, HD)].rearrange("(t p) n -> p t n", p=P),
                                 og[:, :, :]).then_inc(o_stored, 16)
            sp.wait_ge(o_stored, 16 * (B * NH + 1))

        @block.gpsimd
        def _(pool):
            def head(it, part, h, done):
                v = v32[:, bass.ds(part * NT, NT), h, :]
                gate = lambda n: pool.tensor_tensor(pgate[:, n:n + 1], keep.eps[:, 0:1], keep.eps[:, 0:1], ALU.add)
                pool.wait_ge(pv_done, done * STEPS + 1)
                gate(0)
                pool.tensor_copy(vr[:, h % 2, :, 0:HD], v)
                pool.tensor_copy(v16[:, h % 2, :, 0:HD], v).then_inc(vh_ready, 1)
                pool.wait_ge(vh_ready, it * GH + h + 1)
                gate(1)
                pool.tensor_tensor(v16[:, h % 2, :, RW:VW], v, v16[:, h % 2, :, 0:HD], ALU.subtract).then_inc(head_ready, 1)

            with pool.Fori(0, B) as b:
                with pool.Fori(0, NCH) as j:
                    J = b * NCH + j
                    pool.wait_ge(mv_ready, J + 1)
                    pool.tensor_tensor(rstd[:, 0, :], mv[:, :, 1], keep.eps[:, 0:TPC], ALU.add).then_inc(var_ready, 1)
                    pool.wait_ge(var_ready, J + 1)
                    pool.tensor_tensor(rstd[:, 1, :], rstd[:, 0, :], keep.power[:, 0:TPC], ALU.pow).then_inc(rstd_ready, 1)
                with pool.Fori(0, NCH) as j:
                    C = b * NCH + j
                    pool.wait_ge(ssq_ready, C + 1)
                    pool.tensor_tensor(ssq[:, 1, :], ssq[:, 0, :], keep.head_eps[:, :], ALU.add).then_inc(msq_ready, 1)
                    pool.wait_ge(msq_ready, C + 1)
                    pool.tensor_tensor(ssq[:, 1, :], ssq[:, 1, :], keep.power[:, 0:TPC * QK], ALU.pow).then_inc(hrstd_ready, 1)
                pool.wait_ge(v_ready, (b + 1) * NCH)
                pool.tensor_tensor(pgate[:, 2:3], keep.eps[:, 0:1], keep.eps[:, 0:1], ALU.add)
                head(b * NG, 0, 0, b * NG * UNITS)
                with pool.Fori(0, NG - 1) as g:
                    it = b * NG + g
                    for h in range(GH):
                        for qc in range(NCH):
                            X = (b * (NG - 1) + g) * NT + h * NCH + qc
                            pool.wait_ge(t_ssq, X + 2)
                            pool.tensor_tensor(tssq[:, 1, :], tssq[:, 0, :], keep.head_eps[:, 0:QK], ALU.add).then_inc(t_msq, 1)
                            pool.wait_ge(t_msq, X + 1)
                            pool.tensor_tensor(tssq[:, 1, :], tssq[:, 1, :], keep.power[:, 0:QK], ALU.pow).then_inc(t_rstd, 1)
                            if qc == 2 and h + 1 < GH:
                                head(it, g % 2, h + 1, it * UNITS + h * NCH)
                    pool.wait_ge(t_raw, (b * (NG - 1) + g + 1) * NT)
                    pool.tensor_tensor(pgate[:, 3:4], keep.eps[:, 0:1], keep.eps[:, 0:1], ALU.add)
                    head(it + 1, (g + 1) % 2, 0, it * UNITS + (GH - 1) * NCH)
                for h in range(1, GH):
                    head(b * NG + NG - 1, (NG - 1) % 2, h, (b * NG + NG - 1) * UNITS + (h - 1) * NCH)

        @block.scalar
        def _(act):
            def store_tq(bank, i, j):
                t0 = (j * TPC + i) * P
                return act.copy(qkT[0:SW, 0:QK, t0:t0 + P], bank[0:SW, :].rearrange("p (e n) -> p e n", e=QK))

            def tile_high(X):
                act.wait_ge(t_yg, X)
                act.wait_ge(t_tq, X)
                act.copy(tstk[:, :, 1:1 + HD], txc[:, :, :]).then_inc(t_high, 1)

            def tile_high_again():
                act.copy(tstk[:, 0:GH, 1 + 2 * HD:SW], txc[:, 0:GH, :])
                act.copy(tstk[:, GH:QK, 1 + HD:1 + 2 * HD], txc[:, GH:QK, :]).then_inc(t_high, 1)

            def tile_store(X, part, tile):
                act.wait_ge(t_tq, X + 1)
                act.copy(qkT[0:SW, bass.ds(part * QK, QK), bass.ds(tile * P, P)],
                         tile_bank.bitcast(F16)[0:SW, :].rearrange("p (e n) -> p e n", e=QK)).then_inc(t_evac, 1)

            def keep_oT(done):
                act.wait_ge(pv_done, done * STEPS + 1)
                act.wait_ge(fold_ready, done)
                act.copy(oT[:, :], acc[0:VW, bass.ds(((done + 1) % 2) * CH, CH)]).then_inc(oT_ready, 1)

            def exps(unit, u, first=False, cut=None):
                for s in range(STEPS):
                    n = unit * STEPS + s
                    if s == LAG and not first:
                        keep_oT(unit)
                    act.wait_ge(scores_ready, n + 1)
                    act.wait_ge(pv_done, n + 1 - NP + 1 if not first or s >= NP else unit * STEPS + 1)
                    act.activation(p[:, s % NP, :], ps[:, 2 * (s % 2):2 * (s % 2) + 2, :].rearrange("p a n -> p (a n)"),
                                   ACT.Exp).then_inc(exp_done, 1)
                    if cut is None:
                        continue
                    X, part = cut
                    if s == 0 and not first:
                        tile_high(X)
                    if s == 1 and not first:
                        tile_high_again()
                    if s == 2:
                        act.wait_ge(t_mm, X + 1)
                        act.wait_ge(t_ssq, X + 1)
                        act.activation(v32[:, bass.ds(part * NT + u, 1), :, :].rearrange("p a h d -> p (a h d)"), tile_bank[:, 2 * GW:3 * GW],
                                       ACT.Copy, scale=1.0 / WS)
                        act.copy(traw[:, :, :].rearrange("p e d -> p (e d)"), tile_bank[:, 0:2 * GW]).then_inc(t_raw, 1)
                    if s == 4:
                        act.wait_ge(t_xc, X + 1)
                        act.activation(traw[:, :, :], txc[:, :, :], ACT.Square).then_inc(t_sq, 1)
                    if s == 5 and not first:
                        tile_store(X, part, u - 1)

            with act.Fori(0, B) as b:
                with act.Fori(0, NCH) as j:
                    J = b * NCH + j
                    for k in range(KC):
                        n = J * KC + k
                        act.wait_ge(xt_ready, n + 1)
                        act.wait_ge(xlo_ready, n + (0 if k else 1))
                        act.activation(aff[:, k % 2, :], ps[:, 4 + k % 2, :], ACT.Identity,
                                       bias=keep.cols[:, bass.ds(b, 1), 0, k:k + 1].rearrange("p b k -> p (b k)"),
                                       scale=keep.cols[:, bass.ds(b, 1), 1, k:k + 1].rearrange("p b k -> p (b k)")).then_inc(aff_ready, 1)
                        act.wait_ge(aff_ready, n + 2)
                        act.copy(xhi[:, k, bass.ds(j * CH, CH)], aff[:, k % 2, :]).then_inc(xhi_ready, 1)
                act.wait_ge(pv_done, b * NG * UNITS * STEPS + 1)
                for j in range(NCH + 1):
                    C = b * NCH + j
                    if j < NCH:
                        for hh in range(2):
                            act.wait_ge(qkv_ready, 2 * C + hh + 1)
                            if hh == 0:
                                act.wait_ge(xc_ready, C + 1)
                            act.copy(raw[:, 2 * hh:2 * hh + 2, :], ps[:, 2 * hh:2 * hh + 2, 0:3 * GW]).then_inc(raw_ready, 1)
                        act.wait_ge(raw_ready, 2 * C + 2)
                        act.activation(v32[:, j * TPC:(j + 1) * TPC, :, :].rearrange("p i h d -> p i (h d)"), raw[:, :, 2 * GW:3 * GW],
                                       ACT.Copy, scale=1.0 / WS).then_inc(v_ready, 1)
                    for jt in ([j - 2] if j >= 2 else []) + ([j - 1] if j == NCH else []):
                        for i in range(2):
                            act.wait_ge(tq_ready, (b * NCH + jt) * TPC + i + 1)
                            store_tq(tq_bank(i), i, jt).then_inc(tq_act, 1)
                    if j < NCH:
                        act.wait_ge(xc_ready, C + 2)
                        act.activation(sq[:, :, :, :].rearrange("p a b c -> p (a b c)"), xc[:, :, :, :].rearrange("p a b c -> p (a b c)"),
                                       ACT.Square).then_inc(sq_ready, 1)
                        if j >= 2:
                            act.wait_ge(tq_ready, (C - 1) * TPC)
                        act.wait_ge(yg_ready, C + 1)
                        part = stk[:, j % 2, :, :, :]
                        act.copy(part[:, :, :, 1:1 + HD], xc[:, :, :, :]).then_inc(high_ready, 1)
                        act.copy(part[:, :, 0:GH, 1 + 2 * HD:SW], xc[:, :, 0:GH, :])
                        act.copy(part[:, :, GH:QK, 1 + HD:1 + 2 * HD], xc[:, :, GH:QK, :]).then_inc(high_ready, 1)

                def group(g, part, cut):
                    it = b * NG + g
                    X = (b * (NG - 1) + g) * NT
                    exps(it * UNITS, 0, True, (X, part) if cut else None)
                    with act.Fori(1, UNITS) as u:
                        exps(it * UNITS + u, u, False, (X + u, part) if cut else None)
                    if cut:
                        tile_high(X + NT)
                        tile_high_again()
                    keep_oT((it + 1) * UNITS)
                    if cut:
                        tile_store(X + NT, part, NT - 1)

                with act.Fori(0, NG - 1) as g:
                    group(g, (g + 1) % 2, True)
                group(NG - 1, 0, False)

        @block.vector
        def _(dve):
            def low_parts(unit, u, first=False, cut=None):
                for s in range(STEPS):
                    n, X = unit * STEPS + s, cut
                    if cut is not None and s == 3:
                        dve.wait_ge(t_raw, X + 1)
                        nc.vector.tensor_reduce(ttotal[:, :], traw[:, :, :], AX.X, ALU.add).then_inc(t_total, 1)
                    if cut is not None and s == 7:
                        dve.wait_ge(t_rstd, X + 1)
                        nc.vector.scalar_tensor_tensor(out=txc[:, :, :], in0=txc[:, :, :], scalar=HD ** 0.5, in1=bcast(tssq[:, 1, :], 2, HD),
                                                       op0=ALU.mult, op1=ALU.mult).then_inc(t_yn, 1)
                    dve.wait_ge(exp_done, n + 3)
                    high = p[:, s % NP, :].bitcast(BF16).rearrange("p (n t) -> p n t", t=2)[:, :, 1]
                    nc.vector.tensor_tensor(plo[:, s % NP, :], p[:, s % NP, :], high, ALU.subtract).then_inc(plo_ready, 1)
                    if s == LAG + 3 and not first:
                        finish(unit, u - 1)
                    if cut is None:
                        continue
                    if s == 1 and not first:
                        tile_low(X)
                    if s == 3:
                        dve.wait_ge(t_total, X + 1)
                        dve.wait_ge(t_high, 2 * X + 1)
                        nc.vector.scalar_tensor_tensor(out=txc[:, :, :], in0=bcast(ttotal[:, :], 2, HD), scalar=-1.0 / HD, in1=traw[:, :, :],
                                                       op0=ALU.mult, op1=ALU.add).then_inc(t_xc, 1)
                    if s == 5:
                        dve.wait_ge(t_sq, X + 1)
                        nc.vector.tensor_reduce(tssq[:, 0, :], traw[:, :, :], AX.X, ALU.add).then_inc(t_ssq, 1)
                    if s == 7:
                        dve.wait_ge(t_yn, X + 1)
                        nc.vector.tensor_tensor(txc[:, 0:GH, :], txc[:, 0:GH, :], bcast(keep.gain[:, :], 1, GH), ALU.mult).then_inc(t_yg, 1)

            def tile_low(X):
                dve.wait_ge(t_high, 2 * X)
                for e, at in ((0, 1 + HD), (GH, 1 + 2 * HD)):
                    last = nc.vector.tensor_tensor(tstk[:, e:e + GH, at:at + HD], txc[:, e:e + GH, :], tstk[:, e:e + GH, 1:1 + HD], ALU.subtract)
                last.then_inc(t_low, 1)

            def finish(done, u):
                dve.wait_ge(fold_ready, done + 1)
                out = fold_bank[:, 0:TPC * RP].rearrange("p (i d) -> p i d", i=TPC)
                nc.vector.reciprocal(rden[:, :], out[:, :, HD]).then_inc(rden_ready, 1)
                dve.wait_ge(rden_ready, done)
                dve.wait_ge(o_stored, 16 * ((done - 1) // NCH + 1))
                nc.vector.tensor_tensor(og[:, bass.ds((u % NCH) * TPC, TPC), :], out[:, :, 0:HD],
                                        bcast(rden[:, :], 2, HD), ALU.mult).then_inc(o_ready, 1)

            nc.vector.memset(xlo[64:P, KF, :], 1.0)
            nc.vector.memset(v16[:, :, :, HD:HD + 1], 1.0)
            nc.vector.memset(tstk[:, 0:GH, 0:1], 0.0)
            nc.vector.memset(tstk[:, GH:QK, 0:1], 1.0)
            nc.vector.memset(vr[:, :, :, HD:HD + 1].bitcast(F32), 1.0)
            for n, (s_, credit) in enumerate(((y_ready, 2), (x_loaded, 16), (xlo_ready, 1), (aff_ready, 1), (xc_ready, 1), (exp_done, 2), (pv_done, 1),
                               (o_ready, 1), (fold_ready, 1), (o_stored, 16), (g_max, 1),
                                               (t_ssq, 1), (t_high, 1), (t_tq, 1), (t_evac, 2))):
                nc.vector.memset(keep.gate[:, n:n + 1], 0.0).then_inc(s_, credit)

            dve_unsafe = dve.value_load(keep.unsafe[0:1, 0:1], min_val=0, max_val=1)
            with dve.Fori(0, B) as b:
                with dve.Fori(0, NCH) as j:
                    J = b * NCH + j
                    xt = lambda i: xin[:, bass.ds((j % 2) * TPC + i, 1), :].rearrange("p a n -> p (a n)")
                    dve.wait_ge(x_loaded, 16 * (J + 2))
                    nc.vector.memset(keep.gate[:, 25:26], 0.0)
                    for i in range(TPC):
                        for h in range(2):
                            last = nc.vector.bn_stats(stats[:, i, h, :], xt(i)[:, h * HALF:(h + 1) * HALF])
                    last.then_inc(stats_ready, 1)
                    dve.wait_ge(stats_ready, J + 1)
                    nc.vector.memset(keep.gate[:, 26:27], 0.0)
                    for i in range(TPC):
                        last = nc.vector.bn_aggr(mv[:, i, :], stats[:, i, :, :].rearrange("p a b -> p (a b)"))
                    last.then_inc(mv_ready, 1)
                    dve.wait_ge(rstd_ready, J + 1)
                    dve.wait_ge(xlo_ready, J * KC + 1)
                    for i in range(TPC):
                        for c0, c1, at in ((0, H, 0), (KF * P, H, H)):
                            last = nc.vector.tensor_scalar(y[:, i, at:at + c1 - c0], xt(i)[:, c0:c1], mv[:, i, 0:1],
                                                           rstd[:, 1, i:i + 1], ALU.subtract, ALU.mult)
                    last.then_inc(y_ready, 1)
                    for k in range(KC):
                        rows = P if k < KF else KT
                        dve.wait_ge(xhi_ready, J * KC + k + 1)
                        nc.vector.tensor_tensor(xlo[0:rows, k, bass.ds(j * CH, CH)], aff[0:rows, k % 2, :],
                                                xhi[0:rows, k, bass.ds(j * CH, CH)], ALU.subtract).then_inc(xlo_ready, 1)
                for a in range(2):
                    nc.vector.memset(stk[:, a, :, 0:GH, 0:1], 0.0)
                    nc.vector.memset(stk[:, a, :, GH:QK, 0:1], 1.0)
                for j in range(NCH + 1):
                    C = b * NCH + j
                    if j < NCH:
                        dve.wait_ge(raw_ready, 2 * C + 2)
                        qk = raw[:, :, 0:2 * GW].rearrange("p i (e d) -> p i e d", e=QK)
                        nc.vector.tensor_reduce(total[:, :], qk, AX.X, ALU.add).then_inc(total_ready, 1)
                        dve.wait_ge(total_ready, C + 1)
                        for i in range(TPC):
                            last = nc.vector.scalar_tensor_tensor(
                                out=xc[:, i, :, :], in0=bcast(total[:, i * QK:(i + 1) * QK], 2, HD), scalar=-1.0 / HD,
                                in1=qk[:, i, :, :], op0=ALU.mult, op1=ALU.add)
                        last.then_inc(xc_ready, 1)
                    for jt in ([j - 2] if j >= 2 else []) + ([j - 1] if j == NCH else []):
                        for i in range(2, TPC):
                            dve.wait_ge(tq_ready, (b * NCH + jt) * TPC + i + 1)
                            t0 = (jt * TPC + i) * P
                            nc.vector.tensor_copy(qkT[0:SW, 0:QK, t0:t0 + P], tq_bank(i)[0:SW, :].rearrange("p (e n) -> p e n", e=QK)).then_inc(tq_dve, 1)
                    if j < NCH:
                        dve.wait_ge(sq_ready, C + 1)
                        nc.vector.tensor_reduce(ssq[:, 0, :], sq[:, :, :, :], AX.X, ALU.add).then_inc(ssq_ready, 1)
                        dve.wait_ge(hrstd_ready, C + 1)
                        heads = xc[:, :, :, :].rearrange("p i e d -> p (i e) d")
                        nc.vector.scalar_tensor_tensor(out=heads, in0=heads, scalar=HD ** 0.5, in1=bcast(ssq[:, 1, :], 2, HD),
                                                       op0=ALU.mult, op1=ALU.mult).then_inc(yn_ready, 1)
                        dve.wait_ge(yn_ready, C + 1)
                        nc.vector.tensor_tensor(xc[:, :, 0:GH, :], xc[:, :, 0:GH, :], bcast(bcast(keep.gain[:, :], 1, GH), 1, TPC),
                                                ALU.mult).then_inc(yg_ready, 1)
                        part = stk[:, j % 2, :, :, :]
                        dve.wait_ge(high_ready, 2 * C + 1)
                        for e, at in ((0, 1 + HD), (GH, 1 + 2 * HD)):
                            last = nc.vector.tensor_tensor(part[:, :, e:e + GH, at:at + HD], xc[:, :, e:e + GH, :],
                                                           part[:, :, e:e + GH, 1:1 + HD], ALU.subtract)
                        last.then_inc(low_ready, 1)
                        dve.wait_ge(high_ready, 2 * C + 2)

                def group(g, part, cut):
                    it = b * NG + g
                    X = (b * (NG - 1) + g) * NT
                    with dve.If(dve_unsafe > 0):
                        with dve.Fori(0, GH * NT) as n:
                            G, h, i = it * GH * NT + n, n // NT, n % NT
                            dve.wait_ge(g_scores, G + 1)
                            nc.vector.tensor_reduce(nmax[:, 0:1], ps[:, 0:NCH, :].rearrange("p a n -> p (a n)"), AX.X, ALU.max,
                                                    negate=True).then_inc(g_max, 1)
                            dve.wait_ge(g_max, G + 2)
                            nc.vector.tensor_scalar(diag[:, :], keep.ident16[:, :], nmax[:, 0:1], None, ALU.mult).then_inc(g_diag, 1)
                            dve.wait_ge(g_row, G + 1)
                            nc.vector.tensor_copy(qkT[0:1, bass.ds(part * QK + h, 1), bass.ds(i * P, P)].rearrange("p a n -> p (a n)"),
                                                  ps[0:1, 4, 0:P]).then_inc(g_done, 1)
                        dve.nop()
                    low_parts(it * UNITS, 0, True, X if cut else None)
                    with dve.Fori(1, UNITS) as u:
                        low_parts(it * UNITS + u, u, False, X + u if cut else None)
                    if cut:
                        tile_low(X + NT)
                    finish((it + 1) * UNITS, UNITS - 1)

                with dve.Fori(0, NG - 1) as g:
                    group(g, g % 2, True)
                group(NG - 1, (NG - 1) % 2, False)

        @block.tensor
        def _(pe):
            def scores(unit, part, h, qc, s):
                pe.wait_ge(exp_done, unit * STEPS + s + 1)
                for a in range(2):
                    last = nc.tensor.matmul(ps[:, 2 * (s % 2) + a, :],
                                            qkT[0:SW, bass.ds(part * QK + GH + h, 1), (2 * s + a) * P:(2 * s + a + 1) * P].rearrange("p a n -> p (a n)"),
                                            qkT[0:SW, bass.ds(part * QK + h, 1), bass.ds(qc * CH, CH)].rearrange("p a n -> p (a n)"),
                                            start=True, stop=True)
                last.then_inc(scores_ready, 1)

            def sums(unit, h, s):
                pe.wait_ge(plo_ready, unit * STEPS + s + 1)
                for a in range(2):
                    high = p[:, s % NP, a * CH:(a + 1) * CH].bitcast(BF16).rearrange("p (n t) -> p n t", t=2)[:, :, 1]
                    nc.tensor.matmul(acc[0:VW, bass.ds((unit % 2) * CH, CH)],
                                     v16[:, h % 2, 2 * s + a, 0:VW], high,
                                     start=(s == 0 and a == 0), stop=False, skip_group_check=True)
                    last = nc.tensor.matmul(acc[0:RW, bass.ds((unit % 2) * CH, CH)],
                                            vr[:, h % 2, 2 * s + a, 0:RW],
                                            plo[:, s % NP, a * CH:(a + 1) * CH],
                                            start=False, stop=(s == STEPS - 1 and a == 1), skip_group_check=True)
                last.then_inc(pv_done, 1)

            def fold(done):
                pe.wait_ge(oT_ready, done)
                pe.wait_ge(o_ready, done)
                for i in range(TPC):
                    last = nc.tensor.matmul(fold_bank[:, i * RP:(i + 1) * RP], oT[0:VW, i * P:(i + 1) * P], keep.fold[0:VW, :],
                                            start=True, stop=True)
                last.then_inc(fold_ready, 1)

            def tile_products(X, u, g, some):
                ops = list(split_products(xhi, xlo, wq, bass.ds(u * P, P), slice(None)))
                if some.start == 0:
                    pe.wait_ge(t_evac, X + 1)
                for n in some:
                    l, rhs = ops[n]
                    last = nc.tensor.matmul(tile_bank[:, 0:3 * GW], l, rhs[:, bass.ds((g + 1) * 3 * GW, 3 * GW)],
                                            start=(n == 0), stop=(n == len(ops) - 1))
                if some.stop == len(ops):
                    last.then_inc(t_mm, 1)

            def tile_transposes(X):
                pe.wait_ge(t_low, X)
                pe.wait_ge(t_high, 2 * X + 1)
                for e in range(QK):
                    last = nc.tensor.transpose(tile_bank.bitcast(F16)[0:SW, e * P:(e + 1) * P], tstk[:, e, 0:SW], keep.ident16[:, :])
                last.then_inc(t_tq, 1)

            def transposes(b, j):
                for i in range(TPC):
                    C = b * NCH + j
                    if i == 0:
                        pe.wait_ge(low_ready, C + 1)
                        pe.wait_ge(high_ready, 2 * C + 2)
                    if j == 0 and i == 0:
                        pe.wait_ge(o_ready, b * NG * UNITS + 1)
                    elif j > 0 and i == 0:
                        pe.wait_ge(tq_act, 2 * C)
                        pe.wait_ge(tq_dve, 2 * C)
                    for e in range(QK):
                        last = nc.tensor.transpose(tq_bank(i)[0:SW, e * P:(e + 1) * P], stk[:, j % 2, i, e, 0:SW], keep.ident16[:, :])
                    last.then_inc(tq_ready, 1)

            pe_unsafe = pe.value_load(keep.unsafe[0:1, 0:1], min_val=0, max_val=1)
            with pe.Fori(0, B) as b:
                with pe.Fori(0, NCH) as j:
                    J = b * NCH + j
                    pe.wait_ge(y_ready, J + 3)
                    for k in range(KC):
                        pe.wait_ge(aff_ready, J * KC + k + (0 if k else 1))
                        for i in range(TPC):
                            last = nc.tensor.transpose(ps[:, 4 + k % 2, i * P:(i + 1) * P], y[:, i, k * P:(k + 1) * P], keep.ident[:, :])
                        last.then_inc(xt_ready, 1)
                for j in range(NCH):
                    C = b * NCH + j
                    for i in range(TPC):
                        if j == 0 and i == 0:
                            pe.wait_ge(xlo_ready, (b + 1) * NCH * KC + 1)
                            pe.wait_ge(exp_done, b * NG * UNITS * STEPS + 2)
                        elif j > 0 and i % 2 == 0:
                            pe.wait_ge(raw_ready, 2 * C + i // 2 - 1)
                        t0 = (j * TPC + i) * P
                        ops = list(split_products(xhi, xlo, wq, slice(t0, t0 + P), slice(None)))
                        for n, (l, r) in enumerate(ops):
                            last = nc.tensor.matmul(mm_bank(i)[:, 0:3 * GW], l, r[:, 0:3 * GW],
                                                    start=(n == 0), stop=(n == len(ops) - 1))
                        if i % 2:
                            last.then_inc(qkv_ready, 1)
                    if j >= 2:
                        transposes(b, j - 2)
                transposes(b, NCH - 2)
                transposes(b, NCH - 1)

                def group(g, part, cut):
                    it = b * NG + g
                    X0 = (b * (NG - 1) + g) * NT

                    def keys_ready():
                        pe.wait_ge(tq_act, 2 * (b + 1) * NCH)
                        pe.wait_ge(tq_dve, 2 * (b + 1) * NCH)
                        pe.wait_ge(raw_ready, 2 * (b + 1) * NCH)
                        pe.wait_ge(t_evac, X0 + 2)

                    with pe.If(pe_unsafe > 0):
                        with pe.Fori(0, GH * NT) as n:
                            G, h, i = it * GH * NT + n, n // NT, n % NT
                            keys_ready()
                            pe.wait_ge(g_max, G + 1)
                            for c in range(NCH):
                                last = nc.tensor.matmul(ps[:, c, :], qkT[0:RW, bass.ds(part * QK + h, 1), bass.ds(i * P, P)].rearrange("p a n -> p (a n)"),
                                                        qkT[0:RW, bass.ds(part * QK + GH + h, 1), c * CH:(c + 1) * CH].rearrange("p a n -> p (a n)"),
                                                        start=True, stop=True)
                            last.then_inc(g_scores, 1)
                            pe.wait_ge(g_diag, G + 1)
                            nc.tensor.matmul(ps[0:1, 4, 0:P], keep.ones16[:, 0:1], diag[:, :], start=True, stop=True).then_inc(g_row, 1)
                        pe.wait_ge(g_done, (it + 1) * GH * NT)
                        pe.nop()

                    def attend(h, qc, first=False):
                        u = h * NCH + qc
                        unit, X = it * UNITS + u, X0 + u
                        if first:
                            keys_ready()
                        for s in range(STEPS):
                            scores(unit, part, h, qc, s)
                            if s == LAG and isinstance(qc, int):
                                pe.wait_ge(head_ready, it * GH + h + 1)
                            if s >= LAG:
                                sums(unit, h, s - LAG)
                            elif not first:
                                sums(unit - 1, h - 1 if isinstance(qc, int) else h, s - LAG + STEPS)
                            if s == LAG + 2 and not first:
                                fold(unit)
                            if cut and s < 2:
                                tile_products(X, u, g, range(7 * s, 7 * s + 7))
                            if cut and s == 4 and not first:
                                pe.wait_ge(t_raw, X + 1)
                                tile_transposes(X)

                    for h in range(GH):
                        attend(h, 0, first=(h == 0))
                        with pe.Fori(1, NCH) as qc:
                            attend(h, qc)
                    for s in range(STEPS - LAG, STEPS):
                        sums((it + 1) * UNITS - 1, GH - 1, s)
                    if cut:
                        pe.wait_ge(t_raw, X0 + NT)
                        tile_transposes(X0 + NT)
                    fold((it + 1) * UNITS)

                with pe.Fori(0, NG - 1) as g:
                    group(g, g % 2, True)
                group(NG - 1, (NG - 1) % 2, False)


def mlp(nc, keep, x, o_dram, out, wp, w1, w2s, b1col, gates_dram):
    with ExitStack() as ctx:
        sb = lambda n, s, d: ctx.enter_context(nc.sbuf_tensor("ml_" + n, s, d))
        sem = lambda n: ctx.enter_context(nc.semaphore("ml_" + n))
        xf = x.rearrange("b n h -> (b n) h")
        outf = out.rearrange("b n h -> (b n) h")
        gates = sb("gates", [P, B, 3, H], F32)
        tok = sb("tok", [P, TPC, KC * P], F32)
        x1 = sb("x1", [P, 2 * TPC, H], F32)
        part = sb("part", [P, 2, H], F32)
        stats = sb("stats", [P, TPC, 2, 6], F32)
        mv = sb("mv", [P, TPC, 2], F32)
        rstd = sb("rstd", [P, 2, TPC], F32)
        aff = sb("aff", [P, 2, CH], F32)
        ohi = sb("ohi", [P, KC, CH], F16)
        olo = sb("olo", [P, KC, CH], F16)
        xhi = sb("xhi", [P, KC, CH], F16)
        xlo = sb("xlo", [P, KC, CH], F16)
        g32 = sb("g32", [P, 2, CH], F32)
        hhi = sb("hhi", [P, FT, CH], F16)
        hlo = sb("hlo", [P, FT, CH], F16)
        ps = ctx.enter_context(nc.psum_tensor("ml_ps", [P, 8, 512], F32))
        up_bank = lambda f: ps[:, f % 2, :]
        pair = lambda r: ps[:, 2 + 2 * (r % 2):4 + 2 * (r % 2), 0:HALF]
        tr_bank = lambda k: ps[:, 6 + k % 2, :]

        o_loaded, x_loaded, stored = sem("o_loaded"), sem("x_loaded"), sem("stored")
        ot_ready, ohi_ready, olo_ready = sem("ot"), sem("ohi"), sem("olo")
        pair_ready, pair_taken, x1_ready = sem("pair"), sem("pair_taken"), sem("x1r")
        stats_ready, mv_ready, var_ready, rstd_ready, y_ready, x1b_ready = (
            sem("stats"), sem("mv"), sem("var"), sem("rstd"), sem("y"), sem("x1b"))
        xt_ready, aff_ready, xhi_ready, xlo_ready = sem("xt"), sem("aff"), sem("xhi"), sem("xlo")
        up_ready, gelu_done, hhi_ready, hlo_ready, out_ready = sem("up"), sem("gelu"), sem("hhi"), sem("hlo"), sem("outr")
        CHUNKS = B * NCH
        gates_loaded = sem("gates_loaded")
        block = ctx.enter_context(nc.Block())

        @block.sync
        def _(sp):
            def load(J, first=False):
                if not first:
                    sp.wait_ge(xt_ready, J * KC)
                o = o_dram[bass.ds(J * CH, CH), :].rearrange("(i p) n -> p i n", p=P)
                sp.dma_start(tok[:, :, 0:H], o).then_inc(o_loaded, 16)
                sp.dma_start(tok[:, :, H:KC * P], o[:, :, KF * P:H]).then_inc(o_loaded, 16)
                if not first:
                    sp.wait_ge(stored, 16 * J)
                sp.dma_start(x1[:, bass.ds((J % 2) * TPC, TPC), :],
                             xf[bass.ds(J * CH, CH), :].rearrange("(i p) n -> p i n", p=P)).then_inc(x_loaded, 16)

            def store(J):
                sp.wait_ge(out_ready, TPC * (J + 1))
                sp.dma_start(outf[bass.ds(J * CH, CH), :].rearrange("(i p) n -> p i n", p=P),
                             x1[:, bass.ds((J % 2) * TPC, TPC), :]).then_inc(stored, 16)

            sp.dma_start(gates[:, :, :, :].rearrange("p b v n -> p (b v n)"), bcast(gates_dram, 0, P)).then_inc(gates_loaded, 16)
            load(0, first=True)
            with sp.Fori(0, CHUNKS - 1) as J:
                load(J + 1)
                store(J)
            store(CHUNKS - 1)
            sp.wait_ge(stored, 16 * (CHUNKS + 1))

        @block.gpsimd
        def _(pool):
            pool.wait_ge(gates_loaded, 16)
            with pool.Fori(0, CHUNKS) as J:
                pool.wait_ge(mv_ready, J + 1)
                pool.tensor_tensor(rstd[:, 0, :], mv[:, :, 1], keep.eps[:, 0:TPC], ALU.add).then_inc(var_ready, 1)
                pool.wait_ge(var_ready, J + 1)
                pool.tensor_tensor(rstd[:, 1, :], rstd[:, 0, :], keep.power[:, 0:TPC], ALU.pow).then_inc(rstd_ready, 1)
                pool.wait_ge(y_ready, J + 1)
                for i in range(TPC):
                    row = x1[:, bass.ds((J % 2) * TPC + i, 1), :].rearrange("p a n -> p (a n)")
                    last = pool.tensor_tensor(row, row, gates[:, bass.ds(J // NCH, 1), 2, :].rearrange("p a n -> p (a n)"), ALU.add)
                last.then_inc(x1b_ready, 1)

        @block.scalar
        def _(act):
            def high_o(J):
                for k in range(KC):
                    act.wait_ge(ot_ready, J * KC + k + 1)
                    act.copy(ohi[:, k, :], tr_bank(k)).then_inc(ohi_ready, 1)

            def affine(J):
                for k in range(KC):
                    n = J * KC + k
                    act.wait_ge(xt_ready, n + 1)
                    act.wait_ge(xlo_ready, n + (0 if k else 1))
                    b = J // NCH
                    col = lambda v: keep.cols[:, bass.ds(b, 1), v, k:k + 1].rearrange("p b k -> p (b k)")
                    act.activation(aff[:, k % 2, :], tr_bank(k), ACT.Identity, bias=col(2), scale=col(3)).then_inc(aff_ready, 1)
                    act.wait_ge(aff_ready, n + 1)
                    act.copy(xhi[:, k, :], aff[:, k % 2, :]).then_inc(xhi_ready, 1)

            def gelus(J, f0, f1):
                for f in range(f0, f1):
                    m = J * FT + f
                    act.wait_ge(up_ready, m + 1)
                    act.wait_ge(hlo_ready, m + 1)
                    act.activation(g32[:, f % 2, :], up_bank(f), ACT.Gelu_apprx_tanh, bias=b1col[:, f:f + 1],
                                   scale=1.0 / WS).then_inc(gelu_done, 1)

            high_o(0)
            affine(0)
            with act.Fori(0, CHUNKS - 1) as J:
                gelus(J, 0, FT // 2)
                high_o(J + 1)
                gelus(J, FT // 2, FT)
                affine(J + 1)
            gelus(CHUNKS - 1, 0, FT)

        @block.vector
        def _(dve):
            def low_o(J):
                for k in range(KC):
                    rows = P if k < KF else KT
                    dve.wait_ge(ohi_ready, J * KC + k + 1)
                    nc.vector.tensor_tensor(olo[0:rows, k, :], tr_bank(k)[0:rows, :], ohi[0:rows, k, :], ALU.subtract).then_inc(olo_ready, 1)

            def residual(J, i, r, v, after):
                row = x1[:, bass.ds((J % 2) * TPC + i, 1), :].rearrange("p a n -> p (a n)")
                dve.wait_ge(pair_ready, r + 1)
                gate = gates[:, bass.ds(J // NCH, 1), v, :].rearrange("p a (h n) -> p (a h) n", h=2)
                nc.vector.tensor_tensor(part[:, i % 2, :].rearrange("p (h n) -> p h n", h=2), pair(i), gate, ALU.mult).then_inc(pair_taken, 1)
                dve.wait_ge(pair_taken, r + 1)
                nc.vector.tensor_tensor(row, row, part[:, i % 2, :], ALU.add).then_inc(after, 1)

            def project(J, r0):
                dve.wait_ge(x_loaded, 16 * (J + 1))
                for i in range(TPC):
                    residual(J, i, r0 + i, 0, x1_ready)
                dve.wait_ge(x1_ready, TPC * (J + 1))
                nc.vector.memset(keep.gate[:, 27:28], 0.0)
                row = lambda i: x1[:, bass.ds((J % 2) * TPC + i, 1), :].rearrange("p a n -> p (a n)")
                for i in range(TPC):
                    for h in range(2):
                        last = nc.vector.bn_stats(stats[:, i, h, :], row(i)[:, h * HALF:(h + 1) * HALF])
                last.then_inc(stats_ready, 1)
                dve.wait_ge(stats_ready, J + 1)
                nc.vector.memset(keep.gate[:, 26:27], 0.0)
                for i in range(TPC):
                    last = nc.vector.bn_aggr(mv[:, i, :], stats[:, i, :, :].rearrange("p a b -> p (a b)"))
                last.then_inc(mv_ready, 1)
                dve.wait_ge(rstd_ready, J + 1)
                for i in range(TPC):
                    for c0, c1, at in ((0, H, 0), (KF * P, H, H)):
                        last = nc.vector.tensor_scalar(tok[:, i, at:at + c1 - c0], row(i)[:, c0:c1], mv[:, i, 0:1],
                                                       rstd[:, 1, i:i + 1], ALU.subtract, ALU.mult)
                last.then_inc(y_ready, 1)

            def low_x(J):
                for k in range(KC):
                    rows = P if k < KF else KT
                    dve.wait_ge(xhi_ready, J * KC + k + 1)
                    nc.vector.tensor_tensor(xlo[0:rows, k, :], aff[0:rows, k % 2, :], xhi[0:rows, k, :], ALU.subtract).then_inc(xlo_ready, 1)

            def hidden(J, f0, f1):
                for f in range(f0, f1):
                    m = J * FT + f
                    dve.wait_ge(gelu_done, m + 3)
                    nc.vector.tensor_copy(hhi[:, f, :], g32[:, f % 2, :]).then_inc(hhi_ready, 1)
                    dve.wait_ge(hhi_ready, m + 1)
                    nc.vector.tensor_tensor(hlo[:, f, :], g32[:, f % 2, :], hhi[:, f, :], ALU.subtract).then_inc(hlo_ready, 1)

            def down(J, r0):
                dve.wait_ge(x1b_ready, J + 1)
                for i in range(TPC):
                    residual(J, i, r0 + i, 1, out_ready)

            nc.vector.memset(olo[64:P, KF, :], 1.0)
            for n, (s_, credit) in enumerate(((stored, 16), (gelu_done, 2), (hlo_ready, 2), (xlo_ready, 1))):
                nc.vector.memset(keep.gate[:, n:n + 1], 0.0).then_inc(s_, credit)
            low_o(0)
            dve.wait_ge(gates_loaded, 16)
            project(0, 0)
            low_x(0)
            with dve.Fori(0, CHUNKS - 1) as J:
                hidden(J, 0, FT // 2)
                low_o(J + 1)
                hidden(J, FT // 2, FT)
                project(J + 1, TPC + 2 * TPC * J)
                down(J, 2 * TPC + 2 * TPC * J)
                low_x(J + 1)
            hidden(CHUNKS - 1, 0, FT)
            down(CHUNKS - 1, TPC + 2 * TPC * (CHUNKS - 1))

        @block.tensor
        def _(pe):
            def transposes(src, J, k, ready):
                for i in range(TPC):
                    last = nc.tensor.transpose(tr_bank(k)[:, i * P:(i + 1) * P], src[:, i, k * P:(k + 1) * P], keep.ident[:, :])
                last.then_inc(ready, 1)

            def turn_o(J, first=False):
                pe.wait_ge(o_loaded, 32 * (J + 1))
                for k in range(KC):
                    if k >= 2:
                        pe.wait_ge(olo_ready, J * KC + k - 1)
                    elif not first:
                        pe.wait_ge(aff_ready, J * KC)
                    transposes(tok, J, k, ot_ready)

            def turn_y(J):
                pe.wait_ge(y_ready, J + 1)
                for k in range(KC):
                    if k >= 2:
                        pe.wait_ge(aff_ready, J * KC + k - 1)
                    else:
                        pe.wait_ge(olo_ready, (J + 1) * KC)
                    transposes(tok, J, k, xt_ready)

            def by_token(i, r, first, ops):
                if not first or i >= 2:
                    pe.wait_ge(pair_taken, r - 1)
                ops = list(ops)
                for n, (l, w) in enumerate(ops):
                    for half in range(2):
                        last = nc.tensor.matmul(pair(i)[:, half, :], l, w[:, half * HALF:(half + 1) * HALF],
                                                start=(n == 0), stop=(n == len(ops) - 1))
                last.then_inc(pair_ready, 1)

            def project(J, r0, first=False):
                pe.wait_ge(olo_ready, KC * (J + 1))
                for i in range(TPC):
                    by_token(i, r0 + i, first, split_products(ohi, olo, wp, slice(i * P, (i + 1) * P), slice(0, H)))

            def up(J, f0, f1):
                if f0 == 0:
                    pe.wait_ge(xlo_ready, KC * (J + 1) + 1)
                for f in range(f0, f1):
                    m = J * FT + f
                    pe.wait_ge(gelu_done, m + 1)
                    ops = list(split_products(xhi, xlo, w1, slice(0, CH), slice(f * P, (f + 1) * P), bias=False))
                    for n, (xs, w) in enumerate(ops):
                        last = nc.tensor.matmul(up_bank(f), w, xs, start=(n == 0), stop=(n == len(ops) - 1))
                    last.then_inc(up_ready, 1)

            def down(J, r0):
                pe.wait_ge(hlo_ready, FT * (J + 1) + 2)
                for i in range(TPC):
                    t = slice(i * P, (i + 1) * P)
                    by_token(i, r0 + i, False, ((l, w) for f in range(FT) for l, w in (
                        (hhi[:, f, t], w2s[:, 0, f, :]), (hhi[:, f, t], w2s[:, 1, f, :]), (hlo[:, f, t], w2s[:, 0, f, :]))))

            turn_o(0, first=True)
            project(0, 0, first=True)
            turn_y(0)
            with pe.Fori(0, CHUNKS - 1) as J:
                up(J, 0, FT // 2)
                turn_o(J + 1)
                up(J, FT // 2, FT)
                project(J + 1, TPC + 2 * TPC * J)
                down(J, 2 * TPC + 2 * TPC * J)
                turn_y(J + 1)
            up(CHUNKS - 1, 0, FT)
            down(CHUNKS - 1, TPC + 2 * TPC * (CHUNKS - 1))


class Keep:

    def __init__(self, ctx, nc):
        sb = lambda n, s, d: ctx.enter_context(nc.sbuf_tensor(n, s, d))
        self.ident = sb("ident", [P, P], F32)
        self.ident16 = sb("ident16", [P, P], F16)
        self.fold = sb("fold", [P, RP], F32)
        self.power = sb("power", [P, TPC * QK], F32)
        self.eps = sb("eps", [P, TPC], F32)
        self.head_eps = sb("head_eps", [P, TPC * QK], F32)
        self.gate = sb("gate", [P, 28], F32)
        self.ones16 = sb("ones16", [P, 1], F16)
        self.gain = sb("gain", [P, HD], F32)
        self.unsafe = sb("unsafe", [P, 1], I32)
        self.cols = sb("cols", [P, B, 4, KC], F32)


def dit_block(nc, x, c, w_mod, b_mod, w_qkv, b_qkv, g_q, g_k, w_proj, b_proj, w1, b1, w2, b2, out, o_dram, gates_dram):
    o_flat = o_dram.rearrange("b n h -> (b n) h")
    with ExitStack() as ctx:
        keep = Keep(ctx, nc)
        modulation(nc, keep, c, w_mod, b_mod, g_q, g_k, b2, gates_dram)
        with nc.sbuf_tensor("wq", [P, 10, 3 * H], F16) as wq:
            cut_weights(nc, "q_", [Cut(w_qkv, b_qkv, wq, 3 * H, thirds=True)])
            attention(nc, keep, x, o_flat, wq)
        with (nc.sbuf_tensor("wp", [P, 10, H], F16) as wp, nc.sbuf_tensor("w1c", [P, 9, MLP], F16) as w1c,
              nc.sbuf_tensor("w2s", [P, 2, FT, H], F16) as w2s, nc.sbuf_tensor("b1col", [P, FT], F32) as b1col):
            cut_weights(nc, "m_", [Cut(w_proj, b_proj, wp, H), Cut(w1, None, w1c, MLP)], w2, w2s, b1, b1col)
            mlp(nc, keep, x, o_flat, out, wp, w1c, w2s, b1col, gates_dram)


_INS = ["x", "cond_1152"] + ["L0_cond_" + n for n in
        ("w_mod", "b_mod", "w_qkv", "b_qkv", "g_q", "g_k", "w_proj", "b_proj", "w1", "b1", "w2", "b2")]


def kernel(**inputs):
    import numpy as _np
    import concourse.bacc as _bacc
    from concourse.bass_utils import run_bass_kernel_spmd as _run

    nc = _bacc.Bacc("TRN2", target_bir_lowering=False, num_devices=1)
    arrays, args = {}, []
    for name in _INS:
        a = _np.ascontiguousarray(inputs[name])
        arrays[f"in_{name}"] = a
        args.append(nc.dram_tensor(f"in_{name}", a.shape, mybir.dt.from_np(a.dtype), kind="ExternalInput").ap())
    out = nc.dram_tensor("out_0", (B, N, H), F32, kind="ExternalOutput").ap()
    o_dram = nc.dram_tensor("attention_out", (B, N, H), F32, kind="Internal").ap()
    gates_dram = nc.dram_tensor("gates_row", (B * 3 * H,), F32, kind="Internal").ap()
    dit_block(nc, *args, out, o_dram, gates_dram)
    return _run(nc, [arrays], core_ids=[0]).results[0]["out_0"]
```

```python
import concourse.bass as bass
import numpy as np
from concourse import mybir
from contextlib import ExitStack

F32 = mybir.dt.float32
F32R = mybir.dt.float32r
F16 = mybir.dt.float16
BF16 = mybir.dt.bfloat16
I32 = mybir.dt.int32
ALU = mybir.AluOpType
ACT = mybir.ActivationFunctionType
AX = mybir.AxisListType

B, N, H = 2, 2048, 576
NH = 16
HD = H // NH
MLP = 4 * H
EPS = 1e-6
P = 128

KF = H // P
KT = H - KF * P
KC = KF + 1
CH = 512
TPC = CH // P
NCH = N // CH
NT = N // P
GH = 4
NG = NH // GH
GW = GH * HD
QK = 2 * GH
VW = 2 * HD + 1
VP = VW + 1
RW = HD + 1
RP = RW + 1
SW = 3 * HD + 1
SP = 112
FT = MLP // P
HALF = H // 2
WS = 64.0
STEPS = NT // 2
UNITS = GH * NCH
LAG = 3
NP = 4
SAFE = 64.0


def bcast(ap, axis, n):
    v = ap.unsqueeze(axis)
    shape = list(v.shape)
    shape[axis] = n
    return v.broadcast_to(shape)


class Cut:

    def __init__(self, w, bias, out, cols, thirds=False):
        self.w, self.bias, self.out, self.cols, self.thirds = w, bias, out, cols, thirds

    def part(self, p0, p1, slot, c0):
        row = self.out[p0:p1, slot, :]
        if self.thirds:
            return row.rearrange("p (g t j) -> p g t j", g=NG, t=3)[:, :, c0 // H, :]
        return row[:, c0:c0 + H].rearrange("p (g j) -> p g j", g=NG)

    def grouped(self, ap):
        return ap.rearrange("p (g j) -> p g j", g=NG)


class Cutter:

    PIECE = KC * H
    STAGE = PIECE + 2 * H

    def __init__(self, nc, ctx, tag, stage, mats, w2=None, w2s=None):
        sem = lambda n: ctx.enter_context(nc.semaphore(tag + n))
        self.nc, self.mats, self.w2, self.w2s = nc, mats, w2, w2s
        self.pieces = [(m, c0) for m in mats for c0 in range(0, m.cols, H)]
        self.stage = stage
        self.biases = stage[:, :, self.PIECE:self.PIECE + H]
        halves = stage[:, :, self.PIECE + H:self.PIECE + 2 * H].bitcast(F16)
        self.tails, self.bias_hi = halves[:, :, 0:H], halves[:, :, H:2 * H]
        self.lots = [] if w2 is None else [5, 5, 4, 4]
        self.count = len(self.pieces) + len(self.lots)
        self.bufs = stage.shape[1]
        self.landed = [sem(f"landed{i}") for i in range(self.bufs)]
        self.high, self.low, self.blank = sem("high"), sem("low"), sem("blank")

    def staged(self, s):
        return self.stage[:, s, 0:self.PIECE].rearrange("p (k n) -> p k n", k=KC)

    def lot(self, n):
        n -= len(self.pieces)
        a, m = sum(self.lots[:n]), self.lots[n]
        return (a, m, self.stage[:, (len(self.pieces) + n) % self.bufs, 0:m * H], self.w2s[:, 0, a:a + m, :].rearrange("p f n -> p (f n)"),
                self.w2s[:, 1, a:a + m, :].rearrange("p f n -> p (f n)"))

    def loads(self, n):
        if n >= len(self.pieces):
            return 1
        return 3 if self.pieces[n][0].bias is None else 5

    def load(self, sp, n):
        s = n % self.bufs
        if n >= self.bufs:
            sp.wait_ge(self.low, n - self.bufs + 1)
        if n >= len(self.pieces):
            a, m, words, _, _ = self.lot(n)
            sp.dma_start(words.rearrange("p (f n) -> p f n", n=H),
                         self.w2[a * P:(a + m) * P, :].rearrange("(f p) n -> p f n", p=P)).then_inc(self.landed[s], 16)
            return
        m, c0 = self.pieces[n]
        sp.dma_start(self.staged(s)[:, 0:KF, :], m.w[0:KF * P, c0:c0 + H].rearrange("(k p) n -> p k n", p=P)).then_inc(self.landed[s], 16)
        for half in range(2):
            sp.dma_start(self.staged(s)[half * KT:(half + 1) * KT, KF, :], m.w[KF * P:H, c0:c0 + H]).then_inc(self.landed[s], 16)
        if m.bias is not None:
            for row in (64, 96):
                sp.dma_start(self.biases[row:row + 1, s, :], m.bias[c0:c0 + H].unsqueeze(0)).then_inc(self.landed[s], 16)

    def wait_landed(self, eng, n):
        eng.wait_ge(self.landed[n % self.bufs], 16 * sum(self.loads(q) for q in range(n % self.bufs, n + 1, self.bufs)))

    def cut_high(self, act, n):
        self.wait_landed(act, n)
        if n >= len(self.pieces):
            _, _, words, high, _ = self.lot(n)
            act.activation(high, words, ACT.Copy, scale=WS).then_inc(self.high, 1)
            return
        (m, c0), s = self.pieces[n], n % self.bufs
        x = self.staged(s)
        for k in range(KF):
            act.activation(m.part(0, P, k, c0), m.grouped(x[:, k, :]), ACT.Copy, scale=WS)
        act.activation(m.part(0, KT, 8, c0), m.grouped(x[0:KT, KF, :]), ACT.Copy, scale=WS)
        if m.bias is not None:
            act.wait_ge(self.blank, 1)
            act.activation(m.part(0, KT, 9, c0), m.grouped(x[0:KT, KF, :]), ACT.Copy, scale=WS)
            act.activation(m.part(64, 65, 9, c0), m.grouped(self.biases[64:65, s, :]), ACT.Copy, scale=WS)
            act.activation(self.bias_hi[96:97, s, :], self.biases[96:97, s, :], ACT.Copy, scale=WS)
        act.activation(self.tails[KT:P, s, :], x[KT:P, KF, :], ACT.Copy, scale=WS).then_inc(self.high, 1)

    def clear(self):
        for m in self.mats:
            if m.bias is not None:
                self.nc.vector.memset(m.out[64:P, 9, :], 0.0).then_inc(self.blank, 1)

    def cut_low(self, dve, n):
        def lower(out, src, hi):
            return self.nc.vector.scalar_tensor_tensor(out=out, in0=src, scalar=WS, in1=hi, op0=ALU.mult, op1=ALU.subtract)

        self.wait_landed(dve, n)
        dve.wait_ge(self.high, n + 1)
        if n >= len(self.pieces):
            _, _, words, high, low = self.lot(n)
            lower(low, words, high).then_inc(self.low, 1)
            return
        (m, c0), s = self.pieces[n], n % self.bufs
        x = self.staged(s)
        for k in range(KF):
            lower(m.part(0, P, KF + k, c0), m.grouped(x[:, k, :]), m.part(0, P, k, c0))
        last = lower(m.part(KT, P, 8, c0), m.grouped(x[KT:P, KF, :]), m.grouped(self.tails[KT:P, s, :]))
        if m.bias is not None:
            last = lower(m.part(96, 97, 9, c0), m.grouped(self.biases[96:97, s, :]), m.grouped(self.bias_hi[96:97, s, :]))
        last.then_inc(self.low, 1)


def modulation(nc, keep, c, w_mod, b_mod, g_q, g_k, b2, gates_dram, w_qkv):
    with ExitStack() as ctx:
        sb = lambda n, s, d: ctx.enter_context(nc.sbuf_tensor(n, s, d))
        sem = lambda n: ctx.enter_context(nc.semaphore(n))
        wm = sb("wm", [P, KC, 6 * H], F32)
        cT = sb("cT", [P, KC, B], F32)
        sT = sb("sT", [P, KC, B], F32)
        eT = sb("eT", [P, KC, B], F32)
        rT = sb("rT", [P, KC, B], F32)
        rows = sb("rows", [B, 4, KC * P], F32)
        gates = sb("gates", [B, 3, H], F32)
        brow = sb("brow", [B, 6, H], F32)
        b2row = sb("b2row", [B, H], F32)
        gain2 = sb("gain2", [P, 2, HD], F32)
        bound = sb("bound", [P, 2], F32)
        pcol = ctx.enter_context(nc.psum_tensor("pcol", [P, 512], F32))
        prow = ctx.enter_context(nc.psum_tensor("prow", [P, 4, 512], F32))
        pair = lambda n: prow[0:B, 2 * (n % 2):2 * (n % 2) + 2, 0:HALF]
        cutter = Cutter(nc, ctx, "q_", sb("stage", [P, 3, Cutter.STAGE], F32), [w_qkv])
        c_loaded, w_loaded, small_loaded = sem("c_loaded"), [sem(f"wm_loaded{n}") for n in range(6)], sem("small_loaded")
        zeroed, exp_ready, silu_step, silu_ready = sem("zeroed"), sem("silu_exp"), sem("silu_step"), sem("silu_ready")
        cols_ready, rows_ready, rows_taken = sem("cols_ready"), sem("rows_ready"), sem("rows_taken")
        row_step, turn_ready, gain_step, ident_done = sem("row_step"), sem("turn_ready"), sem("gain_step"), sem("ident_done")
        ident_zero, gates_ready, gates_stored = sem("ident_zero"), sem("gates_ready"), sem("gates_stored")
        VECS = (0, 1, 3, 4, 2, 5)
        block = ctx.enter_context(nc.Block())

        @block.sync
        def _(sp):
            with nc.allow_non_contiguous_dma(reason="two short vectors"):
                for b in range(B):
                    sp.dma_start(cT[:, 0:KF, b], c[b, 0:KF * P].rearrange("(k p) -> p k", p=P)).then_inc(c_loaded, 16)
                    sp.dma_start(cT[0:KT, KF, b:b + 1], c[b, KF * P:H].rearrange("(p k) -> p k", k=1)).then_inc(c_loaded, 16)
            for n, vec in enumerate(VECS):
                cols = slice(vec * H, (vec + 1) * H)
                sp.dma_start(wm[:, 0:KF, cols], w_mod[0:KF * P, cols].rearrange("(k p) n -> p k n", p=P)).then_inc(w_loaded[n], 16)
                sp.dma_start(wm[0:KT, KF, cols], w_mod[KF * P:H, cols]).then_inc(w_loaded[n], 16)
            for n in range(cutter.count):
                cutter.load(sp, n)
            sp.wait_ge(gates_ready, 2)
            sp.dma_start(gates_dram.rearrange("(b n) -> b n", b=B), gates[:, :, :].rearrange("b v n -> b (v n)")).then_inc(gates_stored, 16)
            sp.wait_ge(gates_stored, 16)

        @block.scalar
        def _(act):
            act.dma_start(brow[:, :, :].rearrange("b v n -> b (v n)"), bcast(b_mod, 0, B)).then_inc(small_loaded, 16)
            act.dma_start(b2row[:, :], bcast(b2, 0, B)).then_inc(small_loaded, 16)
            act.dma_start(gain2[:, 0, :], bcast(g_q, 0, P)).then_inc(small_loaded, 16)
            act.dma_start(gain2[:, 1, :], bcast(g_k, 0, P)).then_inc(small_loaded, 16)
            act.wait_ge(zeroed, 1)
            act.wait_ge(c_loaded, 16 * 2 * B)
            act.activation(eT[:, :, :], cT[:, :, :], ACT.Exp, scale=-1.0).then_inc(exp_ready, 1)
            for n in range(cutter.count):
                cutter.cut_high(act, n)

        @block.gpsimd
        def _(pool):
            pool.memset(keep.ident[:, :], 0.0).then_inc(ident_zero, 1)
            pool.memset(keep.ident16[:, :], 0.0).then_inc(ident_zero, 1)
            pool.memset(keep.fold[:, :], 0.0).then_inc(ident_zero, 1)
            pool.memset(keep.power[:, :], -0.5)
            pool.memset(keep.eps[:, :], EPS)
            pool.memset(keep.head_eps[:, :], HD * EPS * WS * WS)
            pool.memset(keep.ones16[:, :], 1.0)
            pool.wait_ge(ident_zero, 3)
            for m in (keep.ident, keep.ident16):
                last = pool.affine_select(out=m[:, :], in_=m[:, :], compare_op=ALU.not_equal, fill=1.0,
                                          base=0, pattern=[[-1, P]], channel_multiplier=1)
            last.then_inc(ident_done, 1)
            pool.affine_select(out=keep.fold[:, :], in_=keep.fold[:, :], compare_op=ALU.not_equal, fill=1.0,
                               base=0, pattern=[[-1, RP]], channel_multiplier=1).then_inc(ident_zero, 1)
            pool.wait_ge(ident_zero, 4)
            pool.affine_select(out=keep.fold[:, 0:HD], in_=keep.fold[:, 0:HD], compare_op=ALU.not_equal, fill=1.0,
                               base=-RW, pattern=[[-1, HD]], channel_multiplier=1)

        @block.vector
        def _(dve):
            nc.vector.memset(cT[KT:P, KF, :], 0.0).then_inc(zeroed, 1)
            dve.wait_ge(exp_ready, 1)
            nc.vector.tensor_scalar_add(rT[:, :, :], eT[:, :, :], 1.0).then_inc(silu_step, 1)
            dve.wait_ge(silu_step, 1)
            nc.vector.reciprocal(eT[:, :, :], rT[:, :, :]).then_inc(silu_step, 1)
            dve.wait_ge(silu_step, 2)
            nc.vector.tensor_tensor(sT[:, :, :], cT[:, :, :], eT[:, :, :], ALU.mult).then_inc(silu_ready, 1)
            cutter.clear()
            dve.wait_ge(small_loaded, 16 * 4)
            nc.vector.scalar_tensor_tensor(out=keep.gain[:, :], in0=gain2[:, 0, :], scalar=HD ** -0.5,
                                           in1=gain2[:, 1, :], op0=ALU.mult, op1=ALU.mult).then_inc(gain_step, 1)
            dve.wait_ge(gain_step, 1)
            nc.vector.tensor_reduce(bound[:, 0:1], keep.gain[:, :], AX.X, ALU.max,
                                    apply_absolute_value=True).then_inc(gain_step, 1)
            dve.wait_ge(gain_step, 2)
            nc.vector.tensor_scalar(bound[:, 1:2], bound[:, 0:1], float(HD), SAFE, ALU.mult, ALU.is_gt).then_inc(gain_step, 1)
            dve.wait_ge(gain_step, 3)
            nc.vector.tensor_copy(keep.unsafe[:, :], bound[:, 1:2])
            for n, vec in enumerate(VECS):
                dve.wait_ge(rows_ready, n + 1)
                out = rows[:, n, 0:H] if n < 4 else gates[:, n - 4, :]
                nc.vector.tensor_tensor(out.rearrange("b (h n) -> b h n", h=2), pair(n),
                                        brow[:, vec, :].rearrange("b (h n) -> b h n", h=2), ALU.add).then_inc(rows_taken, 1)
                dve.wait_ge(rows_taken, n + 1)
                if n in (1, 3):
                    nc.vector.tensor_scalar_add(rows[:, n, 0:H], rows[:, n, 0:H], 1.0).then_inc(row_step, 1)
                    dve.wait_ge(row_step, n // 2 + 1)
                if n < 4:
                    nc.vector.tensor_copy(rows[:, n, H:KC * P], rows[:, n, KF * P:H]).then_inc(turn_ready, 1)
                    continue
                if n == 5:
                    nc.vector.tensor_tensor(gates[:, 2, :], gates[:, 1, :], b2row[:, :], ALU.mult).then_inc(gain_step, 1)
                    dve.wait_ge(gain_step, 4)
                nc.vector.tensor_scalar_mul(gates[:, n - 4, :], gates[:, n - 4, :], 1.0 / WS).then_inc(gates_ready, 1)
            dve.wait_ge(cols_ready, 1)
            nc.vector.tensor_copy(keep.cols[:, :, :, :].rearrange("p b v k -> p v k b"),
                                  pcol[:, 0:4 * KC * B].rearrange("p (v k b) -> p v k b", v=4, b=B))
            for n in range(cutter.count):
                cutter.cut_low(dve, n)

        @block.tensor
        def _(pe):
            pe.wait_ge(silu_ready, 1)
            for n, vec in enumerate(VECS):
                pe.wait_ge(w_loaded[n], 32)
                if n >= 2:
                    pe.wait_ge(rows_taken, n - 1)
                for half in range(2):
                    for k in range(KC):
                        kr = P if k < KF else KT
                        last = nc.tensor.matmul(pair(n)[:, half, :], sT[0:kr, k, :],
                                                wm[0:kr, k, vec * H + half * HALF:vec * H + (half + 1) * HALF],
                                                start=(k == 0), stop=(k == KC - 1))
                last.then_inc(rows_ready, 1)
            pe.wait_ge(ident_done, 1)
            pe.wait_ge(turn_ready, 4)
            for n in range(4):
                for k in range(KC):
                    last = nc.tensor.transpose(pcol[:, (n * KC + k) * B:(n * KC + k + 1) * B], rows[:, n, k * P:(k + 1) * P], keep.ident[0:B, 0:B])
            last.then_inc(cols_ready, 1)


def split_products(xhi, xlo, w, tokens, cols, bias=True):
    for k in range(KF):
        yield xhi[:, k, tokens], w[:, k, cols]
        yield xhi[:, k, tokens], w[:, KF + k, cols]
        yield xlo[:, k, tokens], w[:, k, cols]
    yield xhi[:, KF, tokens], w[:, 8, cols]
    if bias:
        yield xlo[0:97, KF, tokens], w[0:97, 9, cols]
    else:
        yield xlo[0:KT, KF, tokens], w[0:KT, 8, cols]


def attention(nc, keep, x, o_dram, wq):
    with ExitStack() as ctx:
        sb = lambda n, s, d: ctx.enter_context(nc.sbuf_tensor("at_" + n, s, d))
        sem = lambda n: ctx.enter_context(nc.semaphore("at_" + n))
        xf = x.rearrange("b n h -> (b n) h")
        mv = sb("mv", [P, TPC, 2], F32)
        rstd = sb("rstd", [P, 2, TPC], F32)
        xhi = sb("xhi", [P, KC, N], F16)
        xlo = sb("xlo", [P, KC, N], F16)
        total = sb("total", [P, TPC * QK], F32)
        ssq = sb("ssq", [P, 2, 2, TPC * QK], F32)
        stats = ssq[:, :, :, :].rearrange("p a b n -> p (a b n)")[:, 0:TPC * 2 * 6].rearrange("p (i h n) -> p i h n", h=2, n=6)
        qkT = sb("qkT", [SP, 2 * QK, N], F16)
        v32 = sb("v32", [P, 2 * NT, GH, HD], F32)
        v16 = sb("v16", [P, 2, NT, VP], F16)
        vr = sb("vr", [P, 2, NT, RP], F32R)
        traw = sb("traw", [P, QK, HD], F32)
        txc = sb("txc", [P, QK, HD], F32)
        ttotal = sb("ttotal", [P, QK], F32)
        diag = txc[:, :, :].rearrange("p e d -> p (e d)").bitcast(F16)[:, 0:P]
        tssq = sb("tssq", [P, 2, QK], F32)
        tstk = sb("tstk", [P, QK, SP], F16)
        oT = sb("oT", [VW, CH], F32)
        rden = sb("rden", [P, TPC], F32)
        og = sb("og", [P, NT, HD], F32)
        pgate = keep.gate[:, 15:19]
        nmax = mv[:, 0, :]

        def overlaid(*sets):
            size = lambda tensors: sum(-(-int(np.prod(shape[1:])) * (2 if d == F16 else 4) // 32) * 32 for _, shape, d in tensors)
            pad = max(map(size, sets)) - size(sets[-1])
            if pad:
                sets = (*sets[:-1], [*sets[-1], (sets[-1][0][0] + "_pad", [P, pad // 4], F32)])
            made = []
            for n, tensors in enumerate(sets):
                with ExitStack() as one:
                    place = ctx if n == len(sets) - 1 else one
                    made += [place.enter_context(nc.sbuf_tensor("at_" + name, shape, d)) for name, shape, d in tensors]
            return made

        xin, y, aff, stk, raw, xc, p, plo, *_ = overlaid(
            [("xin", [P, 2 * TPC, H], F32),
             ("y", [P, TPC, KC * P], F32),
             ("aff", [P, 2, CH], F32)],
            [("stk", [P, 2, TPC, QK, SP], F16),
             ("raw", [P, TPC, 3 * GW], F32), ("xc", [P, 2, TPC, QK, HD], F32)],
            [("p", [P, NP, 2 * CH], F32),
             ("plo", [P, NP, 2 * CH], F32R)])
        sq = raw[:, :, 0:2 * GW]
        ps = ctx.enter_context(nc.psum_tensor("at_ps", [P, 8, 512], F32))
        mm_bank = lambda i: ps[:, i, :]
        tq_bank = lambda i: ps[:, 4 + i, :].bitcast(F16)
        acc = ps[:, 4:6, :].rearrange("p a n -> p (a n)")
        fold_bank = ps[:, 6, :]
        tile_bank = ps[:, 7, :]

        x_loaded = sem("x_loaded")
        stats_ready, mv_ready, var_ready, rstd_ready, y_ready = sem("stats"), sem("mv"), sem("var"), sem("rstd"), sem("y")
        xt_ready, aff_ready, xhi_ready, xlo_ready = sem("xt"), sem("aff"), sem("xhi"), sem("xlo")
        qkv_ready, raw_ready = sem("qkv"), sem("raw")
        v_ready, total_ready, xc_ready, sq_ready, ssq_ready, msq_ready, hrstd_ready = (
            sem("v"), sem("total"), sem("xc"), sem("sq"), sem("ssq"), sem("msq"), sem("hrstd"))
        yn_ready, yg_ready, high_ready, low_ready = sem("yn"), sem("yg"), sem("high"), sem("low")
        tq_ready, tq_act, tq_dve, fixed = sem("tq"), sem("tq_act"), sem("tq_dve"), sem("fixed")
        scores_ready, exp_done, plo_ready, pv_done = sem("scores"), sem("exp"), sem("plo"), sem("pv")
        oT_ready, fold_ready, rden_ready, o_ready, o_stored = sem("oT"), sem("foldr"), sem("rden"), sem("o"), sem("o_stored")
        t_mm, t_raw, t_total, t_xc, t_sq, t_ssq, t_msq, t_rstd, t_yn, t_yg, t_high, t_low, t_tq, t_evac = (
            sem("t_" + n) for n in ("mm", "raw", "total", "xc", "sq", "ssq", "msq", "rstd", "yn", "yg", "high", "low", "tq", "evac"))
        vh_ready, head_ready = sem("vh"), sem("head")
        g_scores, g_max, g_diag, g_row, g_done = sem("g_scores"), sem("g_max"), sem("g_diag"), sem("g_row"), sem("g_done")

        block = ctx.enter_context(nc.Block())

        @block.sync
        def _(sp):
            with sp.Fori(0, B) as b:
                with sp.Fori(0, NCH) as j:
                    J = b * NCH + j
                    sp.wait_ge(y_ready, J + 1)
                    sp.wait_ge(x_loaded, 16 * J + 16)
                    sp.dma_start(xin[:, bass.ds((j % 2) * TPC, TPC), :],
                                 xf[bass.ds(b * N + j * CH, CH), :].rearrange("(i p) n -> p i n", p=P)).then_inc(x_loaded, 16)
                with sp.Fori(0, NH) as h:
                    sp.wait_ge(o_ready, (b * NH + h + 1) * NCH + 1)
                    sp.dma_start(o_dram[bass.ds(b * N, N), bass.ds(h * HD, HD)].rearrange("(t p) n -> p t n", p=P),
                                 og[:, :, :]).then_inc(o_stored, 16)
            sp.wait_ge(o_stored, 16 * (B * NH + 1))

        @block.gpsimd
        def _(pool):
            def head(it, part, h, done):
                v = v32[:, bass.ds(part * NT, NT), h, :]
                gate = lambda n: pool.tensor_tensor(pgate[:, n:n + 1], keep.eps[:, 0:1], keep.eps[:, 0:1], ALU.add)
                pool.wait_ge(pv_done, done * STEPS + 1)
                gate(0)
                pool.tensor_copy(vr[:, h % 2, :, 0:HD], v)
                pool.tensor_copy(v16[:, h % 2, :, 0:HD], v).then_inc(vh_ready, 1)
                pool.wait_ge(vh_ready, it * GH + h + 1)
                gate(1)
                pool.tensor_tensor(v16[:, h % 2, :, RW:VW], v, v16[:, h % 2, :, 0:HD], ALU.subtract).then_inc(head_ready, 1)

            with pool.Fori(0, B) as b:
                with pool.Fori(0, NCH) as j:
                    J = b * NCH + j
                    pool.wait_ge(mv_ready, J + 1)
                    pool.tensor_tensor(rstd[:, 0, :], mv[:, :, 1], keep.eps[:, 0:TPC], ALU.add).then_inc(var_ready, 1)
                    pool.wait_ge(var_ready, J + 1)
                    pool.tensor_tensor(rstd[:, 1, :], rstd[:, 0, :], keep.power[:, 0:TPC], ALU.pow).then_inc(rstd_ready, 1)
                for j in range(NCH):
                    C = b * NCH + j
                    pool.wait_ge(ssq_ready, C + 2)
                    pool.tensor_tensor(ssq[:, j % 2, 1, :], ssq[:, j % 2, 0, :], keep.head_eps[:, :], ALU.add).then_inc(msq_ready, 1)
                    pool.wait_ge(msq_ready, C + 1)
                    pool.tensor_tensor(ssq[:, j % 2, 1, :], ssq[:, j % 2, 1, :], keep.power[:, 0:TPC * QK], ALU.pow).then_inc(hrstd_ready, 1)
                pool.wait_ge(v_ready, (b + 1) * NCH)
                pool.tensor_tensor(pgate[:, 2:3], keep.eps[:, 0:1], keep.eps[:, 0:1], ALU.add)
                head(b * NG, 0, 0, b * NG * UNITS)
                with pool.Fori(0, NG - 1) as g:
                    it = b * NG + g
                    for h in range(GH):
                        for qc in range(NCH):
                            X = (b * (NG - 1) + g) * NT + h * NCH + qc
                            pool.wait_ge(t_ssq, X + 2)
                            pool.tensor_tensor(tssq[:, 1, :], tssq[:, 0, :], keep.head_eps[:, 0:QK], ALU.add).then_inc(t_msq, 1)
                            pool.wait_ge(t_msq, X + 1)
                            pool.tensor_tensor(tssq[:, 1, :], tssq[:, 1, :], keep.power[:, 0:QK], ALU.pow).then_inc(t_rstd, 1)
                            if qc == 2 and h + 1 < GH:
                                head(it, g % 2, h + 1, it * UNITS + h * NCH)
                    pool.wait_ge(t_raw, (b * (NG - 1) + g + 1) * NT)
                    pool.tensor_tensor(pgate[:, 3:4], keep.eps[:, 0:1], keep.eps[:, 0:1], ALU.add)
                    head(it + 1, (g + 1) % 2, 0, it * UNITS + (GH - 1) * NCH)
                for h in range(1, GH):
                    head(b * NG + NG - 1, (NG - 1) % 2, h, (b * NG + NG - 1) * UNITS + (h - 1) * NCH)

        @block.scalar
        def _(act):
            def store_tq(bank, i, j):
                t0 = (j * TPC + i) * P
                return act.copy(qkT[0:SW, 0:QK, t0:t0 + P], bank[0:SW, :].rearrange("p (e n) -> p e n", e=QK))

            def store_half(b, j):
                for i in range(2):
                    act.wait_ge(tq_ready, (b * NCH + j) * TPC + i + 1)
                    store_tq(tq_bank(i), i, j).then_inc(tq_act, 1)

            def tile_high(X):
                act.wait_ge(t_yg, X)
                act.wait_ge(t_tq, X)
                act.copy(tstk[:, :, 1:1 + HD], txc[:, :, :]).then_inc(t_high, 1)

            def tile_high_again():
                act.copy(tstk[:, 0:GH, 1 + 2 * HD:SW], txc[:, 0:GH, :])
                act.copy(tstk[:, GH:QK, 1 + HD:1 + 2 * HD], txc[:, GH:QK, :]).then_inc(t_high, 1)

            def tile_store(X, part, tile):
                act.wait_ge(t_tq, X + 1)
                act.copy(qkT[0:SW, bass.ds(part * QK, QK), bass.ds(tile * P, P)],
                         tile_bank.bitcast(F16)[0:SW, :].rearrange("p (e n) -> p e n", e=QK)).then_inc(t_evac, 1)

            def keep_oT(done):
                act.wait_ge(pv_done, done * STEPS + 1)
                act.wait_ge(fold_ready, done)
                act.copy(oT[:, :], acc[0:VW, bass.ds(((done + 1) % 2) * CH, CH)]).then_inc(oT_ready, 1)

            def exps(unit, u, first=False, cut=None):
                for s in range(STEPS):
                    n = unit * STEPS + s
                    if s == LAG and not first:
                        keep_oT(unit)
                    act.wait_ge(scores_ready, n + 1)
                    act.wait_ge(pv_done, n + 1 - NP + 1 if not first or s >= NP else unit * STEPS + 1)
                    act.activation(p[:, s % NP, :], ps[:, 2 * (s % 2):2 * (s % 2) + 2, :].rearrange("p a n -> p (a n)"),
                                   ACT.Exp).then_inc(exp_done, 1)
                    if cut is None:
                        continue
                    X, part = cut
                    if s == 0 and not first:
                        tile_high(X)
                    if s == 1 and not first:
                        tile_high_again()
                    if s == 2:
                        act.wait_ge(t_mm, X + 1)
                        act.wait_ge(t_ssq, X + 1)
                        act.activation(v32[:, bass.ds(part * NT + u, 1), :, :].rearrange("p a h d -> p (a h d)"), tile_bank[:, 2 * GW:3 * GW],
                                       ACT.Copy, scale=1.0 / WS)
                        act.copy(traw[:, :, :].rearrange("p e d -> p (e d)"), tile_bank[:, 0:2 * GW]).then_inc(t_raw, 1)
                    if s == 4:
                        act.wait_ge(t_xc, X + 1)
                        act.activation(traw[:, :, :], txc[:, :, :], ACT.Square).then_inc(t_sq, 1)
                    if s == 5 and not first:
                        tile_store(X, part, u - 1)

            with act.Fori(0, B) as b:
                with act.Fori(0, NCH) as j:
                    J = b * NCH + j
                    for k in range(KC):
                        n = J * KC + k
                        act.wait_ge(xt_ready, n + 1)
                        act.wait_ge(xlo_ready, n + (0 if k else 1))
                        act.activation(aff[:, k % 2, :], ps[:, 4 + k % 2, :], ACT.Identity,
                                       bias=keep.cols[:, bass.ds(b, 1), 0, k:k + 1].rearrange("p b k -> p (b k)"),
                                       scale=keep.cols[:, bass.ds(b, 1), 1, k:k + 1].rearrange("p b k -> p (b k)")).then_inc(aff_ready, 1)
                        act.wait_ge(aff_ready, n + 2)
                        act.copy(xhi[:, k, bass.ds(j * CH, CH)], aff[:, k % 2, :]).then_inc(xhi_ready, 1)
                act.wait_ge(pv_done, b * NG * UNITS * STEPS + 1)
                for j in range(NCH + 1):
                    C = b * NCH + j
                    if j < NCH:
                        for hh in range(2):
                            act.wait_ge(qkv_ready, 2 * C + hh + 1)
                            if j == 0 and hh == 0:
                                act.wait_ge(xlo_ready, (b + 1) * NCH * KC + 1)
                            if hh == 0:
                                act.wait_ge(ssq_ready, C + 1)
                            act.copy(raw[:, 2 * hh:2 * hh + 2, :], ps[:, 2 * hh:2 * hh + 2, 0:3 * GW]).then_inc(raw_ready, 1)
                        act.wait_ge(raw_ready, 2 * C + 2)
                        act.activation(v32[:, j * TPC:(j + 1) * TPC, :, :].rearrange("p i h d -> p i (h d)"), raw[:, :, 2 * GW:3 * GW],
                                       ACT.Copy, scale=1.0 / WS).then_inc(v_ready, 1)
                    if j >= 2:
                        store_half(b, j - 2)
                    if j < NCH:
                        act.wait_ge(xc_ready, C + 1)
                        act.activation(sq, xc[:, j % 2, :, :, :].rearrange("p i e d -> p i (e d)"), ACT.Square).then_inc(sq_ready, 1)
                    if j >= 1:
                        if j >= 3:
                            act.wait_ge(tq_ready, (C - 2) * TPC)
                        act.wait_ge(yg_ready, C)
                        part, heads = stk[:, (j - 1) % 2, :, :, :], xc[:, (j - 1) % 2, :, :, :]
                        act.copy(part[:, :, :, 1:1 + HD], heads).then_inc(high_ready, 1)
                        act.copy(part[:, :, 0:GH, 1 + 2 * HD:SW], heads[:, :, 0:GH, :])
                        act.copy(part[:, :, GH:QK, 1 + HD:1 + 2 * HD], heads[:, :, GH:QK, :]).then_inc(high_ready, 1)
                store_half(b, NCH - 1)

                def group(g, part, cut):
                    it = b * NG + g
                    X = (b * (NG - 1) + g) * NT
                    exps(it * UNITS, 0, True, (X, part) if cut else None)
                    with act.Fori(1, UNITS) as u:
                        exps(it * UNITS + u, u, False, (X + u, part) if cut else None)
                    if cut:
                        tile_high(X + NT)
                        tile_high_again()
                    keep_oT((it + 1) * UNITS)
                    if cut:
                        tile_store(X + NT, part, NT - 1)

                with act.Fori(0, NG - 1) as g:
                    group(g, (g + 1) % 2, True)
                group(NG - 1, 0, False)

        @block.vector
        def _(dve):
            def low_parts(unit, u, first=False, cut=None):
                for s in range(STEPS):
                    n, X = unit * STEPS + s, cut
                    if cut is not None and s == 3:
                        dve.wait_ge(t_raw, X + 1)
                        nc.vector.tensor_reduce(ttotal[:, :], traw[:, :, :], AX.X, ALU.add).then_inc(t_total, 1)
                    if cut is not None and s == 7:
                        dve.wait_ge(t_rstd, X + 1)
                        nc.vector.scalar_tensor_tensor(out=txc[:, :, :], in0=txc[:, :, :], scalar=HD ** 0.5, in1=bcast(tssq[:, 1, :], 2, HD),
                                                       op0=ALU.mult, op1=ALU.mult).then_inc(t_yn, 1)
                    dve.wait_ge(exp_done, n + 3)
                    high = p[:, s % NP, :].bitcast(BF16).rearrange("p (n t) -> p n t", t=2)[:, :, 1]
                    nc.vector.tensor_tensor(plo[:, s % NP, :], p[:, s % NP, :], high, ALU.subtract).then_inc(plo_ready, 1)
                    if s == LAG + 3 and not first:
                        finish(unit, u - 1)
                    if cut is None:
                        continue
                    if s == 1 and not first:
                        tile_low(X)
                    if s == 3:
                        dve.wait_ge(t_total, X + 1)
                        dve.wait_ge(t_high, 2 * X + 1)
                        nc.vector.scalar_tensor_tensor(out=txc[:, :, :], in0=bcast(ttotal[:, :], 2, HD), scalar=-1.0 / HD, in1=traw[:, :, :],
                                                       op0=ALU.mult, op1=ALU.add).then_inc(t_xc, 1)
                    if s == 5:
                        dve.wait_ge(t_sq, X + 1)
                        nc.vector.tensor_reduce(tssq[:, 0, :], traw[:, :, :], AX.X, ALU.add).then_inc(t_ssq, 1)
                    if s == 7:
                        dve.wait_ge(t_yn, X + 1)
                        nc.vector.tensor_tensor(txc[:, 0:GH, :], txc[:, 0:GH, :], bcast(keep.gain[:, :], 1, GH), ALU.mult).then_inc(t_yg, 1)

            def tile_low(X):
                dve.wait_ge(t_high, 2 * X)
                for e, at in ((0, 1 + HD), (GH, 1 + 2 * HD)):
                    last = nc.vector.tensor_tensor(tstk[:, e:e + GH, at:at + HD], txc[:, e:e + GH, :], tstk[:, e:e + GH, 1:1 + HD], ALU.subtract)
                last.then_inc(t_low, 1)

            def finish(done, u):
                dve.wait_ge(fold_ready, done + 1)
                out = fold_bank[:, 0:TPC * RP].rearrange("p (i d) -> p i d", i=TPC)
                nc.vector.reciprocal(rden[:, :], out[:, :, HD]).then_inc(rden_ready, 1)
                dve.wait_ge(rden_ready, done)
                dve.wait_ge(o_stored, 16 * ((done - 1) // NCH + 1))
                nc.vector.tensor_tensor(og[:, bass.ds((u % NCH) * TPC, TPC), :], out[:, :, 0:HD],
                                        bcast(rden[:, :], 2, HD), ALU.mult).then_inc(o_ready, 1)

            nc.vector.memset(xlo[64:P, KF, :], 1.0)
            nc.vector.memset(v16[:, :, :, HD:HD + 1], 1.0)
            nc.vector.memset(tstk[:, 0:GH, 0:1], 0.0)
            nc.vector.memset(tstk[:, GH:QK, 0:1], 1.0)
            nc.vector.memset(vr[:, :, :, HD:HD + 1].bitcast(F32), 1.0)
            for n, (s_, credit) in enumerate(((y_ready, 2), (x_loaded, 16), (xlo_ready, 1), (aff_ready, 1), (ssq_ready, 1), (exp_done, 2), (pv_done, 1),
                               (o_ready, 1), (fold_ready, 1), (o_stored, 16), (g_max, 1),
                                               (t_ssq, 1), (t_high, 1), (t_tq, 1), (t_evac, 2))):
                nc.vector.memset(keep.gate[:, n:n + 1], 0.0).then_inc(s_, credit)

            dve_unsafe = dve.value_load(keep.unsafe[0:1, 0:1], min_val=0, max_val=1)
            with dve.Fori(0, B) as b:
                xt = lambda j, i: xin[:, bass.ds((j % 2) * TPC + i, 1), :].rearrange("p a n -> p (a n)")

                def stats_of(J, j):
                    dve.wait_ge(x_loaded, 16 * (J + 2))
                    nc.vector.memset(keep.gate[:, 19:20], 0.0)
                    for i in range(TPC):
                        for h in range(2):
                            last = nc.vector.bn_stats(stats[:, i, h, :], xt(j, i)[:, h * HALF:(h + 1) * HALF])
                    last.then_inc(stats_ready, 1)
                    dve.wait_ge(stats_ready, J + 1)
                    nc.vector.memset(keep.gate[:, 20:21], 0.0)
                    for i in range(TPC):
                        last = nc.vector.bn_aggr(mv[:, i, :], stats[:, i, :, :].rearrange("p a b -> p (a b)"))
                    last.then_inc(mv_ready, 1)

                def normalise(J, j):
                    dve.wait_ge(rstd_ready, J + 1)
                    dve.wait_ge(xlo_ready, J * KC + 1)
                    for i in range(TPC):
                        for c0, c1, at in ((0, H, 0), (KF * P, H, H)):
                            last = nc.vector.tensor_scalar(y[:, i, at:at + c1 - c0], xt(j, i)[:, c0:c1], mv[:, i, 0:1],
                                                           rstd[:, 1, i:i + 1], ALU.subtract, ALU.mult)
                    last.then_inc(y_ready, 1)

                def low_x(J, j):
                    for k in range(KC):
                        rows = P if k < KF else KT
                        dve.wait_ge(xhi_ready, J * KC + k + 1)
                        nc.vector.tensor_tensor(xlo[0:rows, k, bass.ds(j * CH, CH)], aff[0:rows, k % 2, :],
                                                xhi[0:rows, k, bass.ds(j * CH, CH)], ALU.subtract).then_inc(xlo_ready, 1)

                stats_of(b * NCH, 0)
                normalise(b * NCH, 0)
                with dve.Fori(0, NCH - 1) as j:
                    J = b * NCH + j
                    stats_of(J + 1, j + 1)
                    low_x(J, j)
                    normalise(J + 1, j + 1)
                low_x(b * NCH + NCH - 1, NCH - 1)
                for a in range(2):
                    nc.vector.memset(stk[:, a, :, 0:GH, 0:1], 0.0)
                    nc.vector.memset(stk[:, a, :, GH:QK, 0:1], 1.0)
                def store_half(j):
                    for i in range(2, TPC):
                        dve.wait_ge(tq_ready, (b * NCH + j) * TPC + i + 1)
                        t0 = (j * TPC + i) * P
                        nc.vector.tensor_copy(qkT[0:SW, 0:QK, t0:t0 + P], tq_bank(i)[0:SW, :].rearrange("p (e n) -> p e n", e=QK)).then_inc(tq_dve, 1)

                for j in range(NCH + 1):
                    C = b * NCH + j
                    if j < NCH:
                        dve.wait_ge(raw_ready, 2 * C + 2)
                        qk = raw[:, :, 0:2 * GW].rearrange("p i (e d) -> p i e d", e=QK)
                        nc.vector.tensor_reduce(total[:, :], qk, AX.X, ALU.add).then_inc(total_ready, 1)
                        dve.wait_ge(total_ready, C + 1)
                        for i in range(TPC):
                            last = nc.vector.scalar_tensor_tensor(
                                out=xc[:, j % 2, i, :, :], in0=bcast(total[:, i * QK:(i + 1) * QK], 2, HD), scalar=-1.0 / HD,
                                in1=qk[:, i, :, :], op0=ALU.mult, op1=ALU.add)
                        last.then_inc(xc_ready, 1)
                    if j >= 2:
                        store_half(j - 2)
                    if j < NCH:
                        dve.wait_ge(sq_ready, C + 1)
                        nc.vector.tensor_reduce(ssq[:, j % 2, 0, :], sq.rearrange("p i (e d) -> p i e d", e=QK), AX.X, ALU.add).then_inc(ssq_ready, 1)
                    if j >= 1:
                        dve.wait_ge(hrstd_ready, C)
                        a = (j - 1) % 2
                        heads = xc[:, a, :, :, :].rearrange("p i e d -> p (i e) d")
                        nc.vector.scalar_tensor_tensor(out=heads, in0=heads, scalar=HD ** 0.5, in1=bcast(ssq[:, a, 1, :], 2, HD),
                                                       op0=ALU.mult, op1=ALU.mult).then_inc(yn_ready, 1)
                        dve.wait_ge(yn_ready, C)
                        nc.vector.tensor_tensor(xc[:, a, :, 0:GH, :], xc[:, a, :, 0:GH, :], bcast(bcast(keep.gain[:, :], 1, GH), 1, TPC),
                                                ALU.mult).then_inc(yg_ready, 1)
                        part = stk[:, a, :, :, :]
                        dve.wait_ge(high_ready, 2 * C - 1)
                        for e, at in ((0, 1 + HD), (GH, 1 + 2 * HD)):
                            last = nc.vector.tensor_tensor(part[:, :, e:e + GH, at:at + HD], xc[:, a, :, e:e + GH, :],
                                                           part[:, :, e:e + GH, 1:1 + HD], ALU.subtract)
                        last.then_inc(low_ready, 1)
                        dve.wait_ge(high_ready, 2 * C)
                store_half(NCH - 1)

                def group(g, part, cut):
                    it = b * NG + g
                    X = (b * (NG - 1) + g) * NT
                    with dve.If(dve_unsafe > 0):
                        with dve.Fori(0, GH * NT) as n:
                            G, h, i = it * GH * NT + n, n // NT, n % NT
                            dve.wait_ge(g_scores, G + 1)
                            nc.vector.tensor_reduce(nmax[:, 0:1], ps[:, 0:NCH, :].rearrange("p a n -> p (a n)"), AX.X, ALU.max,
                                                    negate=True).then_inc(g_max, 1)
                            dve.wait_ge(g_max, G + 2)
                            nc.vector.tensor_scalar(diag[:, :], keep.ident16[:, :], nmax[:, 0:1], None, ALU.mult).then_inc(g_diag, 1)
                            dve.wait_ge(g_row, G + 1)
                            nc.vector.tensor_copy(qkT[0:1, bass.ds(part * QK + h, 1), bass.ds(i * P, P)].rearrange("p a n -> p (a n)"),
                                                  ps[0:1, 4, 0:P]).then_inc(g_done, 1)
                        dve.nop()
                    low_parts(it * UNITS, 0, True, X if cut else None)
                    with dve.Fori(1, UNITS) as u:
                        low_parts(it * UNITS + u, u, False, X + u if cut else None)
                    if cut:
                        tile_low(X + NT)
                    finish((it + 1) * UNITS, UNITS - 1)

                with dve.Fori(0, NG - 1) as g:
                    group(g, g % 2, True)
                group(NG - 1, (NG - 1) % 2, False)

        @block.tensor
        def _(pe):
            def scores(unit, part, h, qc, s):
                pe.wait_ge(exp_done, unit * STEPS + s + 1)
                for a in range(2):
                    last = nc.tensor.matmul(ps[:, 2 * (s % 2) + a, :],
                                            qkT[0:SW, bass.ds(part * QK + GH + h, 1), (2 * s + a) * P:(2 * s + a + 1) * P].rearrange("p a n -> p (a n)"),
                                            qkT[0:SW, bass.ds(part * QK + h, 1), bass.ds(qc * CH, CH)].rearrange("p a n -> p (a n)"),
                                            start=True, stop=True)
                last.then_inc(scores_ready, 1)

            def sums(unit, h, s):
                pe.wait_ge(plo_ready, unit * STEPS + s + 1)
                for a in range(2):
                    high = p[:, s % NP, a * CH:(a + 1) * CH].bitcast(BF16).rearrange("p (n t) -> p n t", t=2)[:, :, 1]
                    nc.tensor.matmul(acc[0:VW, bass.ds((unit % 2) * CH, CH)],
                                     v16[:, h % 2, 2 * s + a, 0:VW], high,
                                     start=(s == 0 and a == 0), stop=False, skip_group_check=True)
                    last = nc.tensor.matmul(acc[0:RW, bass.ds((unit % 2) * CH, CH)],
                                            vr[:, h % 2, 2 * s + a, 0:RW],
                                            plo[:, s % NP, a * CH:(a + 1) * CH],
                                            start=False, stop=(s == STEPS - 1 and a == 1), skip_group_check=True)
                last.then_inc(pv_done, 1)

            def fold(done):
                pe.wait_ge(oT_ready, done)
                pe.wait_ge(o_ready, done)
                for i in range(TPC):
                    last = nc.tensor.matmul(fold_bank[:, i * RP:(i + 1) * RP], oT[0:VW, i * P:(i + 1) * P], keep.fold[0:VW, :],
                                            start=True, stop=True)
                last.then_inc(fold_ready, 1)

            def tile_products(X, u, g, some):
                ops = list(split_products(xhi, xlo, wq, bass.ds(u * P, P), slice(None)))
                if some.start == 0:
                    pe.wait_ge(t_evac, X + 1)
                for n in some:
                    l, rhs = ops[n]
                    last = nc.tensor.matmul(tile_bank[:, 0:3 * GW], l, rhs[:, bass.ds((g + 1) * 3 * GW, 3 * GW)],
                                            start=(n == 0), stop=(n == len(ops) - 1))
                if some.stop == len(ops):
                    last.then_inc(t_mm, 1)

            def tile_transposes(X):
                pe.wait_ge(t_low, X)
                pe.wait_ge(t_high, 2 * X + 1)
                for e in range(QK):
                    last = nc.tensor.transpose(tile_bank.bitcast(F16)[0:SW, e * P:(e + 1) * P], tstk[:, e, 0:SW], keep.ident16[:, :])
                last.then_inc(t_tq, 1)

            def transposes(b, j):
                for i in range(TPC):
                    C = b * NCH + j
                    if i == 0:
                        pe.wait_ge(low_ready, C + 1)
                        pe.wait_ge(high_ready, 2 * C + 2)
                    if j == 0 and i == 0:
                        pe.wait_ge(o_ready, b * NG * UNITS + 1)
                    elif j > 0 and i == 0:
                        pe.wait_ge(tq_act, 2 * C)
                        pe.wait_ge(tq_dve, 2 * C)
                    for e in range(QK):
                        last = nc.tensor.transpose(tq_bank(i)[0:SW, e * P:(e + 1) * P], stk[:, j % 2, i, e, 0:SW], keep.ident16[:, :])
                    last.then_inc(tq_ready, 1)

            pe_unsafe = pe.value_load(keep.unsafe[0:1, 0:1], min_val=0, max_val=1)
            with pe.Fori(0, B) as b:
                def turn(J):
                    pe.wait_ge(y_ready, J + 3)
                    for k in range(KC):
                        pe.wait_ge(aff_ready, J * KC + k + (0 if k else 1))
                        for i in range(TPC):
                            last = nc.tensor.transpose(ps[:, 4 + k % 2, i * P:(i + 1) * P], y[:, i, k * P:(k + 1) * P], keep.ident[:, :])
                        last.then_inc(xt_ready, 1)

                def products(j, tiles):
                    C = b * NCH + j
                    for i in tiles:
                        if j == 0 and i == 0:
                            pe.wait_ge(xlo_ready, (C + 1) * KC + 1)
                            pe.wait_ge(exp_done, b * NG * UNITS * STEPS + 2)
                        elif j > 0 and i % 2 == 0:
                            pe.wait_ge(raw_ready, 2 * C + i // 2 - 1)
                        t0 = (j * TPC + i) * P
                        ops = list(split_products(xhi, xlo, wq, slice(t0, t0 + P), slice(None)))
                        for n, (l, r) in enumerate(ops):
                            last = nc.tensor.matmul(mm_bank(i)[:, 0:3 * GW], l, r[:, 0:3 * GW],
                                                    start=(n == 0), stop=(n == len(ops) - 1))
                        if i % 2:
                            last.then_inc(qkv_ready, 1)

                with pe.Fori(0, NCH - 1) as j:
                    turn(b * NCH + j)
                products(0, (0, 1))
                turn(b * NCH + NCH - 1)
                products(0, (2, 3))
                for j in range(NCH):
                    if j > 0:
                        products(j, range(TPC))
                    if j >= 2:
                        transposes(b, j - 2)
                transposes(b, NCH - 2)
                transposes(b, NCH - 1)

                def group(g, part, cut):
                    it = b * NG + g
                    X0 = (b * (NG - 1) + g) * NT

                    def keys_ready():
                        pe.wait_ge(tq_act, 2 * (b + 1) * NCH)
                        pe.wait_ge(tq_dve, 2 * (b + 1) * NCH)
                        pe.wait_ge(raw_ready, 2 * (b + 1) * NCH)
                        pe.wait_ge(t_evac, X0 + 2)

                    with pe.If(pe_unsafe > 0):
                        with pe.Fori(0, GH * NT) as n:
                            G, h, i = it * GH * NT + n, n // NT, n % NT
                            keys_ready()
                            pe.wait_ge(g_max, G + 1)
                            for c in range(NCH):
                                last = nc.tensor.matmul(ps[:, c, :], qkT[0:RW, bass.ds(part * QK + h, 1), bass.ds(i * P, P)].rearrange("p a n -> p (a n)"),
                                                        qkT[0:RW, bass.ds(part * QK + GH + h, 1), c * CH:(c + 1) * CH].rearrange("p a n -> p (a n)"),
                                                        start=True, stop=True)
                            last.then_inc(g_scores, 1)
                            pe.wait_ge(g_diag, G + 1)
                            nc.tensor.matmul(ps[0:1, 4, 0:P], keep.ones16[:, 0:1], diag[:, :], start=True, stop=True).then_inc(g_row, 1)
                        pe.wait_ge(g_done, (it + 1) * GH * NT)
                        pe.nop()

                    def attend(h, qc, first=False):
                        u = h * NCH + qc
                        unit, X = it * UNITS + u, X0 + u
                        if first:
                            keys_ready()
                        for s in range(STEPS):
                            scores(unit, part, h, qc, s)
                            if s == LAG and isinstance(qc, int):
                                pe.wait_ge(head_ready, it * GH + h + 1)
                            if s >= LAG:
                                sums(unit, h, s - LAG)
                            elif not first:
                                sums(unit - 1, h - 1 if isinstance(qc, int) else h, s - LAG + STEPS)
                            if s == LAG + 2 and not first:
                                fold(unit)
                            if cut and s < 2:
                                tile_products(X, u, g, range(7 * s, 7 * s + 7))
                            if cut and s == 4 and not first:
                                pe.wait_ge(t_raw, X + 1)
                                tile_transposes(X)

                    for h in range(GH):
                        attend(h, 0, first=(h == 0))
                        with pe.Fori(1, NCH) as qc:
                            attend(h, qc)
                    for s in range(STEPS - LAG, STEPS):
                        sums((it + 1) * UNITS - 1, GH - 1, s)
                    if cut:
                        pe.wait_ge(t_raw, X0 + NT)
                        tile_transposes(X0 + NT)
                    fold((it + 1) * UNITS)

                with pe.Fori(0, NG - 1) as g:
                    group(g, g % 2, True)
                group(NG - 1, (NG - 1) % 2, False)


def mlp(nc, keep, x, o_dram, out, w_proj, b_proj, w1_in, b1, w2, gates_dram):
    with ExitStack() as ctx:
        sb = lambda n, s, d: ctx.enter_context(nc.sbuf_tensor("ml_" + n, s, d))
        sem = lambda n: ctx.enter_context(nc.semaphore("ml_" + n))
        xf = x.rearrange("b n h -> (b n) h")
        outf = out.rearrange("b n h -> (b n) h")
        gates = sb("gates", [P, B, 3, H], F32)
        tok = sb("tok", [P, TPC, KC * P], F32)
        x1 = sb("x1", [P, 2 * TPC, H], F32)
        part = sb("part", [P, 2, H], F32)
        stats = sb("stats", [P, TPC, 2, 6], F32)
        mv = sb("mv", [P, TPC, 2], F32)
        rstd = sb("rstd", [P, 2, TPC], F32)
        aff = sb("aff", [P, 2, CH], F32)
        ohi = sb("ohi", [P, KC, CH], F16)
        olo = sb("olo", [P, KC, CH], F16)
        xhi = sb("xhi", [P, KC, CH], F16)
        xlo = sb("xlo", [P, KC, CH], F16)
        g32 = sb("g32", [P, 2, CH], F32)
        hid = sb("hid", [P, 2, FT, CH], F16)
        hhi, hlo = hid[:, 0], hid[:, 1]
        wp = sb("wp", [P, 10, H], F16)
        w1 = sb("w1", [P, 9, MLP], F16)
        w2s = sb("w2s", [P, 2, FT, H], F16)
        b1col = sb("b1col", [P, FT], F32)
        cutter = Cutter(nc, ctx, "m_", hid[:, :, :, :].rearrange("p a f n -> p a (f n)").bitcast(F32),
                        [Cut(w_proj, b_proj, wp, H), Cut(w1_in, None, w1, MLP)], w2, w2s)
        ps = ctx.enter_context(nc.psum_tensor("ml_ps", [P, 8, 512], F32))
        up_bank = lambda f: ps[:, f % 2, :]
        pair = lambda r: ps[:, 2 + 2 * (r % 2):4 + 2 * (r % 2), 0:HALF]
        tr_bank = lambda k: ps[:, 6 + k % 2, :]

        o_loaded, x_loaded, stored = sem("o_loaded"), sem("x_loaded"), sem("stored")
        ot_ready, ohi_ready, olo_ready = sem("ot"), sem("ohi"), sem("olo")
        pair_ready, pair_taken, x1_ready = sem("pair"), sem("pair_taken"), sem("x1r")
        stats_ready, mv_ready, var_ready, rstd_ready, y_ready, x1b_ready = (
            sem("stats"), sem("mv"), sem("var"), sem("rstd"), sem("y"), sem("x1b"))
        xt_ready, aff_ready, xhi_ready, xlo_ready = sem("xt"), sem("aff"), sem("xhi"), sem("xlo")
        up_ready, gelu_done, hhi_ready, hlo_ready, out_ready = sem("up"), sem("gelu"), sem("hhi"), sem("hlo"), sem("outr")
        CHUNKS = B * NCH
        WITH_UP = ((0, FT // 2, (0, 1)), (FT // 2, FT // 2 + 2, (2, 3)), (FT // 2 + 2, FT // 2 + 4, (4,)), (FT // 2 + 4, FT, ()))
        WITH_DOWN = ((0, 1), (2, 3), (4,), ())
        BEFORE_X1, BEFORE_XN = 3, 5
        gates_loaded, b1_loaded = sem("gates_loaded"), sem("b1_loaded")
        block = ctx.enter_context(nc.Block())

        @block.sync
        def _(sp):
            def load(J, first=False, weights=False):
                if not first:
                    sp.wait_ge(xt_ready, J * KC)
                o = o_dram[bass.ds(J * CH, CH), :].rearrange("(i p) n -> p i n", p=P)
                sp.dma_start(tok[:, :, 0:H], o).then_inc(o_loaded, 16)
                sp.dma_start(tok[:, :, H:KC * P], o[:, :, KF * P:H]).then_inc(o_loaded, 16)
                if weights:
                    cutter.load(sp, 0)
                if not first:
                    sp.wait_ge(stored, 16 * J)
                sp.dma_start(x1[:, bass.ds((J % 2) * TPC, TPC), :],
                             xf[bass.ds(J * CH, CH), :].rearrange("(i p) n -> p i n", p=P)).then_inc(x_loaded, 16)

            def store(J):
                sp.wait_ge(out_ready, TPC * (J + 1))
                sp.dma_start(outf[bass.ds(J * CH, CH), :].rearrange("(i p) n -> p i n", p=P),
                             x1[:, bass.ds((J % 2) * TPC, TPC), :]).then_inc(stored, 16)

            load(0, first=True, weights=True)
            sp.dma_start(gates[:, :, :, :].rearrange("p b v n -> p (b v n)"), bcast(gates_dram, 0, P)).then_inc(gates_loaded, 16)
            with nc.allow_non_contiguous_dma(reason="a short vector"):
                sp.dma_start(b1col[:, :], b1.rearrange("(f p) -> p f", p=P)).then_inc(b1_loaded, 16)
            for n in range(1, cutter.count):
                cutter.load(sp, n)
            with sp.Fori(0, CHUNKS - 1) as J:
                load(J + 1)
                store(J)
            for i in range(TPC):
                sp.wait_ge(out_ready, TPC * (CHUNKS - 1) + i + 1)
                sp.dma_start(outf[(CHUNKS - 1) * CH + i * P:(CHUNKS - 1) * CH + (i + 1) * P, :],
                             x1[:, ((CHUNKS - 1) % 2) * TPC + i, :]).then_inc(stored, 16)
            sp.wait_ge(stored, 16 * (CHUNKS + TPC))

        @block.gpsimd
        def _(pool):
            pool.wait_ge(gates_loaded, 16)
            with pool.Fori(0, CHUNKS) as J:
                pool.wait_ge(mv_ready, J + 1)
                pool.tensor_tensor(rstd[:, 0, :], mv[:, :, 1], keep.eps[:, 0:TPC], ALU.add).then_inc(var_ready, 1)
                pool.wait_ge(var_ready, J + 1)
                pool.tensor_tensor(rstd[:, 1, :], rstd[:, 0, :], keep.power[:, 0:TPC], ALU.pow).then_inc(rstd_ready, 1)
                pool.wait_ge(y_ready, J + 1)
                for i in range(TPC):
                    row = x1[:, bass.ds((J % 2) * TPC + i, 1), :].rearrange("p a n -> p (a n)")
                    last = pool.tensor_tensor(row, row, gates[:, bass.ds(J // NCH, 1), 2, :].rearrange("p a n -> p (a n)"), ALU.add)
                last.then_inc(x1b_ready, 1)

        @block.scalar
        def _(act):
            def high_o(J, ks=range(KC)):
                for k in ks:
                    act.wait_ge(ot_ready, J * KC + k + 1)
                    act.copy(ohi[:, k, :], tr_bank(k)).then_inc(ohi_ready, 1)

            def affine(J):
                for k in range(KC):
                    n = J * KC + k
                    act.wait_ge(xt_ready, n + 1)
                    act.wait_ge(xlo_ready, n + (0 if k else 1))
                    b = J // NCH
                    col = lambda v: keep.cols[:, bass.ds(b, 1), v, k:k + 1].rearrange("p b k -> p (b k)")
                    act.activation(aff[:, k % 2, :], tr_bank(k), ACT.Identity, bias=col(2), scale=col(3)).then_inc(aff_ready, 1)
                    act.wait_ge(aff_ready, n + 1)
                    act.copy(xhi[:, k, :], aff[:, k % 2, :]).then_inc(xhi_ready, 1)

            def gelus(J, f0, f1):
                for f in range(f0, f1):
                    m = J * FT + f
                    act.wait_ge(up_ready, m + 1)
                    act.wait_ge(hlo_ready, m + 1)
                    act.activation(g32[:, f % 2, :], up_bank(f), ACT.Gelu_apprx_tanh, bias=b1col[:, f:f + 1],
                                   scale=1.0 / WS).then_inc(gelu_done, 1)

            high_o(0)
            for n in range(BEFORE_XN):
                cutter.cut_high(act, n)
            affine(0)
            for n in range(BEFORE_XN, cutter.count):
                cutter.cut_high(act, n)
            act.wait_ge(b1_loaded, 16)
            with act.Fori(0, CHUNKS - 1) as J:
                for f0, f1, ks in WITH_UP:
                    gelus(J, f0, f1)
                    high_o(J + 1, ks)
                affine(J + 1)
            gelus(CHUNKS - 1, 0, FT)

        @block.vector
        def _(dve):
            def low_o(J, ks=range(KC)):
                for k in ks:
                    rows = P if k < KF else KT
                    dve.wait_ge(ohi_ready, J * KC + k + 1)
                    nc.vector.tensor_tensor(olo[0:rows, k, :], tr_bank(k)[0:rows, :], ohi[0:rows, k, :], ALU.subtract).then_inc(olo_ready, 1)

            def residual(J, i, r, v, after):
                row = x1[:, bass.ds((J % 2) * TPC + i, 1), :].rearrange("p a n -> p (a n)")
                dve.wait_ge(pair_ready, r + 1)
                gate = gates[:, bass.ds(J // NCH, 1), v, :].rearrange("p a (h n) -> p (a h) n", h=2)
                nc.vector.tensor_tensor(part[:, i % 2, :].rearrange("p (h n) -> p h n", h=2), pair(i), gate, ALU.mult).then_inc(pair_taken, 1)
                dve.wait_ge(pair_taken, r + 1)
                nc.vector.tensor_tensor(row, row, part[:, i % 2, :], ALU.add).then_inc(after, 1)

            def project(J, r0):
                dve.wait_ge(x_loaded, 16 * (J + 1))
                for i in range(TPC):
                    residual(J, i, r0 + i, 0, x1_ready)
                dve.wait_ge(x1_ready, TPC * (J + 1))
                nc.vector.memset(keep.gate[:, 21:22], 0.0)
                row = lambda i: x1[:, bass.ds((J % 2) * TPC + i, 1), :].rearrange("p a n -> p (a n)")
                for i in range(TPC):
                    for h in range(2):
                        last = nc.vector.bn_stats(stats[:, i, h, :], row(i)[:, h * HALF:(h + 1) * HALF])
                last.then_inc(stats_ready, 1)
                dve.wait_ge(stats_ready, J + 1)
                nc.vector.memset(keep.gate[:, 20:21], 0.0)
                for i in range(TPC):
                    last = nc.vector.bn_aggr(mv[:, i, :], stats[:, i, :, :].rearrange("p a b -> p (a b)"))
                last.then_inc(mv_ready, 1)
                dve.wait_ge(rstd_ready, J + 1)
                for i in range(TPC):
                    for c0, c1, at in ((0, H, 0), (KF * P, H, H)):
                        last = nc.vector.tensor_scalar(tok[:, i, at:at + c1 - c0], row(i)[:, c0:c1], mv[:, i, 0:1],
                                                       rstd[:, 1, i:i + 1], ALU.subtract, ALU.mult)
                last.then_inc(y_ready, 1)

            def low_x(J, ks=range(KC)):
                for k in ks:
                    rows = P if k < KF else KT
                    dve.wait_ge(xhi_ready, J * KC + k + 1)
                    nc.vector.tensor_tensor(xlo[0:rows, k, :], aff[0:rows, k % 2, :], xhi[0:rows, k, :], ALU.subtract).then_inc(xlo_ready, 1)

            def hidden(J, f0, f1):
                for f in range(f0, f1):
                    m = J * FT + f
                    dve.wait_ge(gelu_done, m + 3)
                    nc.vector.tensor_copy(hhi[:, f, :], g32[:, f % 2, :]).then_inc(hhi_ready, 1)
                    dve.wait_ge(hhi_ready, m + 1)
                    nc.vector.tensor_tensor(hlo[:, f, :], g32[:, f % 2, :], hhi[:, f, :], ALU.subtract).then_inc(hlo_ready, 1)

            def down(J, r0, turn=False):
                dve.wait_ge(x1b_ready, J + 1)
                for i in range(TPC):
                    residual(J, i, r0 + i, 1, out_ready)
                    if turn:
                        low_x(J + 1, WITH_DOWN[i])

            nc.vector.memset(olo[64:P, KF, :], 1.0)
            for n, (s_, credit) in enumerate(((stored, 16), (gelu_done, 2), (hlo_ready, 2), (xlo_ready, 1))):
                nc.vector.memset(keep.gate[:, n:n + 1], 0.0).then_inc(s_, credit)
            cutter.clear()
            low_o(0)
            for n in range(BEFORE_X1):
                cutter.cut_low(dve, n)
            dve.wait_ge(gates_loaded, 16)
            project(0, 0)
            for n in range(BEFORE_X1, BEFORE_XN):
                cutter.cut_low(dve, n)
            low_x(0)
            for n in range(BEFORE_XN, cutter.count):
                cutter.cut_low(dve, n)
            dve.wait_ge(cutter.low, cutter.count)
            nc.vector.memset(keep.gate[:, 22:23], 0.0)
            with dve.Fori(0, CHUNKS - 1) as J:
                for f0, f1, ks in WITH_UP:
                    hidden(J, f0, f1)
                    low_o(J + 1, ks)
                project(J + 1, TPC + 2 * TPC * J)
                down(J, 2 * TPC + 2 * TPC * J, turn=True)
            hidden(CHUNKS - 1, 0, FT)
            down(CHUNKS - 1, TPC + 2 * TPC * (CHUNKS - 1))

        @block.tensor
        def _(pe):
            def transposes(src, J, k, ready):
                for i in range(TPC):
                    last = nc.tensor.transpose(tr_bank(k)[:, i * P:(i + 1) * P], src[:, i, k * P:(k + 1) * P], keep.ident[:, :])
                last.then_inc(ready, 1)

            def turn_o(J, ks=range(KC), first=False):
                if ks:
                    pe.wait_ge(o_loaded, 32 * (J + 1))
                for k in ks:
                    if k >= 2:
                        pe.wait_ge(olo_ready, J * KC + k - 1)
                    elif not first:
                        pe.wait_ge(aff_ready, J * KC)
                    transposes(tok, J, k, ot_ready)

            def turn_y(J, ks=range(KC)):
                pe.wait_ge(y_ready, J + 1)
                for k in ks:
                    if k >= 2:
                        pe.wait_ge(aff_ready, J * KC + k - 1)
                    else:
                        pe.wait_ge(olo_ready, (J + 1) * KC)
                    transposes(tok, J, k, xt_ready)

            def by_token(i, r, first, ops):
                if not first or i >= 2:
                    pe.wait_ge(pair_taken, r - 1)
                ops = list(ops)
                for n, (l, w) in enumerate(ops):
                    for half in range(2):
                        last = nc.tensor.matmul(pair(i)[:, half, :], l, w[:, half * HALF:(half + 1) * HALF],
                                                start=(n == 0), stop=(n == len(ops) - 1))
                last.then_inc(pair_ready, 1)

            def project(J, r0, first=False):
                pe.wait_ge(olo_ready, KC * (J + 1))
                for i in range(TPC):
                    by_token(i, r0 + i, first, split_products(ohi, olo, wp, slice(i * P, (i + 1) * P), slice(0, H)))

            def up(J, f0, f1):
                if f0 == 0:
                    pe.wait_ge(xlo_ready, KC * (J + 1) + 1)
                for f in range(f0, f1):
                    m = J * FT + f
                    piece = ((f + 1) * P - 1) // H
                    if piece > (f * P - 1) // H:
                        pe.wait_ge(cutter.low, piece + 2)
                    pe.wait_ge(gelu_done, m + 1)
                    ops = list(split_products(xhi, xlo, w1, slice(0, CH), slice(f * P, (f + 1) * P), bias=False))
                    for n, (xs, w) in enumerate(ops):
                        last = nc.tensor.matmul(up_bank(f), w, xs, start=(n == 0), stop=(n == len(ops) - 1))
                    last.then_inc(up_ready, 1)

            def down(J, r0, turn=False):
                pe.wait_ge(cutter.low, cutter.count)
                pe.wait_ge(hlo_ready, FT * (J + 1) + 2)
                for i in range(TPC):
                    t = slice(i * P, (i + 1) * P)
                    by_token(i, r0 + i, False, ((l, w) for f in range(FT) for l, w in (
                        (hhi[:, f, t], w2s[:, 0, f, :]), (hhi[:, f, t], w2s[:, 1, f, :]), (hlo[:, f, t], w2s[:, 0, f, :]))))
                    if turn and WITH_DOWN[i]:
                        turn_y(J + 1, WITH_DOWN[i])

            turn_o(0, first=True)
            pe.wait_ge(cutter.low, 1)
            project(0, 0, first=True)
            turn_y(0)
            with pe.Fori(0, CHUNKS - 1) as J:
                for f0, f1, ks in WITH_UP:
                    up(J, f0, f1)
                    turn_o(J + 1, ks)
                project(J + 1, TPC + 2 * TPC * J)
                down(J, 2 * TPC + 2 * TPC * J, turn=True)
            up(CHUNKS - 1, 0, FT)
            down(CHUNKS - 1, TPC + 2 * TPC * (CHUNKS - 1))


class Keep:

    def __init__(self, ctx, nc):
        sb = lambda n, s, d: ctx.enter_context(nc.sbuf_tensor(n, s, d))
        self.ident = sb("ident", [P, P], F32)
        self.ident16 = sb("ident16", [P, P], F16)
        self.fold = sb("fold", [P, RP], F32)
        self.power = sb("power", [P, TPC * QK], F32)
        self.eps = sb("eps", [P, TPC], F32)
        self.head_eps = sb("head_eps", [P, TPC * QK], F32)
        self.gate = sb("gate", [P, 24], F32)
        self.ones16 = sb("ones16", [P, 1], F16)
        self.gain = sb("gain", [P, HD], F32)
        self.unsafe = sb("unsafe", [P, 1], I32)
        self.cols = sb("cols", [P, B, 4, KC], F32)


def dit_block(nc, x, c, w_mod, b_mod, w_qkv, b_qkv, g_q, g_k, w_proj, b_proj, w1, b1, w2, b2, out, o_dram, gates_dram):
    o_flat = o_dram.rearrange("b n h -> (b n) h")
    with ExitStack() as ctx:
        keep = Keep(ctx, nc)
        with nc.sbuf_tensor("wq", [P, 10, 3 * H], F16) as wq:
            modulation(nc, keep, c, w_mod, b_mod, g_q, g_k, b2, gates_dram, Cut(w_qkv, b_qkv, wq, 3 * H, thirds=True))
            attention(nc, keep, x, o_flat, wq)
        mlp(nc, keep, x, o_flat, out, w_proj, b_proj, w1, b1, w2, gates_dram)


_INS = ["x", "cond_1152"] + ["L0_cond_" + n for n in
        ("w_mod", "b_mod", "w_qkv", "b_qkv", "g_q", "g_k", "w_proj", "b_proj", "w1", "b1", "w2", "b2")]


def kernel(**inputs):
    import numpy as _np
    import concourse.bacc as _bacc
    from concourse.bass_utils import run_bass_kernel_spmd as _run

    nc = _bacc.Bacc("TRN2", target_bir_lowering=False, num_devices=1)
    arrays, args = {}, []
    for name in _INS:
        a = _np.ascontiguousarray(inputs[name])
        arrays[f"in_{name}"] = a
        args.append(nc.dram_tensor(f"in_{name}", a.shape, mybir.dt.from_np(a.dtype), kind="ExternalInput").ap())
    out = nc.dram_tensor("out_0", (B, N, H), F32, kind="ExternalOutput").ap()
    o_dram = nc.dram_tensor("attention_out", (B, N, H), F32, kind="Internal").ap()
    gates_dram = nc.dram_tensor("gates_row", (B * 3 * H,), F32, kind="Internal").ap()
    dit_block(nc, *args, out, o_dram, gates_dram)
    return _run(nc, [arrays], core_ids=[0]).results[0]["out_0"]
```
